# Optimizing a Trainium2 kernel written in Bass

```python
import numpy as np
import jax
import jax.numpy as jnp

def _softmax(x, axis=-1):
    return jax.nn.softmax(x, axis=axis)

def _gelu(x):
    return jax.nn.gelu(x, approximate=True)

def _silu(x):
    return jax.nn.silu(x)

def _sigmoid(x):
    return jax.nn.sigmoid(x)

def _layernorm(x, axis=-1, eps=1e-05):
    m = jnp.mean(x, axis=axis, keepdims=True)
    v = jnp.var(x, axis=axis, keepdims=True)
    return (x - m) / jnp.sqrt(v + eps)

def _scatter_add(tgt, idx, src, axis=0):
    return tgt.at[idx].add(src)

def _segment_sum(src, seg, n):
    return jax.ops.segment_sum(src, seg, n)
kernel_name = 'mk_sandwich_d2_jaxref_r8_7b5e5b'

def setup_inputs(seed: int=0):
    np.random.seed(seed)
    _w = jnp.asarray

    def _L0_attn_setup():
        import jax, jax.numpy as jnp
        import numpy as np
        DIM = 128
        HEADS = 16
        EPS = 1e-12
        key = jax.random.key(seed)
        ks = jax.random.split(key, 6)
        b, n, dim, h = (2, 256, DIM, HEADS)
        x = jax.random.normal(ks[0], (b, n, dim), dtype=jnp.float32)
        w_qkv = jax.random.normal(ks[1], (3 * dim, dim), dtype=jnp.float32) / np.sqrt(dim)
        w_out = jax.random.normal(ks[2], (dim, dim), dtype=jnp.float32) / np.sqrt(dim)
        b_out = jax.random.normal(ks[3], (dim,), dtype=jnp.float32) * 0.02
        norm_g = jnp.ones((1, h, 1, 1), dtype=jnp.float32)
        norm_b = jnp.zeros((1, h, 1, 1), dtype=jnp.float32)
        return {'x': x, 'w_qkv': w_qkv, 'w_out': w_out, 'b_out': b_out, 'norm_g': norm_g, 'norm_b': norm_b}
    _L0_attn_in = _L0_attn_setup()

    def _L0_ffn_setup():
        import jax, jax.numpy as jnp
        import numpy as np
        DIM = 128
        DEPTH = 6
        HEADS = 16
        DIM_HEAD = 64
        WINDOW = 32
        INNER = HEADS * DIM_HEAD
        DIM_INNER = int(DIM * 4 * 2 / 3)
        QK_SCALE = 8.0

        def shift_tokens(t):
            a, s = jnp.split(t, 2, -1)
            s = jnp.pad(s, ((0, 0), (1, 0), (0, 0)))[:, :-1]
            return jnp.concatenate([a, s], -1)

        def l2norm(t):
            return t / jnp.maximum(jnp.linalg.norm(t, axis=-1, keepdims=True), 1e-12)

        def rotate_half(x):
            x1, x2 = jnp.split(x, 2, -1)
            return jnp.concatenate([-x2, x1], -1)

        def rotary_tables(n):
            half = jnp.arange(0, DIM_HEAD, 2, dtype=jnp.float32)
            inv_freq = 1.0 / 10000.0 ** (half / DIM_HEAD)
            t = jnp.arange(n, dtype=jnp.float32)
            freqs = t[:, None] * inv_freq[None, :]
            freqs = jnp.concatenate([freqs, freqs], -1)
            base_scale = (half + 0.4 * DIM_HEAD) / (1.4 * DIM_HEAD)
            power = (t - n // 2) / (WINDOW // 2)
            scale = base_scale[None, :] ** power[:, None]
            scale = jnp.concatenate([scale, scale], -1)
            return (freqs, scale)

        def local_attention(q, k, v):
            b, h, n, d = q.shape
            w = WINDOW
            nw = n // w
            bq = q.reshape(b, h, nw, w, d)
            bk = k.reshape(b, h, nw, w, d)
            bv = v.reshape(b, h, nw, w, d)

            def look(t):
                p = jnp.pad(t, ((0, 0), (0, 0), (1, 0), (0, 0), (0, 0)))
                return jnp.concatenate([p[:, :, :nw], p[:, :, 1:]], axis=3)
            bk2, bv2 = (look(bk), look(bv))
            seq = jnp.arange(n).reshape(nw, w)
            seq_p = jnp.pad(seq, ((1, 0), (0, 0)), constant_values=-1)
            jt = jnp.concatenate([seq_p[:nw], seq_p[1:]], axis=1)
            it = seq[:, :, None]
            jb = jt[:, None, :]
            mask = (it < jb) | (it > jb + w) | (jb == -1)
            sim = jnp.einsum('bhwie,bhwje->bhwij', bq, bk2) * QK_SCALE
            sim = jnp.where(mask, -jnp.finfo(sim.dtype).max, sim)
            attn = jax.nn.softmax(sim, -1)
            out = jnp.einsum('bhwij,bhwje->bhwie', attn, bv2)
            return out.reshape(b, h, n, d)

        def attn_layer(x, Wqkv, qs, ksc, Wo):
            b, n, _ = x.shape
            qkv = x @ Wqkv
            q, k, v = jnp.split(qkv, 3, -1)
            sh = lambda t: t.reshape(b, n, HEADS, DIM_HEAD).transpose(0, 2, 1, 3)
            q, k, v = (sh(q), sh(k), sh(v))
            q = l2norm(q) * qs
            k = l2norm(k) * ksc
            freqs, scale = rotary_tables(n)
            cos, sin = (jnp.cos(freqs), jnp.sin(freqs))
            q = q * cos * scale + rotate_half(q) * sin * scale
            inv = 1.0 / scale
            k = k * cos * inv + rotate_half(k) * sin * inv
            out = local_attention(q, k, v)
            out = out.transpose(0, 2, 1, 3).reshape(b, n, INNER)
            return out @ Wo

        def ffn_layer(x, g, bln, W1, b1, W2, b2):
            mu = x.mean(-1, keepdims=True)
            var = ((x - mu) ** 2).mean(-1, keepdims=True)
            xn = (x - mu) / jnp.sqrt(var + 1e-05) * g + bln
            hg = xn @ W1 + b1
            a, gate = jnp.split(hg, 2, -1)
            return a * jax.nn.gelu(gate, approximate=False) @ W2 + b2
        key = jax.random.key(seed)
        ks = jax.random.split(key, 8)
        B, N = (2, 256)
        init = lambda k, shape: jax.random.normal(k, shape, jnp.float32) * 0.02
        return {'x': jax.random.normal(ks[0], (B, N, DIM), jnp.float32), 'Wqkv': init(ks[1], (DEPTH, DIM, 3 * INNER)), 'q_scale': jnp.ones((DEPTH, DIM_HEAD), jnp.float32), 'k_scale': jnp.ones((DEPTH, DIM_HEAD), jnp.float32), 'Wo': init(ks[2], (DEPTH, INNER, DIM)), 'ln_g': jnp.ones((DEPTH, DIM), jnp.float32), 'ln_b': jnp.zeros((DEPTH, DIM), jnp.float32), 'W1': init(ks[3], (DEPTH, DIM, 2 * DIM_INNER)), 'b1': jnp.zeros((DEPTH, 2 * DIM_INNER), jnp.float32), 'W2': init(ks[4], (DEPTH, DIM_INNER, DIM)), 'b2': jnp.zeros((DEPTH, DIM), jnp.float32)}
    _L0_ffn_in = _L0_ffn_setup()

    def _L1_attn_setup():
        import jax, jax.numpy as jnp
        import numpy as np
        from math import log, sqrt
        B, S, D, H = (2, 256, 128, 16)
        HD = D // H
        NUM_BUCKETS = 32
        MAX_DISTANCE = 128
        ROPE_BASE = 10000.0

        def _rope_cos_sin(seq_len, dim, base):
            inv_freq = 1.0 / base ** (jnp.arange(0, dim, 2, dtype=jnp.float32) / dim)
            t = jnp.arange(seq_len, dtype=jnp.float32)
            freqs = jnp.outer(t, inv_freq)
            emb = jnp.concatenate([freqs, freqs], axis=-1)
            return (jnp.cos(emb), jnp.sin(emb))

        def _rotate_half(t):
            d = t.shape[-1] // 2
            return jnp.concatenate([-t[..., d:], t[..., :d]], axis=-1)

        def _rel_pos_bucket(relative_position, num_buckets, max_distance):
            rp = -jnp.minimum(relative_position, 0)
            max_exact = num_buckets // 2
            is_small = rp < max_exact
            rp_f = jnp.maximum(rp.astype(jnp.float32), 1.0)
            large = max_exact + (jnp.log(rp_f / max_exact) / log(max_distance / max_exact) * (num_buckets - max_exact)).astype(jnp.int32)
            large = jnp.minimum(large, num_buckets - 1)
            return jnp.where(is_small, rp, large)
        key = jax.random.key(seed)
        kx, kq, kk, kv, ko, kr = jax.random.split(key, 6)
        scale = 0.02
        return {'x': jax.random.normal(kx, (B, S, D), dtype=jnp.float32), 'Wq': jax.random.normal(kq, (D, D), dtype=jnp.float32) * scale, 'Wk': jax.random.normal(kk, (D, D), dtype=jnp.float32) * scale, 'Wv': jax.random.normal(kv, (D, D), dtype=jnp.float32) * scale, 'Wo': jax.random.normal(ko, (D, D), dtype=jnp.float32) * scale, 'rel_emb': jax.random.normal(kr, (NUM_BUCKETS, H), dtype=jnp.float32) * scale}
    _L1_attn_in = _L1_attn_setup()

    def _L1_ffn_setup():
        import jax, jax.numpy as jnp
        import numpy as np
        HIDDEN = 128
        FFN = 4 * HIDDEN
        NUM_EXPERTS = 8
        TOP_K = 2
        B, S = (4, 256)
        key = jax.random.key(seed)
        ks = jax.random.split(key, 7)
        scale = 0.02
        return {'x': jax.random.normal(ks[0], (B, S, HIDDEN), dtype=jnp.float32), 'gate_w': jax.random.normal(ks[1], (HIDDEN, NUM_EXPERTS), dtype=jnp.float32) * scale, 'gate_b': jnp.zeros((NUM_EXPERTS,), dtype=jnp.float32), 'w1': jax.random.normal(ks[2], (NUM_EXPERTS, HIDDEN, FFN), dtype=jnp.float32) * scale, 'b1': jnp.zeros((NUM_EXPERTS, FFN), dtype=jnp.float32), 'w2': jax.random.normal(ks[3], (NUM_EXPERTS, FFN, HIDDEN), dtype=jnp.float32) * scale, 'b2': jnp.zeros((NUM_EXPERTS, HIDDEN), dtype=jnp.float32)}
    _L1_ffn_in = _L1_ffn_setup()
    _d = {'L0_attn_x': _L0_attn_in['x'], 'L0_attn_w_qkv': _L0_attn_in['w_qkv'], 'L0_attn_w_out': _L0_attn_in['w_out'], 'L0_attn_b_out': _L0_attn_in['b_out'], 'L0_attn_norm_g': _L0_attn_in['norm_g'], 'L0_attn_norm_b': _L0_attn_in['norm_b'], 'L0_ffn_Wqkv': _L0_ffn_in['Wqkv'], 'L0_ffn_q_scale': _L0_ffn_in['q_scale'], 'L0_ffn_k_scale': _L0_ffn_in['k_scale'], 'L0_ffn_Wo': _L0_ffn_in['Wo'], 'L0_ffn_ln_g': _L0_ffn_in['ln_g'], 'L0_ffn_ln_b': _L0_ffn_in['ln_b'], 'L0_ffn_W1': _L0_ffn_in['W1'], 'L0_ffn_b1': _L0_ffn_in['b1'], 'L0_ffn_W2': _L0_ffn_in['W2'], 'L0_ffn_b2': _L0_ffn_in['b2'], 'L1_attn_Wq': _L1_attn_in['Wq'], 'L1_attn_Wk': _L1_attn_in['Wk'], 'L1_attn_Wv': _L1_attn_in['Wv'], 'L1_attn_Wo': _L1_attn_in['Wo'], 'L1_attn_rel_emb': _L1_attn_in['rel_emb'], 'L1_ffn_gate_w': _L1_ffn_in['gate_w'], 'L1_ffn_gate_b': _L1_ffn_in['gate_b'], 'L1_ffn_w1': _L1_ffn_in['w1'], 'L1_ffn_b1': _L1_ffn_in['b1'], 'L1_ffn_w2': _L1_ffn_in['w2'], 'L1_ffn_b2': _L1_ffn_in['b2']}
    _x0 = _d['L0_attn_x']
    _d['L0_attn_x'] = jax.random.normal(jax.random.fold_in(jax.random.key(seed), 1), (8, 256, 128), dtype=_x0.dtype)
    del _x0
    return _d

def reference(L0_attn_x, L0_attn_w_qkv, L0_attn_w_out, L0_attn_b_out, L0_attn_norm_g, L0_attn_norm_b, L0_ffn_Wqkv, L0_ffn_q_scale, L0_ffn_k_scale, L0_ffn_Wo, L0_ffn_ln_g, L0_ffn_ln_b, L0_ffn_W1, L0_ffn_b1, L0_ffn_W2, L0_ffn_b2, L1_attn_Wq, L1_attn_Wk, L1_attn_Wv, L1_attn_Wo, L1_attn_rel_emb, L1_ffn_gate_w, L1_ffn_gate_b, L1_ffn_w1, L1_ffn_b1, L1_ffn_w2, L1_ffn_b2):

    def _L0_attn_ref(x, w_qkv, w_out, b_out, norm_g, norm_b):
        import jax, jax.numpy as jnp
        import numpy as np
        DIM = 128
        HEADS = 16
        EPS = 1e-12
        b, n, dim = x.shape
        h = HEADS
        d = dim // h
        qkv = jnp.einsum('bnm,om->bno', x, w_qkv)
        qkv = qkv.reshape(b, n, 3, h, d)
        q, k, v = [jnp.transpose(qkv[:, :, i], (0, 2, 1, 3)) for i in range(3)]
        dots = jnp.einsum('bhid,bhjd->bhij', q, k)
        norm = jnp.sqrt(jnp.sum(dots * dots, axis=-1, keepdims=True))
        attn = dots / jnp.maximum(norm, EPS) * norm_g + norm_b
        out = jnp.einsum('bhij,bhjd->bhid', attn, v)
        out = jnp.transpose(out, (0, 2, 1, 3)).reshape(b, n, dim)
        return jnp.einsum('bnm,om->bno', out, w_out) + b_out

    def _L0_ffn_ref(x, Wqkv, q_scale, k_scale, Wo, ln_g, ln_b, W1, b1, W2, b2):
        import jax, jax.numpy as jnp
        import numpy as np
        DIM = 128
        DEPTH = 6
        HEADS = 16
        DIM_HEAD = 64
        WINDOW = 32
        INNER = HEADS * DIM_HEAD
        DIM_INNER = int(DIM * 4 * 2 / 3)
        QK_SCALE = 8.0

        def shift_tokens(t):
            a, s = jnp.split(t, 2, -1)
            s = jnp.pad(s, ((0, 0), (1, 0), (0, 0)))[:, :-1]
            return jnp.concatenate([a, s], -1)

        def l2norm(t):
            return t / jnp.maximum(jnp.linalg.norm(t, axis=-1, keepdims=True), 1e-12)

        def rotate_half(x):
            x1, x2 = jnp.split(x, 2, -1)
            return jnp.concatenate([-x2, x1], -1)

        def rotary_tables(n):
            half = jnp.arange(0, DIM_HEAD, 2, dtype=jnp.float32)
            inv_freq = 1.0 / 10000.0 ** (half / DIM_HEAD)
            t = jnp.arange(n, dtype=jnp.float32)
            freqs = t[:, None] * inv_freq[None, :]
            freqs = jnp.concatenate([freqs, freqs], -1)
            base_scale = (half + 0.4 * DIM_HEAD) / (1.4 * DIM_HEAD)
            power = (t - n // 2) / (WINDOW // 2)
            scale = base_scale[None, :] ** power[:, None]
            scale = jnp.concatenate([scale, scale], -1)
            return (freqs, scale)

        def local_attention(q, k, v):
            b, h, n, d = q.shape
            w = WINDOW
            nw = n // w
            bq = q.reshape(b, h, nw, w, d)
            bk = k.reshape(b, h, nw, w, d)
            bv = v.reshape(b, h, nw, w, d)

            def look(t):
                p = jnp.pad(t, ((0, 0), (0, 0), (1, 0), (0, 0), (0, 0)))
                return jnp.concatenate([p[:, :, :nw], p[:, :, 1:]], axis=3)
            bk2, bv2 = (look(bk), look(bv))
            seq = jnp.arange(n).reshape(nw, w)
            seq_p = jnp.pad(seq, ((1, 0), (0, 0)), constant_values=-1)
            jt = jnp.concatenate([seq_p[:nw], seq_p[1:]], axis=1)
            it = seq[:, :, None]
            jb = jt[:, None, :]
            mask = (it < jb) | (it > jb + w) | (jb == -1)
            sim = jnp.einsum('bhwie,bhwje->bhwij', bq, bk2) * QK_SCALE
            sim = jnp.where(mask, -jnp.finfo(sim.dtype).max, sim)
            attn = jax.nn.softmax(sim, -1)
            out = jnp.einsum('bhwij,bhwje->bhwie', attn, bv2)
            return out.reshape(b, h, n, d)

        def attn_layer(x, Wqkv, qs, ksc, Wo):
            b, n, _ = x.shape
            qkv = x @ Wqkv
            q, k, v = jnp.split(qkv, 3, -1)
            sh = lambda t: t.reshape(b, n, HEADS, DIM_HEAD).transpose(0, 2, 1, 3)
            q, k, v = (sh(q), sh(k), sh(v))
            q = l2norm(q) * qs
            k = l2norm(k) * ksc
            freqs, scale = rotary_tables(n)
            cos, sin = (jnp.cos(freqs), jnp.sin(freqs))
            q = q * cos * scale + rotate_half(q) * sin * scale
            inv = 1.0 / scale
            k = k * cos * inv + rotate_half(k) * sin * inv
            out = local_attention(q, k, v)
            out = out.transpose(0, 2, 1, 3).reshape(b, n, INNER)
            return out @ Wo

        def ffn_layer(x, g, bln, W1, b1, W2, b2):
            mu = x.mean(-1, keepdims=True)
            var = ((x - mu) ** 2).mean(-1, keepdims=True)
            xn = (x - mu) / jnp.sqrt(var + 1e-05) * g + bln
            hg = xn @ W1 + b1
            a, gate = jnp.split(hg, 2, -1)
            return a * jax.nn.gelu(gate, approximate=False) @ W2 + b2
        for i in range(DEPTH):
            x = attn_layer(shift_tokens(x), Wqkv[i], q_scale[i], k_scale[i], Wo[i]) + x
            x = ffn_layer(shift_tokens(x), ln_g[i], ln_b[i], W1[i], b1[i], W2[i], b2[i]) + x
        return x

    def _L1_attn_ref(x, Wq, Wk, Wv, Wo, rel_emb):
        import jax, jax.numpy as jnp
        import numpy as np
        from math import log, sqrt
        B, S, D, H = (2, 256, 128, 16)
        HD = D // H
        NUM_BUCKETS = 32
        MAX_DISTANCE = 128
        ROPE_BASE = 10000.0

        def _rope_cos_sin(seq_len, dim, base):
            inv_freq = 1.0 / base ** (jnp.arange(0, dim, 2, dtype=jnp.float32) / dim)
            t = jnp.arange(seq_len, dtype=jnp.float32)
            freqs = jnp.outer(t, inv_freq)
            emb = jnp.concatenate([freqs, freqs], axis=-1)
            return (jnp.cos(emb), jnp.sin(emb))

        def _rotate_half(t):
            d = t.shape[-1] // 2
            return jnp.concatenate([-t[..., d:], t[..., :d]], axis=-1)

        def _rel_pos_bucket(relative_position, num_buckets, max_distance):
            rp = -jnp.minimum(relative_position, 0)
            max_exact = num_buckets // 2
            is_small = rp < max_exact
            rp_f = jnp.maximum(rp.astype(jnp.float32), 1.0)
            large = max_exact + (jnp.log(rp_f / max_exact) / log(max_distance / max_exact) * (num_buckets - max_exact)).astype(jnp.int32)
            large = jnp.minimum(large, num_buckets - 1)
            return jnp.where(is_small, rp, large)
        b, s, d = x.shape

        def heads_split(t):
            return t.reshape(b, s, H, HD).transpose(0, 2, 1, 3)
        q = heads_split(x @ Wq)
        k = heads_split(x @ Wk)
        v = heads_split(x @ Wv)
        cos, sin = _rope_cos_sin(s, HD, ROPE_BASE)
        q = q * cos + _rotate_half(q) * sin
        k = k * cos + _rotate_half(k) * sin
        pos = jnp.arange(s, dtype=jnp.int32)
        rel = pos[None, :] - pos[:, None]
        buckets = _rel_pos_bucket(rel, NUM_BUCKETS, MAX_DISTANCE)
        bias = rel_emb[buckets].transpose(2, 0, 1)[None]
        scores = jnp.einsum('bhqd,bhkd->bhqk', q, k) / sqrt(HD) + bias
        causal = jnp.tril(jnp.ones((s, s), dtype=bool))
        scores = jnp.where(causal, scores, jnp.float32(-1000000000.0))
        attn = jax.nn.softmax(scores, axis=-1)
        ctx = jnp.einsum('bhqk,bhkd->bhqd', attn, v)
        ctx = ctx.transpose(0, 2, 1, 3).reshape(b, s, d)
        return ctx @ Wo

    def _L1_ffn_ref(x, gate_w, gate_b, w1, b1, w2, b2):
        import jax, jax.numpy as jnp
        import numpy as np
        HIDDEN = 128
        FFN = 4 * HIDDEN
        NUM_EXPERTS = 8
        TOP_K = 2
        B, S = (4, 256)
        b, s, h = x.shape
        xt = x.reshape(b * s, h)
        probs = jax.nn.softmax(xt @ gate_w + gate_b, axis=-1)
        _, idx = jax.lax.top_k(probs, TOP_K)
        one_hot = jax.nn.one_hot(idx, NUM_EXPERTS, dtype=xt.dtype)
        mask = (one_hot.sum(axis=1) > 0).astype(xt.dtype)
        h1 = jax.nn.relu(jnp.einsum('th,ehf->etf', xt, w1) + b1[:, None, :])
        out_e = jnp.einsum('etf,efh->eth', h1, w2) + b2[:, None, :]
        out = jnp.einsum('eth,te->th', out_e, mask)
        return out.reshape(b, s, h)
    x = L0_attn_x
    x = x + _layernorm(_L0_attn_ref(_layernorm(x, axis=-1), L0_attn_w_qkv, L0_attn_w_out, L0_attn_b_out, L0_attn_norm_g, L0_attn_norm_b), axis=-1)
    x = x + _layernorm(_L0_ffn_ref(_layernorm(x, axis=-1), L0_ffn_Wqkv, L0_ffn_q_scale, L0_ffn_k_scale, L0_ffn_Wo, L0_ffn_ln_g, L0_ffn_ln_b, L0_ffn_W1, L0_ffn_b1, L0_ffn_W2, L0_ffn_b2), axis=-1)
    x = x + _layernorm(_L1_attn_ref(_layernorm(x, axis=-1), L1_attn_Wq, L1_attn_Wk, L1_attn_Wv, L1_attn_Wo, L1_attn_rel_emb), axis=-1)
    x = x + _layernorm(_L1_ffn_ref(_layernorm(x, axis=-1), L1_ffn_gate_w, L1_ffn_gate_b, L1_ffn_w1, L1_ffn_b1, L1_ffn_w2, L1_ffn_b2), axis=-1)
    return x

_drawn_inputs = setup_inputs


def setup_inputs(seed=0):
    import zlib

    import numpy as np

    out = dict(_drawn_inputs(seed))
    spreads = {'L0_attn_norm_g': (1.0, 0.2),
     'L0_attn_norm_b': (0.0, 0.1),
     'L0_ffn_q_scale': (1.0, 0.573),
     'L0_ffn_k_scale': (1.0, 0.2),
     'L0_ffn_ln_g': (1.0, 0.554),
     'L0_ffn_ln_b': (0.0, 0.46),
     'L0_ffn_b1': (0.0, 0.1),
     'L0_ffn_b2': (0.0, 0.1),
     'L1_ffn_gate_b': (0.0, 0.1),
     'L1_ffn_b1': (0.0, 0.1),
     'L1_ffn_b2': (0.0, 0.1)}
    factors = {'L1_attn_rel_emb': 3.614}
    for name, (base, spread) in spreads.items():
        noise = np.random.default_rng([zlib.crc32(name.encode()), seed]).standard_normal(out[name].shape)
        drawn = base * np.exp(spread * noise) if base else spread * noise
        out[name] = jnp.asarray(drawn.astype(out[name].dtype))
    for name, factor in factors.items():
        out[name] = (out[name] * factor).astype(out[name].dtype)
    return out
```

```python
from contextlib import ExitStack

import concourse.bass as bass
from concourse import mybir
from concourse.alu_op_type import AluOpType as ALU

ACT = mybir.ActivationFunctionType
F32 = mybir.dt.float32
BF16 = mybir.dt.bfloat16
AX = mybir.AxisListType.X

P = 128
B, S, DIM, H = 8, 256, 128, 16
TOK = B * S
DEPTH = 6
ITEMS = DEPTH * B
DH = 64
PAIRS = H // 2
WIN = 32
NW = S // WIN
FF = int(DIM * 4 * 2 / 3)
FFR = FF - 2 * P
HD = DIM // H
NE, EF = 8, 512
VB = 2 * (DH + 1)
KW = WIN + S

WIDTHS = [("ident", P), ("onesm", P), ("blk", P), ("rot", 4 * 2 * DH), ("headm", H),
          ("rope", 4 * S), ("onehot", 384), ("neg", 384), ("lower", NE * NE), ("upper", NE * NE),
          ("eps", 1), ("ones", WIN), ("mhalf", PAIRS)]
COL = {}
NCONST = 0
for _name, _width in WIDTHS:
    COL[_name] = (NCONST, NCONST + _width)
    NCONST += _width

LN_S1 = 0
LN_S2 = LN_S1 + 3 * (B // 2)
LN_S3 = LN_S2 + ITEMS
LN_S4 = LN_S3 + 3 * B


JOBS = [job for n in range(0, H, 4)
        for job in ((0, range(n, n + 4)), (1, range(n, n + 2)), (1, range(n + 2, n + 4)))]
NJ = len(JOBS)
GATE_OPS = 19


def wait(eng, s, value):
    if not isinstance(value, int) or value > 0:
        eng.wait_ge(s, value)


def build(nc, a, out):
    ctx = ExitStack()
    with ctx:
        def sb(name, shape, dt=F32):
            return ctx.enter_context(nc.sbuf_tensor(name, shape, dt))

        def sem(name):
            return ctx.enter_context(nc.semaphore(name))

        bank = [ctx.enter_context(nc.psum_tensor(f"bank{i}", [P, 512], F32)) for i in range(5)]
        obank = ctx.enter_context(nc.psum_tensor("obank", [P, 2, 512], F32))
        lnbank = ctx.enter_context(nc.psum_tensor("lnbank", [P, 512], F32))

        cst = sb("cst", [P, NCONST])
        cbf = sb("cbf", [P, P + 2 * 512], BF16)

        def const(name):
            return cst[:, COL[name][0]:COL[name][1]]

        ident, onesm, blk = const("ident"), const("onesm"), const("blk")
        eps = const("eps")
        ident_bf = cbf[:, 0:P]
        maskv = cbf[:, P:].rearrange("p (r n) -> p r n", r=2)
        X = sb("X", [P, B, S])
        Z = sb("Z", [P, B, S])
        work = sb("work", [P, 4, 2, 512])
        xin = work[:, 0:2].rearrange("p k a (i m) -> p (k a i) m", m=DIM)
        lnd = sb("lnd", [P, 512])
        lnsq = sb("lnsq", [P, 512])
        lnsd = sb("lnsd", [P, 512])
        lnt = sb("lnt", [P, 512])
        lnr = sb("lnr", [P, 512])

        wqk = sb("wqk", [P, 2 * H * DH])
        wv = sb("wv", [P, H * DH])
        wo = sb("wo", [P, PAIRS, DIM])
        w1 = sb("w1", [P, 2 * FF])
        w2 = sb("w2", [P, 3, DIM])
        lng = sb("lng", [P, DEPTH])
        lnb = sb("lnb", [P, DEPTH])
        b2c = sb("b2c", [P, DEPTH])
        b1a = sb("b1a", [P, 3, DEPTH])
        b1g = sb("b1g", [P, 3, DEPTH])
        scales = sb("scales", [P, 2, DEPTH, DH])
        tab = sb("tab", [P, DEPTH, 4, 2, DH])
        touch = sb("touch", [P, 8])
        xs = sb("xs", [P, KW])
        xf = sb("xf", [P, S])
        sq = work[:, 0]
        n2 = sb("n2", [P, 2, PAIRS])
        n2m = sb("n2m", [P, 2, PAIRS])
        rn = sb("rn", [P, 2, PAIRS])
        qn = work[:, 1]
        t1 = work[:, 2]
        t2 = work[:, 3]
        rot = sb("rot", [P, 2, 2, H * DH])
        qT = sb("qT", [P, PAIRS, S])
        kT = sb("kT", [P, PAIRS, 2, KW])
        vp = sb("vp", [P, NW, PAIRS, VB])
        mx = sb("mx", [P, 2, PAIRS])
        sh = sb("sh", [P, 2, 512])
        px = sb("px", [P, 2, 512])
        pT = sb("pT", [P, 2, 512])
        rd = sb("rd", [P, 2, PAIRS])
        ao = sb("ao", [P, 2, 512])
        aoT = sb("aoT", [P, PAIRS, S])
        ge = sb("ge", [P, 3, S])
        hT = sb("hT", [P, 3, S])

        vflat = vp[:, :, :, :].rearrange("p w q n -> p (w q n)")
        qTf = qT[:, :, :].rearrange("p a t -> p (a t)")
        aoTf = aoT[:, :, :].rearrange("p a t -> p (a t)")
        kTf = kT[:, :, :, :].rearrange("p a b t -> p (a b t)")
        rotf = rot[:, :, :, :].rearrange("p r k n -> p (r k n)")
        w1raw = rotf[:, 0:512].rearrange("p (c m) -> p c m", c=4)
        w1t = rotf[:, 512:1024]
        s1xn, s1q, s1pr, s1n2 = (qTf[:, 512 * i:512 * i + 512] for i in range(4))
        s1nr, s1qg, s1o, s1y = (aoTf[:, 512 * i:512 * i + 512] for i in range(4))
        s1kv = rotf[:, 1024:2048].rearrange("p (i n) -> p i n", i=4)
        s1bd = rotf[:, 2048:2560].rearrange("p (c n) -> p c n", c=4)
        s1bv = rotf[:, 2560:2562]
        nrm = sb("nrm", [P, 2])
        bout = sb("bout", [P, 1])
        bias = kTf[:, 0:H * S].rearrange("p (h t) -> p h t", h=H)
        relv = sb("relv", [WIN, H])
        uh = sb("uh", [H, 384])
        relu_dram = nc.dram_tensor("rel_by_distance", [H, 384], F32)
        s3w = wqk[:, 0:5 * P]
        s3wo = wv[:, 0:4 * P].rearrange("p (g n) -> p g n", g=4)
        s3xn = t1[:, 0, 0:S]
        s3part = qn
        s3den = sq
        s3q, s3k = t1[:, 1, 0:S], t1[:, 1, S:2 * S]
        qm = rotf.rearrange("p (h t) -> p h t", h=H)
        vs = qTf[:, 0:2 * H * WIN].rearrange("p (i h n) -> p i h n", i=2, h=H)
        s3s = sh
        s3nm = mx[:, :, 0:4]
        s3ot = aoTf[:, 0:4 * S].rearrange("p (g t) -> p g t", g=4)
        s3y = aoTf[:, 4 * S:5 * S]
        mw1 = vflat[:, 0:NE * EF].rearrange("p (e f) -> p e f", e=NE)
        mw2 = vflat[:, NE * EF:2 * NE * EF].rearrange("p (e c n) -> p e c n", e=NE, c=4)
        gw = sb("gw", [P, NE])
        gb = sb("gb", [P, NE])
        mb1 = sb("mb1", [P, NE, 4])
        mb2 = sb("mb2", [P, NE, DIM])
        s4xn = t1[:, 0, :]
        s4x = ao[:, 0, :]
        s4xt = t1[:, 1, :]
        h1 = rotf.rearrange("p (s f n) -> p s f n", s=2, f=4)
        lg, lh, pe_, pr_ = (sb(f"gate{i}", [P, 4, NE]) for i in range(4))
        g1 = sb("g1", [P, 4])
        g2 = sb("g2", [P, 4])
        cmp1, cmp2, cmp3 = (ge[:, i, :].rearrange("p (i n) -> p i n", i=4) for i in range(3))
        cmp4 = hT[:, 0, :].rearrange("p (i n) -> p i n", i=4)
        rank = sb("rank", [P, 4, NE])
        msk = sb("msk", [P, 4, NE])
        ob2 = qn
        oms = t2
        acc = ao[:, 1, :]
        st = sb("st", [P, 4, 4])
        yc = sh[:, 0, :]
        ysq = sh[:, 1, :]
        yn = px[:, 0, :]
        outs = px[:, 1, :]

        ld_const, ld_x, ld_s1, ld_vec = sem("ld_const"), sem("ld_x"), sem("ld_s1"), sem("ld_vec")
        ld_qk, ld_v, ld_c = sem("ld_qk"), sem("ld_v"), sem("ld_c")
        ld_s3, ld_s4, ld_gate = sem("ld_s3"), sem("ld_s4"), sem("ld_gate")
        rel_in = sem("rel_in")
        stored = sem("stored")
        cleared, tab_done, masks_cast = sem("cleared"), sem("tab_done"), sem("masks_cast")
        ln_mean, ln_d, ln_sq, ln_var, ln_std, ln_rec = (sem("ln_" + n) for n in ("mean", "d", "sq", "var", "std", "rec"))
        s1 = {n: sem("s1_" + n) for n in ("wt", "wts", "xt", "x", "xn", "qkv", "sb", "g", "bd", "u", "pr", "n2",
                                          "n2m", "nr", "rn", "qg", "o", "os", "y", "ys", "t", "x1")}
        z_ready = sem("z_ready")
        xs_ready = sem("xs_ready")
        p_full = sem("p_full")
        vt_free = sem("vt_free")
        sq_done, n2_done, n2_raw, rn_done = sem("sq_done"), sem("n2_done"), sem("n2_raw"), sem("rn_done")
        qn_done, t1_done, t2_done, rot_done = sem("qn_done"), sem("t1_done"), sem("t2_done"), sem("rot_done")
        s_full = [sem("s0_full"), sem("s1_full")]
        mx_done, sh_done, px_done = sem("mx_done"), sem("sh_done"), sem("px_done")
        pt_full, pt_done = sem("pt_full"), sem("pt_done")
        o_full, rd_done, ao_done = sem("o_full"), sem("rd_done"), sem("ao_done")
        z1_done, xf_ready, xg_done, ffn_in = sem("z1_done"), sem("xf_ready"), sem("xg_done"), sem("ffn_in")
        ge_done, h_done = sem("ge_done"), sem("h_done")
        s3 = {n: sem("s3_" + n) for n in ("w", "t", "xn", "qkv", "part", "qk", "qm", "v", "full", "add", "mx", "px",
                                          "ptf", "pts", "pv", "den", "ot", "y", "ys", "u", "ub")}
        x2_ready, x3_ready = sem("x2_ready"), sem("x3_ready")
        s4 = {n: sem("s4_" + n) for n in ("xn", "gate", "xc", "xt", "xts", "d", "ex", "hf", "relu", "of", "ofr", "om", "acc",
                                          "ysq", "ystd", "out")}

        block = ctx.enter_context(nc.Block())

        @block.sync
        def _(sp):
            sp.dma_start(cst[:, :], a["consts"]).then_inc(ld_const, 16)
            sp.dma_start(xin[:, :, :], a["L0_attn_x"].rearrange("b (i p) m -> p (b i) m", p=P)).then_inc(ld_x, 16)
            sp.dma_start(w1raw[:, 0:3, :], a["L0_attn_w_qkv"].rearrange("(c p) m -> p c m", p=P)).then_inc(ld_s1, 16)
            sp.dma_start(w1raw[:, 3, :], a["L0_attn_w_out"]).then_inc(ld_s1, 16)
            sp.dma_start(bout[:, :], a["L0_attn_b_out"].rearrange("(p o) -> p o", o=1)).then_inc(ld_s1, 16)
            for col, name in enumerate(("L0_attn_norm_g", "L0_attn_norm_b")):
                per_head = a[name].rearrange("o h c d -> h (o c d)")
                sp.dma_start(nrm[:, col:col + 1], bass.AP(per_head.tensor, 0, [[1, H], [0, HD], [1, 1]])).then_inc(ld_s1, 16)
            sp.dma_start(work[:, 2], a["window_masks"].rearrange("p (r n) -> p r n", r=2)).then_inc(ld_const, 16)
            sp.dma_start(relv[:, :], a["L1_attn_rel_emb"]).then_inc(ld_const, 16)
            for k, name in enumerate(("L0_ffn_q_scale", "L0_ffn_k_scale")):
                sp.dma_start(scales[:, k, :, :].rearrange("p l d -> p (l d)"),
                             a[name].rearrange("l d -> (l d)").partition_broadcast(P)).then_inc(ld_vec, 16)

            def load_qk(l):
                sp.dma_start(wqk[:, :], a["L0_ffn_Wqkv"][l, :, 0:2 * H * DH]).then_inc(ld_qk, 16)

            def load_v(l):
                sp.dma_start(wv[:, :], a["L0_ffn_Wqkv"][l, :, 2 * H * DH:3 * H * DH]).then_inc(ld_v, 16)

            def load_c(l):
                sp.dma_start(wo[:, :, :], a["L0_ffn_Wo"][l].rearrange("(c p) n -> p c n", p=P)).then_inc(ld_c, 16)
                sp.dma_start(w1[:, :], a["L0_ffn_W1"][l]).then_inc(ld_c, 16)
                sp.dma_start(w2[:, 0:2, :], a["L0_ffn_W2"][l, 0:2 * P, :].rearrange("(c p) n -> p c n", p=P)).then_inc(ld_c, 16)
                sp.dma_start(w2[0:FFR, 2, :], a["L0_ffn_W2"][l, 2 * P:FF, :]).then_inc(ld_c, 16)

            load_qk(0)
            load_v(0)
            sp.wait_ge(cleared, 1)
            load_c(0)
            for t, name in ((lng, "L0_ffn_ln_g"), (lnb, "L0_ffn_ln_b"), (b2c, "L0_ffn_b2")):
                sp.dma_start(t[:, :], a[name].rearrange("l p -> p l"), allow_slow_non_contiguous=True).then_inc(ld_vec, 16)
            for half, t in ((0, b1a), (1, b1g)):
                for c in range(3):
                    n = P if c < 2 else FFR
                    lo = half * FF + c * P
                    sp.dma_start(t[0:n, c, :], a["L0_ffn_b1"][:, lo:lo + n].rearrange("l p -> p l"), allow_slow_non_contiguous=True).then_inc(ld_vec, 16)
            sp.wait_ge(s3["ub"], 1)
            sp.dma_start(relu_dram.ap(), uh[:, :]).then_inc(stored, 16)
            sp.wait_ge(stored, 16)
            sp.dma_start(gw[:, :], a["L1_ffn_gate_w"]).then_inc(ld_gate, 16)
            sp.dma_start(gb[:, :], a["L1_ffn_gate_b"].partition_broadcast(P)).then_inc(ld_gate, 16)
            sp.dma_start(mb1[:, :, :], a["L1_ffn_b1"].rearrange("e (c p) -> p e c", p=P), allow_slow_non_contiguous=True).then_inc(ld_gate, 16)
            sp.dma_start(mb2[:, :, :].rearrange("p e n -> p (e n)"),
                         a["L1_ffn_b2"].rearrange("e n -> (e n)").partition_broadcast(P)).then_inc(ld_gate, 16)
            with sp.Fori(1, DEPTH) as l:
                sp.wait_ge(p_full, l * (24 * B) - 16)
                load_qk(l)
                sp.wait_ge(p_full, l * (24 * B) - 8)
                load_v(l)
                sp.wait_ge(s_full[0], l * (5 * B))
                load_c(l)
            sp.wait_ge(p_full, 24 * ITEMS)
            for k, name in ((0, "L1_attn_Wq"), (2, "L1_attn_Wk"), (4, "L1_attn_Wv")):
                sp.dma_start(s3w[:, k * P:k * P + P], a[name]).then_inc(ld_s3, 16)
            sp.wait_ge(cleared, 2)
            src = a["L1_attn_Wo"].rearrange("(g j d) n -> j d g n", g=4, j=4)
            for j in range(4):
                sp.dma_start(s3wo[WIN * j:WIN * j + HD, :, :], src[j]).then_inc(ld_s3, 16)
            sp.wait_ge(o_full, 4 * ITEMS)
            sp.dma_start(bias, bass.AP(relu_dram.ap().tensor, 0, [[1, P], [384, H], [1, S]])).then_inc(rel_in, 16)
            sp.dma_start(mw1, a["L1_ffn_w1"].rearrange("e m f -> m e f")).then_inc(ld_s4, 16)
            for e in range(NE):
                sp.dma_start(mw2[:, e], a["L1_ffn_w2"][e].rearrange("(c p) n -> p c n", p=P)).then_inc(ld_s4, 16)
            outv = out.rearrange("(g b) (i p) m -> g p (b i) m", b=2, p=P)
            with sp.Fori(0, B // 2) as g:
                sp.wait_ge(s4["out"], g + 1)
                sp.dma_start(outv[g], outs.rearrange("p (i m) -> p i m", i=4)).then_inc(stored, 16)
            sp.wait_ge(stored, 16 + 16 * (B // 2))

        @block.tensor
        def _(pe):
            def ln_mean_pe(src, w, u):
                wait(pe, ln_std, u)
                nc.tensor.matmul(lnbank[:, 0:w], onesm, src, start=True, stop=True).then_inc(ln_mean, 1)

            def ln_var_pe(w, u):
                pe.wait_ge(ln_sq, u + 1)
                nc.tensor.matmul(lnbank[:, 0:w], onesm, lnsq[:, 0:w], start=True, stop=True).then_inc(ln_var, 1)

            pe.wait_ge(ld_const, 48)
            pe.wait_ge(ld_s1, 80)
            for c in range(4):
                mm = nc.tensor.transpose(bank[1][:, c * P:c * P + P], w1raw[:, c, :], ident)
            mm.then_inc(s1["wt"], 1)
            nc.tensor.matmul(bank[2][0:H, 0:384], relv[:, :], const("onehot")[0:WIN, :], start=True, stop=True).then_inc(s3["u"], 1)
            pe.wait_ge(ld_x, 16)
            pe.wait_ge(s1["wts"], 1)
            pe.wait_ge(s3["ub"], 1)
            for j in range(B // 2):
                wait(pe, s1["x"], j)
                for i in range(4):
                    mm = nc.tensor.transpose(bank[0][:, i * P:i * P + P], xin[:, 4 * j + i, :], ident)
                mm.then_inc(s1["xt"], 1)
                pe.wait_ge(s1["x"], j + 1)
                xj = X[:, 2 * j:2 * j + 2, :].rearrange("p b t -> p (b t)")
                ln_mean_pe(xj, 512, LN_S1 + 3 * j)
                ln_var_pe(512, LN_S1 + 3 * j)
                pe.wait_ge(s1["xn"], j + 1)
                nc.tensor.matmul(bank[0][:, :], w1t[:, 0:P], s1xn, start=True, stop=True)
                for i in range(4):
                    mm = nc.tensor.matmul(bank[1 + i // 2][:, (i % 2) * 256:(i % 2) * 256 + 256], s1xn[:, i * P:i * P + P],
                                          w1t[:, P:3 * P], start=True, stop=True)
                mm.then_inc(s1["qkv"], 1)
                pe.wait_ge(s1["sb"], j + 1)
                for bb in range(2):
                    for i in range(2):
                        nc.tensor.matmul(bank[3][:, bb * 256:bb * 256 + 256], s1kv[:, 2 * bb + i, 0:P], s1kv[:, 2 * bb + i, :],
                                         start=(i == 0), stop=(i == 1))
                for bb in range(2):
                    for i in range(2):
                        mm = nc.tensor.matmul(bank[4][:, 2 * bb:2 * bb + 2], s1kv[:, 2 * bb + i, P:2 * P], const("ones")[:, 0:2],
                                              start=(i == 0), stop=(i == 1))
                mm.then_inc(s1["g"], 1)
                pe.wait_ge(s1["bd"], j + 1)
                for bb in range(2):
                    mm = nc.tensor.matmul(obank[:, 0, bb * 256:bb * 256 + 256], s1bd[:, 2 * bb, :], s1q[:, bb * 256:bb * 256 + 256],
                                          start=True, stop=True)
                mm.then_inc(s1["u"], 1)
                pe.wait_ge(s1["pr"], j + 1)
                nc.tensor.matmul(obank[:, 1, :], blk, s1pr, start=True, stop=True).then_inc(s1["n2"], 1)
                pe.wait_ge(s1["qg"], j + 1)
                for bb in range(2):
                    mm = nc.tensor.matmul(obank[:, 0, bb * 256:bb * 256 + 256], s1bd[:, 2 * bb + 1, :],
                                          s1qg[:, bb * 256:bb * 256 + 256], start=True, stop=True)
                mm.then_inc(s1["o"], 1)
                pe.wait_ge(s1["os"], j + 1)
                nc.tensor.matmul(obank[:, 1, :], w1t[:, 3 * P:4 * P], s1o, start=True, stop=True).then_inc(s1["y"], 1)
                pe.wait_ge(s1["ys"], j + 1)
                ln_mean_pe(s1y, 512, LN_S1 + 3 * j + 1)
                ln_var_pe(512, LN_S1 + 3 * j + 1)
                pe.wait_ge(s1["x1"], j + 1)
                ln_mean_pe(xj, 512, LN_S1 + 3 * j + 2)
                ln_var_pe(512, LN_S1 + 3 * j + 2)

            def projection(t, c):
                r, kind, half = c // 4, (c // 2) % 2, c % 2
                if c == 0:
                    pe.wait_ge(xs_ready, t + 1)
                    pe.wait_ge(ld_qk, (t // B) * 16 + 16)
                if c < 2:
                    wait(pe, vt_free, 16 * t + c - 1)
                else:
                    pe.wait_ge(qn_done, 8 * t + c - 1)
                lo = kind * H * DH + half * 512
                nc.tensor.matmul(bank[c % 2][:, :], xs[:, WIN + r * P:WIN + r * P + P], wqk[:, lo:lo + 512],
                                 start=True, stop=True).then_inc(p_full, 1)

            def values(t, w):
                if w == 0:
                    pe.wait_ge(ld_v, (t // B) * 16 + 16)
                if w < 2:
                    pe.wait_ge(qn_done, 8 * t + 7 + w)
                else:
                    pe.wait_ge(vt_free, 16 * t + w - 1)
                for odd in range(2):
                    mm = nc.tensor.matmul(bank[w % 2][64 * odd:64 * odd + 64, :], xs[:, w * WIN:w * WIN + 2 * WIN],
                                          wv[:, :].rearrange("p (a o d) -> p o a d", o=2, d=DH)[:, odd],
                                          start=True, stop=True)
                mm.then_inc(p_full, 1)

            def turn(t, c):
                r, kind, half = c // 4, (c // 2) % 2, c % 2
                pe.wait_ge(rot_done, 8 * t + c + 1)
                pe.wait_ge(vt_free, 16 * t + 7 + c)
                for q in range(4):
                    mm = nc.tensor.transpose(bank[c % 2][:, q * P:q * P + P],
                                             rot[:, r, kind, half * 512 + q * P:half * 512 + q * P + P], ident)
                mm.then_inc(p_full, 1)

            def scores(i, k):
                r, g = k // 2, k % 2
                if k == 0:
                    pe.wait_ge(vt_free, 16 * i + 16)
                if k == 0:
                    pe.wait_ge(z_ready, B + i)
                elif k > 1:
                    pe.wait_ge(sh_done, 4 * i + k - 1)
                s = bank[2 + k % 2]
                nc.tensor.matmul(s[:, :], ident_bf, maskv[:, r, :], start=True, stop=False, skip_group_check=True)
                for q in range(4):
                    for w in range(4):
                        lo = r * P + w * WIN
                        mm = nc.tensor.matmul(s[WIN * w:WIN * w + WIN, q * P:q * P + P], qT[:, 4 * g + q, lo:lo + WIN],
                                              kT[:, 4 * g + q, :, lo:lo + 2 * WIN], start=False, stop=True,
                                              skip_group_check=True)
                mm.then_inc(s_full[k % 2], 1)

            def turn_probs(i, k):
                pe.wait_ge(px_done, 4 * i + k + 1)
                if k:
                    pe.wait_ge(pt_done, 8 * i + 2 * k)
                for q in range(4):
                    mm = nc.tensor.transpose(bank[4][:, q * P:q * P + P], px[:, k % 2, q * P:q * P + P], ident)
                mm.then_inc(pt_full, 1)

            def weigh(i, k):
                r, g = k // 2, k % 2
                pe.wait_ge(pt_done, 8 * i + 2 * k + 1)
                if k:
                    pe.wait_ge(ao_done, 4 * i + k)
                for w in range(4):
                    for q in range(4):
                        mm = nc.tensor.matmul(obank[WIN * w:WIN * w + WIN, q // 2, (q % 2) * VB:(q % 2) * VB + VB],
                                              pT[:, k % 2, q * P + w * WIN:q * P + w * WIN + WIN],
                                              vp[:, 4 * r + w, 4 * g + q, :], start=True, stop=True)
                mm.then_inc(o_full, 1)

            def turn_out(i, k):
                pe.wait_ge(ao_done, 4 * i + k + 1)
                pe.wait_ge(pt_done, 8 * i + 2 * k + 1)
                for q in range(4):
                    mm = nc.tensor.transpose(bank[4][:, q * P:q * P + P], ao[:, k % 2, q * P:q * P + P], ident)
                mm.then_inc(pt_full, 1)

            def project_out(i):
                pe.wait_ge(pt_done, 8 * i + 8)
                pe.wait_ge(ld_c, (i // B) * 64 + 64)
                pe.wait_ge(sh_done, 4 * i + 3)
                for c in range(PAIRS):
                    mm = nc.tensor.matmul(bank[2][:, 0:S], wo[:, c, :], aoT[:, c, :], start=(c == 0), stop=(c == PAIRS - 1))
                mm.then_inc(s_full[0], 1)

            def hidden(i, c):
                if c == 0:
                    pe.wait_ge(ffn_in, i + 1)
                b = (c + 1) % 2
                pe.wait_ge(*((sh_done, 4 * i + 4), (z1_done, i + 1), (h_done, 3 * i + 1))[c])
                n = P if c < 2 else FFR
                for half in range(2):
                    mm = nc.tensor.matmul(bank[2 + b][0:n, half * S:half * S + S], w1[:, half * FF + c * P:half * FF + c * P + n],
                                          lnt[:, S:2 * S], start=True, stop=True)
                mm.then_inc(s_full[b], 1)

            def contract(i):
                pe.wait_ge(h_done, 3 * i + 3)
                for c in range(3):
                    mm = nc.tensor.matmul(bank[2][:, 0:S], w2[:, c, :], hT[:, c, :], start=(c == 0), stop=(c == 2))
                mm.then_inc(s_full[0], 1)

            def step(t, part_a, part_b):
                i = t - 1
                for s in range(8):
                    if part_a:
                        projection(t, s)
                    if part_b:
                        if s % 2 == 0:
                            scores(i, s // 2)
                        if s in (4, 6):
                            turn_out(i, s // 2 - 2)
                        if s in (2, 4, 6):
                            turn_probs(i, s // 2 - 1)
                        if s in (3, 5, 7):
                            weigh(i, (s - 3) // 2)
                if part_b:
                    turn_out(i, 2)
                    turn_probs(i, 3)
                if part_a:
                    values(t, 0)
                if part_b:
                    weigh(i, 3)
                if part_a:
                    values(t, 1)
                if part_b:
                    turn_out(i, 3)
                if part_a:
                    values(t, 2)
                if part_b:
                    project_out(i)
                if part_a:
                    values(t, 3)
                    values(t, 4)
                if part_b:
                    pe.wait_ge(xf_ready, i + 1)
                    ln_mean_pe(xf[:, :], S, LN_S2 + i)
                if part_a:
                    values(t, 5)
                if part_b:
                    ln_var_pe(S, LN_S2 + i)
                if part_a:
                    values(t, 6)
                    values(t, 7)
                if part_b:
                    hidden(i, 0)
                    hidden(i, 1)
                if part_a:
                    turn(t, 0)
                    turn(t, 1)
                if part_b:
                    hidden(i, 2)
                if part_a:
                    turn(t, 2)
                if part_b:
                    contract(i)
                if part_a:
                    for c in range(3, 8):
                        turn(t, c)

            pe.wait_ge(masks_cast, 1)
            step(0, True, False)
            with pe.Fori(1, ITEMS) as t:
                step(t, True, True)
            step(ITEMS, False, True)

            pe.wait_ge(ld_s3, 16 * 7)
            pe.wait_ge(s3["w"], 1)
            with pe.Fori(0, B) as b:
                pe.wait_ge(z_ready, b + (ITEMS + 1))
                ln_mean_pe(Z[:, b, :], S, 3 * b + LN_S3)
                ln_var_pe(S, 3 * b + LN_S3)
                pe.wait_ge(x2_ready, b + 1)
                ln_mean_pe(X[:, b, :], S, 3 * b + (LN_S3 + 1))
                ln_var_pe(S, 3 * b + (LN_S3 + 1))
                pe.wait_ge(s3["xn"], b + 1)
                for k in range(4):
                    nc.tensor.matmul(bank[k // 2][:, (k % 2) * S:(k % 2) * S + S], s3w[:, k * P:k * P + P], s3xn,
                                     start=True, stop=True)
                for i in range(2):
                    mm = nc.tensor.matmul(bank[2][:, i * P:i * P + P], s3xn[:, i * P:i * P + P], s3w[:, 4 * P:5 * P],
                                          start=True, stop=True)
                mm.then_inc(s3["qkv"], 1)
                for m in range(len(JOBS) + 2):
                    if m < len(JOBS):
                        r, heads = JOBS[m]
                        w = P * (r + 1)
                        if m == 0:
                            pe.wait_ge(s3["qk"], 2 * b + 2)
                        if m in (0, 6):
                            pe.wait_ge(s3["qm"], 2 * b + 1 + m // 6)
                        if m >= 2:
                            pe.wait_ge(s3["add"], len(JOBS) * b + m - 1)
                        for n, h in enumerate(heads):
                            mm = nc.tensor.matmul(bank[3 + m % 2][:, n * w:n * w + w], qm[:, h, r * P:r * P + P],
                                                  s3k[:, 0:w], start=True, stop=True)
                        mm.then_inc(s3["full"], 1)
                    if 1 <= m <= len(JOBS):
                        n = m - 1
                        pe.wait_ge(s3["px"], len(JOBS) * b + n + 1)
                        if n >= 1:
                            pe.wait_ge(s3["pts"], len(JOBS) * b + n)
                        for q in range(4):
                            mm = nc.tensor.transpose(lnbank[:, q * P:q * P + P], px[:, n % 2, q * P:q * P + P], ident)
                        mm.then_inc(s3["ptf"], 1)
                    if m >= 2:
                        n = m - 2
                        r, heads = JOBS[n]
                        pe.wait_ge(s3["pts"], len(JOBS) * b + n + 1)
                        if n == 0:
                            pe.wait_ge(s3["v"], b + 1)
                        for y, h in enumerate(heads):
                            g, row = h // 4, WIN * (h % 4)
                            lo = (g % 2) * S + r * P
                            for kb in range(r + 1):
                                q = y * (r + 1) + kb
                                nc.tensor.matmul(bank[g // 2][row:row + WIN, lo:lo + P], vs[:, kb, h, :],
                                                 pT[:, n % 2, q * P:q * P + P], start=(kb == 0), stop=(kb == r))
                            for kb in range(r + 1):
                                q = y * (r + 1) + kb
                                mm = nc.tensor.matmul(obank[row:row + WIN, g // 2, lo:lo + P], const("ones"),
                                                      pT[:, n % 2, q * P:q * P + P], start=(kb == 0), stop=(kb == r))
                        mm.then_inc(s3["pv"], 1)
                pe.wait_ge(s3["ot"], b + 1)
                for g in range(4):
                    mm = nc.tensor.matmul(bank[3][:, 0:S], s3wo[:, g, :], s3ot[:, g, :], start=(g == 0), stop=(g == 3))
                mm.then_inc(s3["y"], 1)
                pe.wait_ge(s3["ys"], b + 1)
                ln_mean_pe(s3y, S, 3 * b + (LN_S3 + 2))
                ln_var_pe(S, 3 * b + (LN_S3 + 2))

            pe.wait_ge(ld_gate, 64)
            pe.wait_ge(ld_s4, 16 * (NE + 1))
            pe.wait_ge(x3_ready, B)
            with pe.Fori(0, B // 2) as g:
                xg = X[:, :, :].rearrange("p (g b) t -> p g (b t)", b=2)[:, g, :]
                ln_mean_pe(xg, 512, g + LN_S4)
                ln_var_pe(512, g + LN_S4)
                pe.wait_ge(s4["xn"], g + 1)
                for i in range(4):
                    mm = nc.tensor.matmul(bank[0][:, NE * i:NE * i + NE], s4xn[:, i * P:i * P + P], gw[:, :], start=True, stop=True)
                mm.then_inc(s4["gate"], 1)
                pe.wait_ge(s4["xc"], g + 1)
                for i in range(4):
                    mm = nc.tensor.transpose(bank[1][:, i * P:i * P + P], s4x[:, i * P:i * P + P], ident)
                mm.then_inc(s4["xt"], 1)

                def up(e, c):
                    n = 4 * e + c
                    if n >= 2:
                        pe.wait_ge(s4["relu"], 4 * NE * g + n - 1)
                    nc.tensor.matmul(bank[2 + n % 2][:, :], mw1[:, e, c * P:c * P + P], s4xn, start=True,
                                     stop=True).then_inc(s4["hf"], 1)

                def down(e):
                    pe.wait_ge(s4["relu"], 4 * NE * g + 4 * e + 4)
                    if e >= 2:
                        pe.wait_ge(s4["ofr"], NE * g + e - 1)
                    ob = (bank[4][:, :], obank[:, 0, :])[e % 2]
                    for i in range(4):
                        for c in range(4):
                            mm = nc.tensor.matmul(ob[:, i * P:i * P + P], h1[:, e % 2, c, i * P:i * P + P], mw2[:, e, c, :],
                                                  start=(c == 0), stop=(c == 3))
                    mm.then_inc(s4["of"], 1)

                for e in range(NE + 1):
                    if e < NE:
                        for c in range(4):
                            up(e, c)
                    if e >= 1:
                        down(e - 1)

        @block.scalar
        def _(act):
            def ln_sq_act(w, u):
                act.wait_ge(ln_d, u + 1)
                nc.scalar.activation(lnsq[:, 0:w], lnd[:, 0:w], ACT.Square).then_inc(ln_sq, 1)

            def ln_std_act(w, u):
                act.wait_ge(ln_var, u + 1)
                nc.scalar.activation(lnsd[:, 0:w], lnbank[:, 0:w], ACT.Sqrt, bias=eps).then_inc(ln_std, 1)

            act.wait_ge(ld_const, 48)
            act.wait_ge(s1["wt"], 1)
            nc.scalar.copy(w1t, bank[1][:, :]).then_inc(s1["wts"], 1)
            act.wait_ge(ld_s1, 80)
            for j in range(B // 2):
                act.wait_ge(s1["xt"], j + 1)
                nc.scalar.copy(X[:, 2 * j:2 * j + 2, :].rearrange("p b t -> p (b t)"), bank[0][:, :]).then_inc(s1["x"], 1)
                ln_sq_act(512, LN_S1 + 3 * j)
                ln_std_act(512, LN_S1 + 3 * j)
                act.wait_ge(s1["qkv"], j + 1)
                nc.scalar.copy(s1q, bank[0][:, :])
                for i in range(2):
                    last = nc.scalar.copy(s1kv[:, 2 * i:2 * i + 2, :].rearrange("p i n -> p (i n)"), bank[1 + i][:, :])
                last.then_inc(s1["sb"], 1)
                act.wait_ge(s1["n2m"], j + 1)
                nc.scalar.activation(s1nr, s1n2, ACT.Sqrt).then_inc(s1["nr"], 1)
                act.wait_ge(s1["o"], j + 1)
                for bb in range(2):
                    last = nc.scalar.activation(s1o[:, bb * 256:bb * 256 + 256], obank[:, 0, bb * 256:bb * 256 + 256],
                                                ACT.Identity, bias=s1bv[:, bb:bb + 1], scale=nrm[:, 0:1])
                last.then_inc(s1["os"], 1)
                act.wait_ge(s1["y"], j + 1)
                nc.scalar.activation(s1y, obank[:, 1, :], ACT.Identity, bias=bout[:, :]).then_inc(s1["ys"], 1)
                for n in (1, 2):
                    ln_sq_act(512, LN_S1 + 3 * j + n)
                    ln_std_act(512, LN_S1 + 3 * j + n)

            def shifted(dst, batch, at):
                nc.scalar.copy(dst[0:64, at:at + S], Z[0:64, batch, :])
                return nc.scalar.copy(dst[64:P, at + 1:at + S], Z[64:P, batch, 0:S - 1])

            def take_xs(t):
                act.wait_ge(z_ready, t + 1)
                shifted(xs, t % B, WIN).then_inc(xs_ready, 1)

            def squares(t, c):
                act.wait_ge(p_full, 24 * t + c + 1)
                wait(act, n2_done, 8 * t + c - 1)
                nc.scalar.activation(sq[:, c % 2, :], bank[c % 2][:, :], ACT.Square).then_inc(sq_done, 1)

            def take_values(t, w):
                act.wait_ge(p_full, 24 * t + 9 + w)
                nc.scalar.copy(vp[0:64, w, :, 0:DH], bank[w % 2][0:64, :].rearrange("p (a d) -> p a d", d=DH))
                nc.scalar.copy(vp[64:P, w, :, DH + 1:2 * DH + 1],
                               bank[w % 2][64:P, :].rearrange("p (a d) -> p a d", d=DH)).then_inc(vt_free, 1)

            def take_turned(t, c):
                r, kind, half = c // 4, (c // 2) % 2, c % 2
                act.wait_ge(p_full, 24 * t + 17 + c)
                src = bank[c % 2][:, :].rearrange("p (a n) -> p a n", a=4)
                pairs = slice(4 * half, 4 * half + 4)
                if kind == 0:
                    last = nc.scalar.copy(qT[:, pairs, r * P:r * P + P], src)
                else:
                    lo = WIN + r * P
                    nc.scalar.copy(kT[0:64, pairs, 0, lo:lo + P], src[0:64])
                    last = nc.scalar.copy(kT[64:P, pairs, 1, lo:lo + P], src[64:P])
                last.then_inc(vt_free, 1)

            def exps(i, k):
                act.wait_ge(sh_done, 4 * i + k + 1)
                nc.scalar.activation(px[:, k % 2, :], sh[:, k % 2, :], ACT.Exp).then_inc(px_done, 1)

            def take_probs(i, k):
                act.wait_ge(pt_full, 8 * i + 2 * k + 1)
                nc.scalar.copy(pT[:, k % 2, :], bank[4][:, :]).then_inc(pt_done, 1)

            def take_out(i, k):
                r, g = k // 2, k % 2
                act.wait_ge(pt_full, 8 * i + 2 * k + 2)
                nc.scalar.copy(aoT[:, 4 * g:4 * g + 4, r * P:r * P + P],
                               bank[4][:, :].rearrange("p (a n) -> p a n", a=4)).then_inc(pt_done, 1)

            def gelu(i, c):
                b = (c + 1) % 2
                n = P if c < 2 else FFR
                act.wait_ge(s_full[b], 4 * i + 3 + c // 2 if b else 5 * i + 4)
                nc.scalar.activation(ge[0:n, c, :], bank[2 + b][0:n, S:2 * S], ACT.Gelu,
                                     bias=b1g[0:n, c, bass.ds(i // B, 1)]).then_inc(ge_done, 1)

            def step(t, part_a, part_b):
                i = t - 1
                for s in range(8):
                    if part_a:
                        squares(t, s)
                    if part_b:
                        if s in (1, 3, 5, 7):
                            exps(i, s // 2)
                        if s in (4, 6):
                            take_out(i, s // 2 - 2)
                        if s in (2, 4, 6):
                            take_probs(i, s // 2 - 1)
                if part_b:
                    take_out(i, 2)
                    take_probs(i, 3)
                if part_a:
                    take_values(t, 0)
                    take_values(t, 1)
                if part_b:
                    take_out(i, 3)
                if part_a:
                    take_values(t, 2)
                    take_values(t, 3)
                if part_b:
                    act.wait_ge(z1_done, i + 1)
                    shifted(xf, i % B, 0).then_inc(xf_ready, 1)
                if part_a:
                    take_values(t, 4)
                if part_b:
                    ln_sq_act(S, LN_S2 + i)
                if part_a:
                    take_values(t, 5)
                    take_values(t, 6)
                if part_b:
                    ln_std_act(S, LN_S2 + i)
                if part_a:
                    take_values(t, 7)
                    take_xs(t + 1)
                if part_b:
                    gelu(i, 0)
                    gelu(i, 1)
                if part_a:
                    take_turned(t, 0)
                    take_turned(t, 1)
                if part_b:
                    gelu(i, 2)
                if part_a:
                    for c in range(2, 8):
                        take_turned(t, c)

            act.wait_ge(cleared, 1)
            act.wait_ge(ld_vec, 16 * 11)
            take_xs(0)
            step(0, True, False)
            with act.Fori(1, ITEMS) as t:
                step(t, True, True)
            step(ITEMS, False, True)

            act.wait_ge(s3["w"], 1)
            with act.Fori(0, B) as b:
                for n in range(2):
                    ln_sq_act(S, 3 * b + (LN_S3 + n))
                    ln_std_act(S, 3 * b + (LN_S3 + n))
                act.wait_ge(s3["qkv"], b + 1)
                nc.scalar.copy(vs[:, :, :, 0:HD], bank[2][:, 0:2 * P].rearrange("p (i h d) -> p i h d", i=2, h=H))\
                    .then_inc(s3["v"], 1)
                for m in range(NJ + 1):
                    if m < NJ:
                        r, heads = JOBS[m]
                        w = P * (r + 1)
                        act.wait_ge(s3["mx"], NJ * b + m + 1)
                        if m >= 2:
                            act.wait_ge(s3["ptf"], NJ * b + m - 1)
                        for n in range(len(heads)):
                            last = nc.scalar.activation(px[:, m % 2, n * w:n * w + w], sh[:, m % 2, n * w:n * w + w], ACT.Exp,
                                                        bias=mx[:, m % 2, n:n + 1])
                        last.then_inc(s3["px"], 1)
                    if m >= 1:
                        act.wait_ge(s3["ptf"], NJ * b + m)
                        if m >= 3:
                            act.wait_ge(s3["pv"], NJ * b + m - 2)
                        nc.scalar.copy(pT[:, (m - 1) % 2, :], lnbank[:, :]).then_inc(s3["pts"], 1)
                act.wait_ge(s3["y"], b + 1)
                nc.scalar.copy(s3y, bank[3][:, 0:S]).then_inc(s3["ys"], 1)
                ln_sq_act(S, 3 * b + (LN_S3 + 2))
                ln_std_act(S, 3 * b + (LN_S3 + 2))

            act.wait_ge(ld_gate, 64)
            with act.Fori(0, B // 2) as g:
                ln_sq_act(512, g + LN_S4)
                xg = X[:, :, :].rearrange("p (g b) t -> p g (b t)", b=2)[:, g, :]
                nc.scalar.copy(s4x, xg).then_inc(s4["xc"], 1)
                ln_std_act(512, g + LN_S4)
                act.wait_ge(s4["xt"], g + 1)
                nc.scalar.copy(s4xt, bank[1][:, :]).then_inc(s4["xts"], 1)
                act.wait_ge(s4["d"], GATE_OPS * g + 3)
                nc.scalar.activation(pe_[:, :, :], lh[:, :, :], ACT.Exp).then_inc(s4["ex"], 1)
                for n in range(4 * NE):
                    act.wait_ge(s4["hf"], 4 * NE * g + n + 1)
                    nc.scalar.activation(h1[:, (n // 4) % 2, n % 4, :], bank[2 + n % 2][:, :], ACT.Relu,
                                         bias=mb1[:, n // 4, n % 4:n % 4 + 1]).then_inc(s4["relu"], 1)
                act.wait_ge(s4["d"], GATE_OPS * g + 16)
                nc.scalar.activation(ysq, yc, ACT.Square).then_inc(s4["ysq"], 1)
                act.wait_ge(s4["d"], GATE_OPS * g + 17)
                nc.scalar.activation(st[:, 3, :], st[:, 2, :], ACT.Sqrt, bias=eps, scale=1.0 / DIM).then_inc(s4["ystd"], 1)

        @block.vector
        def _(dve):
            tt, red = nc.vector.tensor_tensor, nc.vector.tensor_reduce

            def ln_d_dve(src, w, u):
                dve.wait_ge(ln_mean, u + 1)
                tt(lnd[:, 0:w], src, lnbank[:, 0:w], ALU.subtract).then_inc(ln_d, 1)

            def ln_rec_dve(w, u):
                dve.wait_ge(ln_std, u + 1)
                nc.vector.reciprocal(lnr[:, 0:w], lnsd[:, 0:w]).then_inc(ln_rec, 1)
                dve.wait_ge(ln_rec, u + 1)

            dve.wait_ge(ld_const, 48)
            nc.vector.tensor_copy(ident_bf, ident)
            nc.vector.tensor_copy(maskv, work[:, 2]).then_inc(masks_cast, 1)
            nc.vector.memset(w2[:, 2, :], 0.0)
            nc.vector.memset(hT[:, 2, :], 0.0)
            nc.vector.memset(xs[:, :], 0.0)
            nc.vector.memset(xf[:, :], 0.0)
            nc.vector.memset(kT[:, :, :, :], 0.0)
            nc.vector.memset(vp[:, :, :, :], 0.0).then_inc(cleared, 1)
            dve.wait_ge(cleared, 1)
            nc.vector.memset(vp[0:64, :, :, DH:DH + 1], 1.0)
            nc.vector.memset(vp[64:P, :, :, VB - 1:VB], 1.0)

            dve.wait_ge(ld_const, 48)
            dve.wait_ge(ld_s1, 80)
            dve.wait_ge(s3["u"], 1)
            tt(uh[:, :], bank[2][0:H, 0:384], const("neg")[0:H, :], ALU.add).then_inc(s3["ub"], 1)
            for j in range(B // 2):
                xj = X[:, 2 * j:2 * j + 2, :].rearrange("p b t -> p (b t)")
                u = LN_S1 + 3 * j
                wait(dve, z_ready, 2 * j)
                ln_d_dve(xj, 512, u)
                ln_rec_dve(512, u)
                tt(s1xn, lnd[:, :], lnr[:, :], ALU.mult).then_inc(s1["xn"], 1)
                dve.wait_ge(s1["g"], j + 1)
                tt(s1bd, bank[3][:, :].rearrange("p (c n) -> p c n", c=4), blk.unsqueeze(1).broadcast_to([P, 4, P]), ALU.mult)
                nc.vector.tensor_scalar(s1bv, bank[4][:, 0:4].rearrange("p (b o) -> p b o", o=2)[:, :, 0], nrm[:, 1:2], None,
                                        ALU.mult).then_inc(s1["bd"], 1)
                dve.wait_ge(s1["u"], j + 1)
                tt(s1pr, s1q, obank[:, 0, :], ALU.mult).then_inc(s1["pr"], 1)
                dve.wait_ge(s1["n2"], j + 1)
                nc.vector.tensor_scalar(s1n2, obank[:, 1, :], 1e-24, None, ALU.max).then_inc(s1["n2m"], 1)
                dve.wait_ge(s1["nr"], j + 1)
                nc.vector.reciprocal(s1pr, s1nr).then_inc(s1["rn"], 1)
                dve.wait_ge(s1["rn"], j + 1)
                tt(s1qg, s1q, s1pr, ALU.mult).then_inc(s1["qg"], 1)
                ln_d_dve(s1y, 512, u + 1)
                ln_rec_dve(512, u + 1)
                tt(lnt[:, :], lnd[:, :], lnr[:, :], ALU.mult).then_inc(s1["t"], 1)
                dve.wait_ge(s1["t"], j + 1)
                tt(xj, xj, lnt[:, :], ALU.add).then_inc(s1["x1"], 1)
                dve.wait_ge(s1["x1"], j + 1)
                ln_d_dve(xj, 512, u + 2)
                ln_rec_dve(512, u + 2)
                for bb in range(2):
                    tt(Z[:, 2 * j + bb, :], lnd[:, bb * S:bb * S + S], lnr[:, bb * S:bb * S + S], ALU.mult).then_inc(z_ready, 1)

            dve.wait_ge(ld_vec, 16 * 11)
            rotc = const("rot").rearrange("p (k r d) -> p k r d", k=4, r=2)
            for k in range(2):
                scale = scales[:, k, :, :]
                tt(tab[:, :, 2 * k, :, :], rotc[:, 2 * k].unsqueeze(1).broadcast_to([P, DEPTH, 2, DH]),
                   scale.unsqueeze(2).broadcast_to([P, DEPTH, 2, DH]), ALU.mult)
                for lo, other in ((0, DH // 2), (DH // 2, 0)):
                    last = tt(tab[:, :, 2 * k + 1, :, lo:lo + DH // 2],
                              rotc[:, 2 * k + 1, :, lo:lo + DH // 2].unsqueeze(1).broadcast_to([P, DEPTH, 2, DH // 2]),
                              scale[:, :, other:other + DH // 2].unsqueeze(2).broadcast_to([P, DEPTH, 2, DH // 2]), ALU.mult)
            last.then_inc(tab_done, 1)
            dve.wait_ge(tab_done, 1)

            def heads(ap):
                return ap.rearrange("p (h d) -> p h d", d=DH)

            def norms(t, c):
                dve.wait_ge(sq_done, 8 * t + c + 1)
                red(n2[:, c % 2, :], heads(sq[:, c % 2, :]), AX, ALU.add).then_inc(n2_raw, 1)
                dve.wait_ge(n2_raw, 8 * t + c + 1)
                nc.vector.tensor_scalar(n2m[:, c % 2, :], n2[:, c % 2, :], 1e-24, None, ALU.max).then_inc(n2_done, 1)

            def normalise(t, c):
                r, kind = c // 4, (c // 2) % 2
                dve.wait_ge(rn_done, 8 * t + c + 1)
                tt(heads(qn[:, c % 2, :]), heads(bank[c % 2][:, :]), rn[:, c % 2, :].unsqueeze(2).broadcast_to([P, PAIRS, DH]),
                   ALU.mult).then_inc(qn_done, 1)
                dve.wait_ge(qn_done, 8 * t + c + 1)
                cos = tab[:, bass.ds(t // B, 1), 2 * kind, r, :].broadcast_to([P, PAIRS, DH])
                tt(heads(t1[:, c % 2, :]), heads(qn[:, c % 2, :]), cos, ALU.mult).then_inc(t1_done, 1)

            def rotated(t, c):
                r, kind, half = c // 4, (c // 2) % 2, c % 2
                dve.wait_ge(t1_done, 8 * t + c + 1)
                dve.wait_ge(t2_done, 8 * t + c + 1)
                tt(rot[:, r, kind, half * 512:half * 512 + 512], t1[:, c % 2, :], t2[:, c % 2, :], ALU.add).then_inc(rot_done, 1)

            def shift_scores(i, k):
                b = k % 2
                dve.wait_ge(s_full[b], (4 if b else 5) * i + k // 2 + 1)
                red(mx[:, b, :], heads(bank[2 + b][:, :]), AX, ALU.max).then_inc(mx_done, 1)
                dve.wait_ge(mx_done, 4 * i + k + 1)
                tt(heads(sh[:, b, :]), heads(bank[2 + b][:, :]), mx[:, b, :].unsqueeze(2).broadcast_to([P, PAIRS, DH]),
                   ALU.subtract).then_inc(sh_done, 1)

            def divide_out(i, k):
                b = k % 2
                dve.wait_ge(o_full, 4 * i + k + 1)
                o = obank[:, :, 0:2 * VB].rearrange("p c (h n) -> p c h n", n=DH + 1)
                nc.vector.reciprocal(rd[:, b, :].rearrange("p (c h) -> p c h", c=2), o[:, :, :, DH]).then_inc(rd_done, 1)
                dve.wait_ge(rd_done, 4 * i + k + 1)
                tt(ao[:, b, :].rearrange("p (c h n) -> p c h n", c=2, h=4), o[:, :, :, 0:DH],
                   rd[:, b, :].rearrange("p (c h) -> p c h", c=2).unsqueeze(3).broadcast_to([P, 2, 4, DH]),
                   ALU.mult).then_inc(ao_done, 1)

            def feed_forward(i):
                l = bass.ds(i // B, 1)
                z = Z[:, i % B, :]
                dve.wait_ge(s_full[0], 5 * i + 3)
                tt(z, z, bank[2][:, 0:S], ALU.add).then_inc(z1_done, 1)
                ln_d_dve(xf[:, :], S, LN_S2 + i)
                ln_rec_dve(S, LN_S2 + i)
                tt(lnt[:, 0:S], lnd[:, 0:S], lnr[:, 0:S], ALU.mult).then_inc(xg_done, 1)
                dve.wait_ge(xg_done, i + 1)
                nc.vector.tensor_scalar(lnt[:, S:2 * S], lnt[:, 0:S], lng[:, l], lnb[:, l], ALU.mult, ALU.add).then_inc(ffn_in, 1)
                for c in range(3):
                    n = P if c < 2 else FFR
                    dve.wait_ge(ge_done, 3 * i + c + 1)
                    nc.vector.scalar_tensor_tensor(out=hT[0:n, c, :], in0=bank[2 + (c + 1) % 2][0:n, 0:S], scalar=b1a[0:n, c, l],
                                                   in1=ge[0:n, c, :], op0=ALU.add, op1=ALU.mult).then_inc(h_done, 1)
                dve.wait_ge(s_full[0], 5 * i + 5)
                nc.vector.scalar_tensor_tensor(out=z, in0=bank[2][:, 0:S], scalar=b2c[:, l], in1=z, op0=ALU.add,
                                               op1=ALU.add).then_inc(z_ready, 1)

            def step(t, part_a, part_b):
                i = t - 1
                for s in range(10):
                    if part_a:
                        if s < 8:
                            norms(t, s)
                        if 1 <= s <= 8:
                            normalise(t, s - 1)
                        if s >= 2:
                            rotated(t, s - 2)
                    if part_b:
                        if s in (0, 2, 4, 6):
                            shift_scores(i, s // 2)
                        if s in (3, 5, 7, 9):
                            divide_out(i, (s - 3) // 2)
                if part_b:
                    feed_forward(i)

            step(0, True, False)
            with dve.Fori(1, ITEMS) as t:
                step(t, True, True)
            step(ITEMS, False, True)

            dve.wait_ge(rel_in, 16)
            with dve.Fori(0, B) as b:
                x, u = X[:, b, :], 3 * b + LN_S3
                ln_d_dve(Z[:, b, :], S, u)
                ln_rec_dve(S, u)
                tt(lnt[:, 0:S], lnd[:, 0:S], lnr[:, 0:S], ALU.mult).then_inc(s3["t"], 1)
                dve.wait_ge(s3["t"], 2 * b + 1)
                tt(x, x, lnt[:, 0:S], ALU.add).then_inc(x2_ready, 1)
                dve.wait_ge(x2_ready, b + 1)
                ln_d_dve(x, S, u + 1)
                ln_rec_dve(S, u + 1)
                tt(s3xn, lnd[:, 0:S], lnr[:, 0:S], ALU.mult).then_inc(s3["xn"], 1)
                dve.wait_ge(s3["qkv"], b + 1)
                for n in range(2):
                    tt(s3part[:, n, :], bank[n][:, :], const("rope")[:, 512 * n:512 * n + 512], ALU.mult).then_inc(s3["part"], 1)
                for n, dst in enumerate((s3q, s3k)):
                    dve.wait_ge(s3["part"], 2 * b + n + 1)
                    tt(dst, s3part[:, n, 0:S], s3part[:, n, S:2 * S], ALU.add).then_inc(s3["qk"], 1)
                for m, (r, hs) in enumerate(JOBS):
                    w = P * (r + 1)
                    dve.wait_ge(s3["full"], NJ * b + m + 1)
                    if m >= 2:
                        dve.wait_ge(s3["px"], NJ * b + m - 1)
                    part = sh[:, m % 2, :].rearrange("p (h n) -> p h n", n=w)
                    tt(part, bank[3 + m % 2][:, :].rearrange("p (h n) -> p h n", n=w), bias[:, hs[0]:hs[-1] + 1, S - w:S]
                       if r == 0 else bias[:, hs[0]:hs[-1] + 1, :], ALU.add).then_inc(s3["add"], 1)
                    dve.wait_ge(s3["add"], NJ * b + m + 1)
                    red(mx[:, m % 2, 0:len(hs)], part, AX, ALU.max, negate=True).then_inc(s3["mx"], 1)
                dve.wait_ge(s3["pv"], NJ * b + NJ)
                nc.vector.reciprocal(s3den, obank[:, :, :]).then_inc(s3["den"], 1)
                dve.wait_ge(s3["den"], b + 1)
                for n in range(2):
                    last = tt(aoTf[:, 512 * n:512 * n + 512].rearrange("p (c t) -> p c t", c=4),
                              bank[n][:, :].rearrange("p (c t) -> p c t", c=4)[:, :, ::-1],
                              s3den[:, n, :].rearrange("p (c t) -> p c t", c=4)[:, :, ::-1], ALU.mult)
                last.then_inc(s3["ot"], 1)
                ln_d_dve(s3y, S, u + 2)
                ln_rec_dve(S, u + 2)
                tt(lnt[:, 0:S], lnd[:, 0:S], lnr[:, 0:S], ALU.mult).then_inc(s3["t"], 1)
                dve.wait_ge(s3["t"], 2 * b + 2)
                tt(x, x, lnt[:, 0:S], ALU.add).then_inc(x3_ready, 1)

            dve.wait_ge(ld_gate, 64)
            dve.wait_ge(x3_ready, B)
            with dve.Fori(0, B // 2) as g:
                ln_d_dve(X[:, :, :].rearrange("p (g b) t -> p g (b t)", b=2)[:, g, :], 512, g + LN_S4)
                ln_rec_dve(512, g + LN_S4)
                tt(s4xn, lnd[:, :], lnr[:, :], ALU.mult).then_inc(s4["xn"], 1)
                done = [0]

                def link(ins):
                    done[0] += 1
                    ins.then_inc(s4["d"], 1)
                    dve.wait_ge(s4["d"], GATE_OPS * g + done[0])

                def by_expert(ap):
                    return ap.unsqueeze(2).broadcast_to([P, 4, NE])

                dve.wait_ge(s4["gate"], g + 1)
                link(tt(lg[:, :, :], bank[0][:, 0:4 * NE].rearrange("p (i e) -> p i e", i=4),
                        gb[:, :].unsqueeze(1).broadcast_to([P, 4, NE]), ALU.add))
                link(red(g1[:, :], lg[:, :, :], AX, ALU.max))
                link(tt(lh[:, :, :], lg[:, :, :], by_expert(g1[:, :]), ALU.subtract))
                dve.wait_ge(s4["ex"], g + 1)
                link(red(g1[:, :], pe_[:, :, :], AX, ALU.add))
                link(nc.vector.reciprocal(g2[:, :], g1[:, :]))
                link(tt(pr_[:, :, :], pe_[:, :, :], by_expert(g2[:, :]), ALU.mult))
                other = pr_[:, :, :].unsqueeze(2).broadcast_to([P, 4, NE, NE])
                own = pr_[:, :, :].unsqueeze(3).broadcast_to([P, 4, NE, NE])

                def square(ap):
                    return ap.rearrange("p i (e o) -> p i e o", e=NE)

                link(tt(square(cmp1[:, :, :]), other, own, ALU.is_ge))
                link(tt(square(cmp2[:, :, :]), other, own, ALU.is_gt))
                link(tt(cmp3[:, :, :], cmp1[:, :, :], const("lower").unsqueeze(1).broadcast_to([P, 4, NE * NE]), ALU.mult))
                link(tt(cmp4[:, :, :], cmp2[:, :, :], const("upper").unsqueeze(1).broadcast_to([P, 4, NE * NE]), ALU.mult))
                link(tt(cmp1[:, :, :], cmp3[:, :, :], cmp4[:, :, :], ALU.add))
                link(red(rank[:, :, :], square(cmp1[:, :, :]), AX, ALU.add))
                link(nc.vector.tensor_scalar(msk[:, :, :], rank[:, :, :], 1.5, None, ALU.is_lt))

                def tokens(ap):
                    return ap.rearrange("p (i n) -> p i n", i=4)

                for e in range(NE):
                    dve.wait_ge(s4["of"], NE * g + e + 1)
                    ob = (bank[4][:, :], obank[:, 0, :])[e % 2]
                    tt(tokens(ob2[:, e % 2, :]), tokens(ob), mb2[:, e, :].unsqueeze(1).broadcast_to([P, 4, DIM]), ALU.add)\
                        .then_inc(s4["ofr"], 1)
                    dve.wait_ge(s4["ofr"], NE * g + e + 1)
                    if e >= 2:
                        dve.wait_ge(s4["acc"], (NE - 1) * g + max(e - 2, 1))
                    tt(tokens(oms[:, e % 2, :]), tokens(ob2[:, e % 2, :]), msk[:, :, e:e + 1].broadcast_to([P, 4, DIM]), ALU.mult)\
                        .then_inc(s4["om"], 1)
                dve.wait_ge(s4["acc"], (NE - 1) * g + NE - 1)
                link(red(st[:, 0, :], tokens(acc[:, :]), AX, ALU.add))
                link(nc.vector.tensor_scalar(st[:, 1, :], st[:, 0, :], 1.0 / DIM, None, ALU.mult))
                link(tt(tokens(yc), tokens(acc[:, :]), st[:, 1, :].unsqueeze(2).broadcast_to([P, 4, DIM]), ALU.subtract))
                dve.wait_ge(s4["ysq"], g + 1)
                link(red(st[:, 2, :], tokens(ysq), AX, ALU.add))
                dve.wait_ge(s4["ystd"], g + 1)
                link(nc.vector.reciprocal(st[:, 0, :], st[:, 3, :]))
                link(tt(tokens(yn), tokens(yc), st[:, 0, :].unsqueeze(2).broadcast_to([P, 4, DIM]), ALU.mult))
                assert done[0] == GATE_OPS
                dve.wait_ge(s4["xts"], g + 1)
                dve.wait_ge(stored, g * 16 + 16)
                tt(outs, yn, s4xt, ALU.add).then_inc(s4["out"], 1)

        @block.gpsimd
        def _(pool):
            tt = nc.gpsimd.tensor_tensor
            pool.wait_ge(ld_const, 48)
            pool.wait_ge(tab_done, 1)

            def inverse_norms(t, c):
                pool.wait_ge(n2_done, 8 * t + c + 1)
                tt(rn[:, c % 2, :], n2m[:, c % 2, :], const("mhalf"), ALU.pow).then_inc(rn_done, 1)

            def sines(t, c):
                r, kind = c // 4, (c // 2) % 2
                pool.wait_ge(qn_done, 8 * t + c + 1)
                tt(touch[:, c:c + 1], const("mhalf")[:, 0:1], const("mhalf")[:, 0:1], ALU.mult)
                swapped = qn[:, c % 2, :].rearrange("p (h o d) -> p h o d", o=2, d=DH // 2)[:, :, ::-1, :]
                sin = tab[:, bass.ds(t // B, 1), 2 * kind + 1, r, :].rearrange("p l (o d) -> p l o d", o=2)\
                    .broadcast_to([P, PAIRS, 2, DH // 2])
                tt(t2[:, c % 2, :].rearrange("p (h o d) -> p h o d", o=2, d=DH // 2), swapped, sin, ALU.mult).then_inc(t2_done, 1)

            def step(t):
                for c in range(9):
                    if c < 8:
                        inverse_norms(t, c)
                    if c >= 1:
                        sines(t, c - 1)

            step(0)
            with pool.Fori(1, ITEMS) as t:
                step(t)

            pool.wait_ge(p_full, 24 * ITEMS)
            nc.gpsimd.memset(wv[:, 0:4 * P], 0.0).then_inc(cleared, 1)
            pool.wait_ge(o_full, 4 * ITEMS)
            nc.gpsimd.memset(qTf[:, 0:2 * H * WIN], 0.0)
            pool.wait_ge(ld_s3, 16 * 7)
            for k in (0, 2):
                src = s3w[:, k * P:k * P + P].rearrange("p (h o d) -> p h o d", o=2, d=HD // 2)
                dst = s3w[:, k * P + P:k * P + 2 * P].rearrange("p (h o d) -> p h o d", o=2, d=HD // 2)
                nc.gpsimd.tensor_scalar(dst[:, :, 0, :], src[:, :, 1, :], -1.0, None, ALU.mult)
                last = nc.gpsimd.tensor_copy(dst[:, :, 1, :], src[:, :, 0, :])
            last.then_inc(s3["w"], 1)
            with pool.Fori(0, B) as b:
                pool.wait_ge(s3["qk"], 2 * b + 1)
                for n in range(2):
                    hs = slice(8 * n, 8 * n + 8)
                    for r in range(2):
                        back = s3q.rearrange("p (r t) -> p r t", r=2)[:, r, ::-1]
                        last = tt(qm[:, hs, r * P:r * P + P], back.unsqueeze(1).broadcast_to([P, 8, P]),
                                  const("headm")[:, hs].unsqueeze(2).broadcast_to([P, 8, P]), ALU.mult)
                    last.then_inc(s3["qm"], 1)
            with pool.Fori(0, B // 2) as g:
                pool.wait_ge(s4["om"], NE * g + 2)
                tt(acc[:, :], oms[:, 0, :], oms[:, 1, :], ALU.add).then_inc(s4["acc"], 1)
                for e in range(2, NE):
                    pool.wait_ge(s4["om"], NE * g + e + 1)
                    pool.wait_ge(s4["acc"], (NE - 1) * g + e - 1)
                    tt(acc[:, :], acc[:, :], oms[:, e % 2, :], ALU.add).then_inc(s4["acc"], 1)


def constants():
    import math

    import numpy as np

    f = np.float32
    c = {}
    c["ident"] = np.eye(P, dtype=f)
    c["onesm"] = np.full((P, P), 1.0 / DIM, f)
    head = np.arange(P) // HD
    c["blk"] = (head[:, None] == head[None, :]).astype(f)
    c["headm"] = (head[:, None] == np.arange(H)[None, :]).astype(f)
    half = np.arange(0, DH, 2, dtype=f)
    inv_freq = (f(1.0) / f(10000.0) ** (half / f(DH))).astype(f)
    t = np.arange(S, dtype=f)
    freqs = t[:, None] * inv_freq[None, :]
    freqs = np.concatenate([freqs, freqs], -1)
    base = (half + f(0.4 * DH)) / f(1.4 * DH)
    power = (t - f(S // 2)) / f(WIN // 2)
    scale = base[None, :] ** power[:, None]
    scale = np.concatenate([scale, scale], -1).astype(f)
    sign = np.where(np.arange(DH) < DH // 2, -1.0, 1.0).astype(f)
    cos, sin = np.cos(freqs), np.sin(freqs)
    inv = f(1.0) / scale
    rot = np.stack([cos * scale * f(8), sin * scale * sign * f(8), cos * inv, sin * inv * sign])
    c["rot"] = rot.reshape(4, 2, P, DH).transpose(2, 0, 1, 3).reshape(P, -1)
    inv_freq = (f(1.0) / f(10000.0) ** (np.arange(0, HD, 2, dtype=f) / f(HD))).astype(f)
    emb = t[:, None] * inv_freq[None, :]
    emb = np.tile(np.concatenate([emb, emb], -1), (1, H)).T
    cos, sin, down = np.cos(emb), np.sin(emb), f(1.0 / math.sqrt(HD))
    c["rope"] = np.concatenate([cos * down, sin * down, cos, sin], 1)
    dist = (S - 1) - np.arange(384)
    rp = np.maximum(dist, 0)
    large = 16 + (np.log(np.maximum(rp, 1).astype(f) / f(16)) / f(math.log(8.0)) * f(16)).astype(np.int32)
    bucket = np.where(rp < 16, rp, np.minimum(large, 31))
    c["onehot"] = np.zeros((P, 384), f)
    c["onehot"][bucket, np.arange(384)] = 1.0
    c["onehot"][:, dist < 0] = 0.0
    c["neg"] = np.tile(np.where(dist < 0, -1e9, 0.0).astype(f), (P, 1))
    e = np.arange(NE)
    c["lower"] = np.tile((e[None, :] < e[:, None]).astype(f).reshape(1, -1), (P, 1))
    c["upper"] = np.tile((e[None, :] > e[:, None]).astype(f).reshape(1, -1), (P, 1))
    c["eps"] = np.full((P, 1), 1e-5, f)
    c["ones"] = np.ones((P, WIN), f)
    c["mhalf"] = np.full((P, PAIRS), -0.5, f)
    packed = np.concatenate([c[n].astype(f) for n, _ in WIDTHS], 1)
    q, key = np.arange(WIN)[:, None], np.arange(2 * WIN)[None, :] - WIN
    hidden = np.where((key > q) | (key < q - WIN), -1e30, 0.0)
    tile = np.tile(hidden, (4, PAIRS))
    first = tile.copy()
    first[0:WIN] = np.tile(np.where(key < 0, -1e30, hidden), (1, PAIRS))
    return packed, np.concatenate([first, tile], 1).astype(f)


_INS = ["L0_attn_x", "L0_attn_w_qkv", "L0_attn_w_out", "L0_attn_b_out", "L0_attn_norm_g", "L0_attn_norm_b",
        "L0_ffn_Wqkv", "L0_ffn_q_scale", "L0_ffn_k_scale", "L0_ffn_Wo", "L0_ffn_ln_g", "L0_ffn_ln_b", "L0_ffn_W1",
        "L0_ffn_b1", "L0_ffn_W2", "L0_ffn_b2", "L1_attn_Wq", "L1_attn_Wk", "L1_attn_Wv", "L1_attn_Wo",
        "L1_attn_rel_emb", "L1_ffn_gate_w", "L1_ffn_gate_b", "L1_ffn_w1", "L1_ffn_b1", "L1_ffn_w2", "L1_ffn_b2"]


def kernel(**inputs):
    import numpy as _np
    import concourse.bacc as _bacc
    from concourse import mybir as _mybir
    from concourse.bass_utils import run_bass_kernel_spmd as _run

    nc = _bacc.Bacc("TRN2", target_bir_lowering=False, num_devices=1)
    arrays, args = {}, {}
    packed, masks = constants()
    for name, arr in [(n, inputs[n]) for n in _INS] + [("consts", packed), ("window_masks", masks)]:
        arr = _np.ascontiguousarray(arr)
        arrays[f"in_{name}"] = arr
        args[name] = nc.dram_tensor(f"in_{name}", arr.shape, _mybir.dt.from_np(arr.dtype), kind="ExternalInput").ap()
    out = nc.dram_tensor("out_0", (B, S, DIM), _mybir.dt.float32, kind="ExternalOutput").ap()
    build(nc, args, out)
    r = _run(nc, [arrays], core_ids=[0])
    return r.results[0]["out_0"]
```

```python
from contextlib import ExitStack

import concourse.bass as bass
from concourse import mybir
from concourse.alu_op_type import AluOpType as ALU

ACT = mybir.ActivationFunctionType
F32 = mybir.dt.float32
BF16 = mybir.dt.bfloat16
AX = mybir.AxisListType.X

P = 128
B, S, DIM, H = 8, 256, 128, 16
TOK = B * S
DEPTH = 6
ITEMS = DEPTH * B
DH = 64
PAIRS = H // 2
WIN = 32
NW = S // WIN
FF = int(DIM * 4 * 2 / 3)
FFR = FF - 2 * P
HD = DIM // H
NE, EF = 8, 512
VB = 2 * (DH + 1)
KW = WIN + S

WIDTHS = [("ident", P), ("onesm", P), ("blk", P), ("rot", 4 * 2 * DH), ("headm", H),
          ("rope", 4 * S), ("onehot", 384), ("neg", 384), ("lower", NE * NE), ("upper", NE * NE),
          ("eps", 1), ("ones", WIN), ("mhalf", PAIRS)]
COL = {}
NCONST = 0
for _name, _width in WIDTHS:
    COL[_name] = (NCONST, NCONST + _width)
    NCONST += _width

LN_S1 = 0
LN_S2 = LN_S1 + 3 * (B // 2)
LN_S3 = LN_S2 + ITEMS
LN_S4 = LN_S3 + 3 * B


JOBS = [job for n in range(0, H, 4)
        for job in ((0, range(n, n + 4)), (1, range(n, n + 2)), (1, range(n + 2, n + 4)))]
NJ = len(JOBS)
SC_BANK = (3, 2, 2, 3)
PT_PROBS = (0, 1, 4, 5)
PT_OUT = (2, 3, 6, 7)
GATE_OPS = 19


def wait(eng, s, value):
    if not isinstance(value, int) or value > 0:
        eng.wait_ge(s, value)


def build(nc, a, out):
    ctx = ExitStack()
    with ctx:
        def sb(name, shape, dt=F32):
            return ctx.enter_context(nc.sbuf_tensor(name, shape, dt))

        def sem(name):
            return ctx.enter_context(nc.semaphore(name))

        bank = [ctx.enter_context(nc.psum_tensor(f"bank{i}", [P, 512], F32)) for i in range(5)]
        obank = ctx.enter_context(nc.psum_tensor("obank", [P, 2, 512], F32))
        lnbank = ctx.enter_context(nc.psum_tensor("lnbank", [P, 512], F32))

        cst = sb("cst", [P, NCONST])
        cbf = sb("cbf", [P, P + 2 * 512], BF16)

        def const(name):
            return cst[:, COL[name][0]:COL[name][1]]

        ident, onesm, blk = const("ident"), const("onesm"), const("blk")
        eps = const("eps")
        ident_bf = cbf[:, 0:P]
        maskv = cbf[:, P:].rearrange("p (r n) -> p r n", r=2)
        X = sb("X", [P, B, S])
        Z = sb("Z", [P, B, S])
        work = sb("work", [P, 4, 2, 512])
        xin = work[:, 0:2].rearrange("p k a (i m) -> p (k a i) m", m=DIM)
        lnd = sb("lnd", [P, 512])
        lnsq = sb("lnsq", [P, 512])
        lnt = sb("lnt", [P, 512])
        lnv = sb("lnv", [P, 4])
        lnr = sb("lnr", [P, 4])

        wqk = sb("wqk", [P, 2 * H * DH])
        wv = sb("wv", [P, H * DH])
        wo = sb("wo", [P, PAIRS, DIM])
        w1 = sb("w1", [P, 2 * FF])
        w2 = sb("w2", [P, 3, DIM])
        lng = sb("lng", [P, DEPTH])
        lnb = sb("lnb", [P, DEPTH])
        b2c = sb("b2c", [P, DEPTH])
        b1a = sb("b1a", [P, 3, DEPTH])
        b1g = sb("b1g", [P, 3, DEPTH])
        scales = sb("scales", [P, 2, DEPTH, DH])
        tab = sb("tab", [P, DEPTH, 4, 2, DH])
        touch = sb("touch", [P, 8])
        xs = sb("xs", [P, 2, KW])
        xf = sb("xf", [P, S])
        sq = work[:, 0]
        n2 = sb("n2", [P, 2, PAIRS])
        n2m = sb("n2m", [P, 2, PAIRS])
        rn = sb("rn", [P, 2, PAIRS])
        qn = work[:, 1]
        t1 = work[:, 2]
        t2 = work[:, 3]
        rot = sb("rot", [P, 8, 512])
        qT = sb("qT", [P, PAIRS, S])
        kT = sb("kT", [P, PAIRS, 2, KW])
        vp = sb("vp", [P, NW, PAIRS, VB])
        mx = sb("mx", [P, 2, PAIRS])
        sh = sb("sh", [P, 2, 512])
        px = sb("px", [P, 2, 512])
        pT = sb("pT", [P, 2, 512])
        rd = sb("rd", [P, 2, PAIRS])
        ao = sb("ao", [P, 2, 512])
        aoT = sb("aoT", [P, PAIRS, S])
        ge = sb("ge", [P, 3, S])
        hT = sb("hT", [P, 3, S])

        vflat = vp[:, :, :, :].rearrange("p w q n -> p (w q n)")
        qTf = qT[:, :, :].rearrange("p a t -> p (a t)")
        aoTf = aoT[:, :, :].rearrange("p a t -> p (a t)")
        kTf = kT[:, :, :, :].rearrange("p a b t -> p (a b t)")
        rotf = rot[:, :, :].rearrange("p c n -> p (c n)")
        w1raw = rotf[:, 0:512].rearrange("p (c m) -> p c m", c=4)
        w1t = rotf[:, 512:1024]
        s1xn, s1q, s1pr, s1n2 = (qTf[:, 512 * i:512 * i + 512] for i in range(4))
        s1nr, s1qg, s1o, s1y = (aoTf[:, 512 * i:512 * i + 512] for i in range(4))
        s1kv = rotf[:, 1024:2048].rearrange("p (i n) -> p i n", i=4)
        s1bd = rotf[:, 2048:2560].rearrange("p (c n) -> p c n", c=4)
        s1bv = rotf[:, 2560:2562]
        nrm = sb("nrm", [P, 2])
        bout = sb("bout", [P, 1])
        bias = kTf[:, 0:H * S].rearrange("p (h t) -> p h t", h=H)
        relv = sb("relv", [WIN, H])
        uh = sb("uh", [H, 384])
        relu_dram = nc.dram_tensor("rel_by_distance", [H, 384], F32)
        s3w = wqk[:, 0:5 * P]
        s3wo = wv[:, 0:4 * P].rearrange("p (g n) -> p g n", g=4)
        s3xn = t1[:, 0, 0:S]
        s3part = qn
        s3den = sq
        s3q, s3k = t1[:, 1, 0:S], t1[:, 1, S:2 * S]
        qm = rotf.rearrange("p (h t) -> p h t", h=H)
        vs = qTf[:, 0:2 * H * WIN].rearrange("p (i h n) -> p i h n", i=2, h=H)
        s3s = sh
        s3nm = mx[:, :, 0:4]
        s3ot = aoTf[:, 0:4 * S].rearrange("p (g t) -> p g t", g=4)
        s3y = aoTf[:, 4 * S:5 * S]
        mw1 = vflat[:, 0:NE * EF].rearrange("p (e f) -> p e f", e=NE)
        mw2 = vflat[:, NE * EF:2 * NE * EF].rearrange("p (e c n) -> p e c n", e=NE, c=4)
        gw = sb("gw", [P, NE])
        gb = sb("gb", [P, NE])
        mb1 = sb("mb1", [P, NE, 4])
        mb2 = sb("mb2", [P, NE, DIM])
        s4xn = t1[:, 0, :]
        s4x = ao[:, 0, :]
        s4xt = t1[:, 1, :]
        h1 = rotf.rearrange("p (s f n) -> p s f n", s=2, f=4)
        lg, lh, pe_, pr_ = (sb(f"gate{i}", [P, 4, NE]) for i in range(4))
        g1 = sb("g1", [P, 4])
        g2 = sb("g2", [P, 4])
        cmp1, cmp2, cmp3 = (ge[:, i, :].rearrange("p (i n) -> p i n", i=4) for i in range(3))
        cmp4 = hT[:, 0, :].rearrange("p (i n) -> p i n", i=4)
        rank = sb("rank", [P, 4, NE])
        msk = sb("msk", [P, 4, NE])
        ob2 = qn
        oms = t2
        acc = ao[:, 1, :]
        st = sb("st", [P, 4, 4])
        yc = sh[:, 0, :]
        ysq = sh[:, 1, :]
        yn = px[:, 0, :]
        outs = px[:, 1, :]

        ld_const, ld_x, ld_s1, ld_vec = sem("ld_const"), sem("ld_x"), sem("ld_s1"), sem("ld_vec")
        ld_qk, ld_v = sem("ld_qk"), sem("ld_v")
        ld_o, ld_w1, ld_w2 = sem("ld_o"), sem("ld_w1"), sem("ld_w2")
        ld_s3, ld_s4, ld_gate = sem("ld_s3"), sem("ld_s4"), sem("ld_gate")
        rel_in = sem("rel_in")
        stored = sem("stored")
        cleared, tab_done, masks_cast = sem("cleared"), sem("tab_done"), sem("masks_cast")
        ln_mean, ln_d, ln_sq, ln_var, ln_eps, ln_rstd, ln_wide, ln_done = (
            sem("ln_" + n) for n in ("mean", "d", "sq", "var", "eps", "rstd", "wide", "done"))
        s1 = {n: sem("s1_" + n) for n in ("wt", "wts", "xt", "x", "qkv", "sb", "g", "bd", "u", "pr", "n2",
                                          "n2m", "nr", "rn", "qg", "o", "os", "y", "ys", "x1")}
        z_ready = sem("z_ready")
        xs_ready = sem("xs_ready")
        p_full, v_full, t_full = sem("p_full"), sem("v_full"), sem("t_full")
        raw_done, v_done, t_done = sem("raw_done"), sem("v_done"), sem("t_done")
        sq_done, n2_done, n2_raw, rn_done = sem("sq_done"), sem("n2_done"), sem("n2_raw"), sem("rn_done")
        qn_done, t1_done, t2_done, rot_done = sem("qn_done"), sem("t1_done"), sem("t2_done"), sem("rot_done")
        sc_full, po_full, hd_full, ct_full = sem("sc_full"), sem("po_full"), sem("hd_full"), sem("ct_full")
        mx_done, sh_done, px_done = sem("mx_done"), sem("sh_done"), sem("px_done")
        pt_full, pt_done = sem("pt_full"), sem("pt_done")
        o_full, rd_done, ao_done = sem("o_full"), sem("rd_done"), sem("ao_done")
        z1_done, xf_ready, ffn_in = sem("z1_done"), sem("xf_ready"), sem("ffn_in")
        ge_done, h_done = sem("ge_done"), sem("h_done")
        s3 = {n: sem("s3_" + n) for n in ("w", "qkv", "part", "qk", "qm", "v", "full", "add", "mx", "px",
                                          "ptf", "pts", "pv", "den", "ot", "y", "ys", "u", "ub")}
        x2_ready, x3_ready = sem("x2_ready"), sem("x3_ready")
        s4 = {n: sem("s4_" + n) for n in ("gate", "xc", "xt", "xts", "d", "ex", "hf", "relu", "of", "ofr", "om", "acc",
                                          "ysq", "ystd", "out")}

        block = ctx.enter_context(nc.Block())

        @block.sync
        def _(sp):
            sp.dma_start(cst[:, :], a["consts"]).then_inc(ld_const, 16)
            sp.dma_start(xin[:, :, :], a["L0_attn_x"].rearrange("b (i p) m -> p (b i) m", p=P)).then_inc(ld_x, 16)
            sp.dma_start(w1raw[:, 0:3, :], a["L0_attn_w_qkv"].rearrange("(c p) m -> p c m", p=P)).then_inc(ld_s1, 16)
            sp.dma_start(w1raw[:, 3, :], a["L0_attn_w_out"]).then_inc(ld_s1, 16)
            sp.dma_start(bout[:, :], a["L0_attn_b_out"].rearrange("(p o) -> p o", o=1)).then_inc(ld_s1, 16)
            for col, name in enumerate(("L0_attn_norm_g", "L0_attn_norm_b")):
                per_head = a[name].rearrange("o h c d -> h (o c d)")
                sp.dma_start(nrm[:, col:col + 1], bass.AP(per_head.tensor, 0, [[1, H], [0, HD], [1, 1]])).then_inc(ld_s1, 16)
            sp.dma_start(work[:, 2], a["window_masks"].rearrange("p (r n) -> p r n", r=2)).then_inc(ld_const, 16)
            sp.dma_start(relv[:, :], a["L1_attn_rel_emb"]).then_inc(ld_const, 16)
            for k, name in enumerate(("L0_ffn_q_scale", "L0_ffn_k_scale")):
                sp.dma_start(scales[:, k, :, :].rearrange("p l d -> p (l d)"),
                             a[name].rearrange("l d -> (l d)").partition_broadcast(P)).then_inc(ld_vec, 16)

            def load_qk(l):
                sp.dma_start(wqk[:, :], a["L0_ffn_Wqkv"][l, :, 0:2 * H * DH]).then_inc(ld_qk, 16)

            def load_v(l):
                sp.dma_start(wv[:, :], a["L0_ffn_Wqkv"][l, :, 2 * H * DH:3 * H * DH]).then_inc(ld_v, 16)

            def load_o(l):
                sp.dma_start(wo[:, :, :], a["L0_ffn_Wo"][l].rearrange("(c p) n -> p c n", p=P)).then_inc(ld_o, 16)

            def load_w1(l):
                sp.dma_start(w1[:, :], a["L0_ffn_W1"][l]).then_inc(ld_w1, 16)

            def load_w2(l):
                sp.dma_start(w2[:, 0:2, :], a["L0_ffn_W2"][l, 0:2 * P, :].rearrange("(c p) n -> p c n", p=P)).then_inc(ld_w2, 16)
                sp.dma_start(w2[0:FFR, 2, :], a["L0_ffn_W2"][l, 2 * P:FF, :]).then_inc(ld_w2, 16)

            load_qk(0)
            load_v(0)
            sp.wait_ge(cleared, 1)
            load_o(0)
            load_w1(0)
            load_w2(0)
            for t, name in ((lng, "L0_ffn_ln_g"), (lnb, "L0_ffn_ln_b"), (b2c, "L0_ffn_b2")):
                sp.dma_start(t[:, :], a[name].rearrange("l p -> p l"), allow_slow_non_contiguous=True).then_inc(ld_vec, 16)
            for half, t in ((0, b1a), (1, b1g)):
                for c in range(3):
                    n = P if c < 2 else FFR
                    lo = half * FF + c * P
                    sp.dma_start(t[0:n, c, :], a["L0_ffn_b1"][:, lo:lo + n].rearrange("l p -> p l"), allow_slow_non_contiguous=True).then_inc(ld_vec, 16)
            sp.wait_ge(s3["ub"], 1)
            sp.dma_start(relu_dram.ap(), uh[:, :]).then_inc(stored, 16)
            sp.wait_ge(stored, 16)
            sp.dma_start(gw[:, :], a["L1_ffn_gate_w"]).then_inc(ld_gate, 16)
            sp.dma_start(gb[:, :], a["L1_ffn_gate_b"].partition_broadcast(P)).then_inc(ld_gate, 16)
            sp.dma_start(mb1[:, :, :], a["L1_ffn_b1"].rearrange("e (c p) -> p e c", p=P), allow_slow_non_contiguous=True).then_inc(ld_gate, 16)
            sp.dma_start(mb2[:, :, :].rearrange("p e n -> p (e n)"),
                         a["L1_ffn_b2"].rearrange("e n -> (e n)").partition_broadcast(P)).then_inc(ld_gate, 16)
            with sp.Fori(1, DEPTH) as l:
                sp.wait_ge(p_full, l * (8 * B))
                load_qk(l)
                sp.wait_ge(v_full, l * (8 * B))
                load_v(l)
                sp.wait_ge(po_full, l * B)
                load_o(l)
                sp.wait_ge(hd_full, l * (3 * B))
                load_w1(l)
                sp.wait_ge(ct_full, l * B)
                load_w2(l)
            sp.wait_ge(p_full, 8 * ITEMS)
            for k, name in ((0, "L1_attn_Wq"), (2, "L1_attn_Wk"), (4, "L1_attn_Wv")):
                sp.dma_start(s3w[:, k * P:k * P + P], a[name]).then_inc(ld_s3, 16)
            sp.wait_ge(cleared, 2)
            src = a["L1_attn_Wo"].rearrange("(g j d) n -> j d g n", g=4, j=4)
            for j in range(4):
                sp.dma_start(s3wo[WIN * j:WIN * j + HD, :, :], src[j]).then_inc(ld_s3, 16)
            sp.wait_ge(o_full, 4 * ITEMS)
            sp.dma_start(bias, bass.AP(relu_dram.ap().tensor, 0, [[1, P], [384, H], [1, S]])).then_inc(rel_in, 16)
            sp.dma_start(mw1, a["L1_ffn_w1"].rearrange("e m f -> m e f")).then_inc(ld_s4, 16)
            for e in range(NE):
                sp.dma_start(mw2[:, e], a["L1_ffn_w2"][e].rearrange("(c p) n -> p c n", p=P)).then_inc(ld_s4, 16)
            outv = out.rearrange("(g b) (i p) m -> g p (b i) m", b=2, p=P)
            with sp.Fori(0, B // 2) as g:
                sp.wait_ge(s4["out"], g + 1)
                sp.dma_start(outv[g], outs.rearrange("p (i m) -> p i m", i=4)).then_inc(stored, 16)
            sp.wait_ge(stored, 16 + 16 * (B // 2))

        @block.tensor
        def _(pe):
            def ln_mean_pe(src, w, u):
                wait(pe, ln_done, u)
                nc.tensor.matmul(lnbank[:, 0:w], onesm, src, start=True, stop=True).then_inc(ln_mean, 1)

            def ln_var_pe(w, u):
                pe.wait_ge(ln_sq, u + 1)
                for i in range(w // P):
                    mm = nc.tensor.matmul(lnbank[:, 2 * i:2 * i + 2], lnsq[:, i * P:i * P + P], onesm[:, 0:2], start=True, stop=True)
                mm.then_inc(ln_var, 1)

            def ln_wide_pe(w, u):
                pe.wait_ge(ln_rstd, u + 1)
                for i in range(w // P):
                    mm = nc.tensor.matmul(lnbank[:, i * P:i * P + P], lnr[:, i:i + 1].broadcast_to([P, P]), ident,
                                          start=True, stop=True)
                mm.then_inc(ln_wide, 1)

            pe.wait_ge(ld_const, 48)
            pe.wait_ge(ld_s1, 80)
            for c in range(4):
                mm = nc.tensor.transpose(bank[1][:, c * P:c * P + P], w1raw[:, c, :], ident)
            mm.then_inc(s1["wt"], 1)
            nc.tensor.matmul(bank[2][0:H, 0:384], relv[:, :], const("onehot")[0:WIN, :], start=True, stop=True).then_inc(s3["u"], 1)
            pe.wait_ge(ld_x, 16)
            pe.wait_ge(s1["wts"], 1)
            pe.wait_ge(s3["ub"], 1)
            for j in range(B // 2):
                wait(pe, s1["x"], j)
                for i in range(4):
                    mm = nc.tensor.transpose(bank[0][:, i * P:i * P + P], xin[:, 4 * j + i, :], ident)
                mm.then_inc(s1["xt"], 1)
                pe.wait_ge(s1["x"], j + 1)
                xj = X[:, 2 * j:2 * j + 2, :].rearrange("p b t -> p (b t)")
                ln_mean_pe(xj, 512, LN_S1 + 3 * j)
                ln_var_pe(512, LN_S1 + 3 * j)
                ln_wide_pe(512, LN_S1 + 3 * j)
                pe.wait_ge(ln_done, LN_S1 + 3 * j + 1)
                nc.tensor.matmul(bank[0][:, :], w1t[:, 0:P], s1xn, start=True, stop=True)
                for i in range(4):
                    mm = nc.tensor.matmul(bank[1 + i // 2][:, (i % 2) * 256:(i % 2) * 256 + 256], s1xn[:, i * P:i * P + P],
                                          w1t[:, P:3 * P], start=True, stop=True)
                mm.then_inc(s1["qkv"], 1)
                pe.wait_ge(s1["sb"], j + 1)
                for bb in range(2):
                    for i in range(2):
                        nc.tensor.matmul(bank[3][:, bb * 256:bb * 256 + 256], s1kv[:, 2 * bb + i, 0:P], s1kv[:, 2 * bb + i, :],
                                         start=(i == 0), stop=(i == 1))
                for bb in range(2):
                    for i in range(2):
                        mm = nc.tensor.matmul(bank[4][:, 2 * bb:2 * bb + 2], s1kv[:, 2 * bb + i, P:2 * P], const("ones")[:, 0:2],
                                              start=(i == 0), stop=(i == 1))
                mm.then_inc(s1["g"], 1)
                pe.wait_ge(s1["bd"], j + 1)
                for bb in range(2):
                    mm = nc.tensor.matmul(obank[:, 0, bb * 256:bb * 256 + 256], s1bd[:, 2 * bb, :], s1q[:, bb * 256:bb * 256 + 256],
                                          start=True, stop=True)
                mm.then_inc(s1["u"], 1)
                pe.wait_ge(s1["pr"], j + 1)
                nc.tensor.matmul(obank[:, 1, :], blk, s1pr, start=True, stop=True).then_inc(s1["n2"], 1)
                pe.wait_ge(s1["qg"], j + 1)
                for bb in range(2):
                    mm = nc.tensor.matmul(obank[:, 0, bb * 256:bb * 256 + 256], s1bd[:, 2 * bb + 1, :],
                                          s1qg[:, bb * 256:bb * 256 + 256], start=True, stop=True)
                mm.then_inc(s1["o"], 1)
                pe.wait_ge(s1["os"], j + 1)
                nc.tensor.matmul(obank[:, 1, :], w1t[:, 3 * P:4 * P], s1o, start=True, stop=True).then_inc(s1["y"], 1)
                pe.wait_ge(s1["ys"], j + 1)
                ln_mean_pe(s1y, 512, LN_S1 + 3 * j + 1)
                ln_var_pe(512, LN_S1 + 3 * j + 1)
                ln_wide_pe(512, LN_S1 + 3 * j + 1)
                pe.wait_ge(s1["x1"], j + 1)
                ln_mean_pe(xj, 512, LN_S1 + 3 * j + 2)
                ln_var_pe(512, LN_S1 + 3 * j + 2)
                ln_wide_pe(512, LN_S1 + 3 * j + 2)

            def projection(t, s, odd):
                r, kind, half = s // 4, (s // 2) % 2, s % 2
                if s == 0:
                    pe.wait_ge(xs_ready, t + 1)
                    pe.wait_ge(ld_qk, (t // B) * 16 + 16)
                wait(pe, t_done, 8 * t + s - 2)
                if isinstance(t, int) and (t, s) == (0, 2):
                    pe.wait_ge(raw_done, 1)
                lo = kind * H * DH + half * 512
                nc.tensor.matmul(bank[s % 2][:, :], xs[:, odd, WIN + r * P:WIN + r * P + P], wqk[:, lo:lo + 512],
                                 start=True, stop=True).then_inc(p_full, 1)

            def turn(i, c, s):
                pe.wait_ge(rot_done, 8 * i + c + 1)
                wait(pe, v_done, 8 * i + c)
                if isinstance(i, int) and (i, c) == (0, 0):
                    pe.wait_ge(raw_done, 2)
                for q in range(4):
                    mm = nc.tensor.transpose(bank[(s + 1) % 2][:, q * P:q * P + P], rot[:, c, q * P:q * P + P], ident)
                mm.then_inc(t_full, 1)

            def values(i, w, s, odd, after_projection):
                if w == 0:
                    pe.wait_ge(ld_v, (i // B) * 16 + 16)
                if after_projection:
                    pe.wait_ge(raw_done, 8 * i + w + 3)
                else:
                    pe.wait_ge(t_done, 8 * i + w)
                for o in range(2):
                    mm = nc.tensor.matmul(bank[s % 2][64 * o:64 * o + 64, :], xs[:, odd, w * WIN:w * WIN + 2 * WIN],
                                          wv[:, :].rearrange("p (a o d) -> p o a d", o=2, d=DH)[:, o],
                                          start=True, stop=True)
                mm.then_inc(v_full, 1)

            def scores(i, k, *free):
                r, g = k // 2, k % 2
                if g == 0:
                    pe.wait_ge(t_done, 8 * i + 4 * r + 4)
                for bank_free, count in free:
                    wait(pe, bank_free, count)
                s = bank[SC_BANK[k]]
                nc.tensor.matmul(s[:, :], ident_bf, maskv[:, r, :], start=True, stop=False, skip_group_check=True)
                for q in range(4):
                    for w in range(4):
                        lo = r * P + w * WIN
                        mm = nc.tensor.matmul(s[WIN * w:WIN * w + WIN, q * P:q * P + P], qT[:, 4 * g + q, lo:lo + WIN],
                                              kT[:, 4 * g + q, :, lo:lo + 2 * WIN], start=False, stop=True,
                                              skip_group_check=True)
                mm.then_inc(sc_full, 1)

            def turn_probs(i, k):
                pe.wait_ge(px_done, 4 * i + k + 1)
                wait(pe, pt_done, 8 * i + PT_PROBS[k])
                for q in range(4):
                    mm = nc.tensor.transpose(bank[4][:, q * P:q * P + P], px[:, k % 2, q * P:q * P + P], ident)
                mm.then_inc(pt_full, 1)

            def weigh(i, k):
                r, g = k // 2, k % 2
                pe.wait_ge(pt_done, 8 * i + PT_PROBS[k] + 1)
                if g == 0:
                    pe.wait_ge(v_done, 8 * i + 4 * r + 4)
                wait(pe, ao_done, 4 * i + k)
                for w in range(4):
                    for q in range(4):
                        mm = nc.tensor.matmul(obank[WIN * w:WIN * w + WIN, q // 2, (q % 2) * VB:(q % 2) * VB + VB],
                                              pT[:, k % 2, q * P + w * WIN:q * P + w * WIN + WIN],
                                              vp[:, 4 * r + w, 4 * g + q, :], start=True, stop=True)
                mm.then_inc(o_full, 1)

            def turn_out(i, k):
                pe.wait_ge(ao_done, 4 * i + k + 1)
                pe.wait_ge(pt_done, 8 * i + PT_OUT[k])
                for q in range(4):
                    mm = nc.tensor.transpose(bank[4][:, q * P:q * P + P], ao[:, k % 2, q * P:q * P + P], ident)
                mm.then_inc(pt_full, 1)

            def project_out(i, next_scores):
                pe.wait_ge(pt_done, 8 * i + 8)
                pe.wait_ge(ld_o, (i // B) * 16 + 16)
                if next_scores:
                    pe.wait_ge(sh_done, 4 * i + 6)
                for c in range(PAIRS):
                    mm = nc.tensor.matmul(bank[2][:, 0:S], wo[:, c, :], aoT[:, c, :], start=(c == 0), stop=(c == PAIRS - 1))
                mm.then_inc(po_full, 1)

            def hidden(i, c, next_scores):
                if c == 0:
                    pe.wait_ge(ffn_in, i + 1)
                    pe.wait_ge(ld_w1, (i // B) * 16 + 16)
                if c == 2:
                    pe.wait_ge(h_done, 3 * i + 1)
                elif next_scores:
                    pe.wait_ge(sh_done, 4 * i + 7 + c)
                elif c == 1:
                    pe.wait_ge(z_ready, B + i)
                n = P if c < 2 else FFR
                for half in range(2):
                    mm = nc.tensor.matmul(bank[2 + c % 2][0:n, half * S:half * S + S], w1[:, half * FF + c * P:half * FF + c * P + n],
                                          lnt[:, S:2 * S], start=True, stop=True)
                mm.then_inc(hd_full, 1)

            def contract(i, next_scores):
                pe.wait_ge(h_done, 3 * i + 3)
                pe.wait_ge(ld_w2, (i // B) * 32 + 32)
                if next_scores:
                    pe.wait_ge(sh_done, 4 * i + 9)
                for c in range(3):
                    mm = nc.tensor.matmul(bank[3][:, 0:S], w2[:, c, :], hT[:, c, :], start=(c == 0), stop=(c == 2))
                mm.then_inc(ct_full, 1)

            def step(t, odd, p0, p1, p2):
                i, f = t - 1, t - 2
                for s in range(8):
                    if p0:
                        projection(t, s, odd)
                    if s == 0 and p1:
                        turn_probs(i, 1)
                    if s == 2 and p1:
                        scores(i, 2, (sh_done, 4 * i + 2), (z1_done, i))
                    if s == 3 and p1:
                        scores(i, 3, (sh_done, 4 * i + 1), (z_ready, B - 1 + i))
                    if s == 4 and p1:
                        turn_probs(i, 3)
                    if s in (4, 5, 6) and p2:
                        hidden(f, s - 4, p1)
                    if s == 6 and p0:
                        scores(t, 0, (sh_done, 4 * t), *([(h_done, 3 * f + 2)] if p2 else []))
                    if s == 7 and p0:
                        scores(t, 1, (sh_done, 4 * t - 1), *([(h_done, 3 * f + 3)] if p2 else []))
                    if s >= 2 and p0:
                        turn(t, s - 2, s)
                    if s < 2 and p1:
                        turn(i, s + 6, s)
                    if s in (0, 1, 4, 5) and p1:
                        weigh(i, (0, 1, 0, 0, 2, 3)[s])
                    if s == 0 and p2:
                        pe.wait_ge(xf_ready, f + 1)
                        ln_mean_pe(xf[:, :], S, LN_S2 + f)
                    if s == 3 and p1:
                        turn_probs(i, 2)
                    if s == 7 and p0:
                        turn_probs(t, 0)
                    if s >= 2 and p0:
                        values(t, s - 2, s, odd, True)
                    if s < 2 and p1:
                        values(i, s + 6, s, 1 - odd, p0)
                    if s in (1, 2, 5, 6) and p1:
                        turn_out(i, (0, 0, 1, 0, 0, 2, 3)[s])
                    if s == 1 and p2:
                        ln_var_pe(S, LN_S2 + f)
                    if s == 2 and p2:
                        ln_wide_pe(S, LN_S2 + f)
                    if s == 7 and p2:
                        contract(f, p0)
                    if s == 7 and p1:
                        project_out(i, p0)

            pe.wait_ge(masks_cast, 1)
            step(0, 0, True, False, False)
            step(1, 1, True, True, False)
            with pe.Fori(2, ITEMS - 1, 2) as t:
                step(t, 0, True, True, True)
                step(t + 1, 1, True, True, True)
            step(ITEMS, 0, False, True, True)
            step(ITEMS + 1, 1, False, False, True)

            pe.wait_ge(ld_s3, 16 * 7)
            pe.wait_ge(s3["w"], 1)
            with pe.Fori(0, B) as b:
                pe.wait_ge(z_ready, b + (ITEMS + 1))
                ln_mean_pe(Z[:, b, :], S, 3 * b + LN_S3)
                ln_var_pe(S, 3 * b + LN_S3)
                ln_wide_pe(S, 3 * b + LN_S3)
                pe.wait_ge(x2_ready, b + 1)
                ln_mean_pe(X[:, b, :], S, 3 * b + (LN_S3 + 1))
                ln_var_pe(S, 3 * b + (LN_S3 + 1))
                ln_wide_pe(S, 3 * b + (LN_S3 + 1))
                pe.wait_ge(ln_done, 3 * b + (LN_S3 + 2))
                for k in range(4):
                    nc.tensor.matmul(bank[k // 2][:, (k % 2) * S:(k % 2) * S + S], s3w[:, k * P:k * P + P], s3xn,
                                     start=True, stop=True)
                for i in range(2):
                    mm = nc.tensor.matmul(bank[2][:, i * P:i * P + P], s3xn[:, i * P:i * P + P], s3w[:, 4 * P:5 * P],
                                          start=True, stop=True)
                mm.then_inc(s3["qkv"], 1)
                for m in range(len(JOBS) + 2):
                    if m < len(JOBS):
                        r, heads = JOBS[m]
                        w = P * (r + 1)
                        if m == 0:
                            pe.wait_ge(s3["qk"], 2 * b + 2)
                        if m in (0, 6):
                            pe.wait_ge(s3["qm"], 2 * b + 1 + m // 6)
                        if m >= 2:
                            pe.wait_ge(s3["add"], len(JOBS) * b + m - 1)
                        for n, h in enumerate(heads):
                            mm = nc.tensor.matmul(bank[3 + m % 2][:, n * w:n * w + w], qm[:, h, r * P:r * P + P],
                                                  s3k[:, 0:w], start=True, stop=True)
                        mm.then_inc(s3["full"], 1)
                    if 1 <= m <= len(JOBS):
                        n = m - 1
                        pe.wait_ge(s3["px"], len(JOBS) * b + n + 1)
                        if n >= 1:
                            pe.wait_ge(s3["pts"], len(JOBS) * b + n)
                        for q in range(4):
                            mm = nc.tensor.transpose(lnbank[:, q * P:q * P + P], px[:, n % 2, q * P:q * P + P], ident)
                        mm.then_inc(s3["ptf"], 1)
                    if m >= 2:
                        n = m - 2
                        r, heads = JOBS[n]
                        pe.wait_ge(s3["pts"], len(JOBS) * b + n + 1)
                        if n == 0:
                            pe.wait_ge(s3["v"], b + 1)
                        for y, h in enumerate(heads):
                            g, row = h // 4, WIN * (h % 4)
                            lo = (g % 2) * S + r * P
                            for kb in range(r + 1):
                                q = y * (r + 1) + kb
                                nc.tensor.matmul(bank[g // 2][row:row + WIN, lo:lo + P], vs[:, kb, h, :],
                                                 pT[:, n % 2, q * P:q * P + P], start=(kb == 0), stop=(kb == r))
                            for kb in range(r + 1):
                                q = y * (r + 1) + kb
                                mm = nc.tensor.matmul(obank[row:row + WIN, g // 2, lo:lo + P], const("ones"),
                                                      pT[:, n % 2, q * P:q * P + P], start=(kb == 0), stop=(kb == r))
                        mm.then_inc(s3["pv"], 1)
                pe.wait_ge(s3["ot"], b + 1)
                for g in range(4):
                    mm = nc.tensor.matmul(bank[3][:, 0:S], s3wo[:, g, :], s3ot[:, g, :], start=(g == 0), stop=(g == 3))
                mm.then_inc(s3["y"], 1)
                pe.wait_ge(s3["ys"], b + 1)
                ln_mean_pe(s3y, S, 3 * b + (LN_S3 + 2))
                ln_var_pe(S, 3 * b + (LN_S3 + 2))
                ln_wide_pe(S, 3 * b + (LN_S3 + 2))

            pe.wait_ge(ld_gate, 64)
            pe.wait_ge(ld_s4, 16 * (NE + 1))
            pe.wait_ge(x3_ready, B)
            with pe.Fori(0, B // 2) as g:
                xg = X[:, :, :].rearrange("p (g b) t -> p g (b t)", b=2)[:, g, :]
                ln_mean_pe(xg, 512, g + LN_S4)
                ln_var_pe(512, g + LN_S4)
                ln_wide_pe(512, g + LN_S4)
                pe.wait_ge(ln_done, g + (LN_S4 + 1))
                for i in range(4):
                    mm = nc.tensor.matmul(bank[0][:, NE * i:NE * i + NE], s4xn[:, i * P:i * P + P], gw[:, :], start=True, stop=True)
                mm.then_inc(s4["gate"], 1)
                pe.wait_ge(s4["xc"], g + 1)
                for i in range(4):
                    mm = nc.tensor.transpose(bank[1][:, i * P:i * P + P], s4x[:, i * P:i * P + P], ident)
                mm.then_inc(s4["xt"], 1)

                def up(e, c):
                    n = 4 * e + c
                    if n >= 2:
                        pe.wait_ge(s4["relu"], 4 * NE * g + n - 1)
                    nc.tensor.matmul(bank[2 + n % 2][:, :], mw1[:, e, c * P:c * P + P], s4xn, start=True,
                                     stop=True).then_inc(s4["hf"], 1)

                def down(e):
                    pe.wait_ge(s4["relu"], 4 * NE * g + 4 * e + 4)
                    if e >= 2:
                        pe.wait_ge(s4["ofr"], NE * g + e - 1)
                    ob = (bank[4][:, :], obank[:, 0, :])[e % 2]
                    for i in range(4):
                        for c in range(4):
                            mm = nc.tensor.matmul(ob[:, i * P:i * P + P], h1[:, e % 2, c, i * P:i * P + P], mw2[:, e, c, :],
                                                  start=(c == 0), stop=(c == 3))
                    mm.then_inc(s4["of"], 1)

                for e in range(NE + 1):
                    if e < NE:
                        for c in range(4):
                            up(e, c)
                    if e >= 1:
                        down(e - 1)

        @block.scalar
        def _(act):
            def ln_sq_act(w, u):
                act.wait_ge(ln_d, u + 1)
                nc.scalar.activation(lnsq[:, 0:w], lnd[:, 0:w], ACT.Square).then_inc(ln_sq, 1)

            act.wait_ge(ld_const, 48)
            act.wait_ge(s1["wt"], 1)
            nc.scalar.copy(w1t, bank[1][:, :]).then_inc(s1["wts"], 1)
            act.wait_ge(ld_s1, 80)
            for j in range(B // 2):
                act.wait_ge(s1["xt"], j + 1)
                nc.scalar.copy(X[:, 2 * j:2 * j + 2, :].rearrange("p b t -> p (b t)"), bank[0][:, :]).then_inc(s1["x"], 1)
                ln_sq_act(512, LN_S1 + 3 * j)
                act.wait_ge(s1["qkv"], j + 1)
                nc.scalar.copy(s1q, bank[0][:, :])
                for i in range(2):
                    last = nc.scalar.copy(s1kv[:, 2 * i:2 * i + 2, :].rearrange("p i n -> p (i n)"), bank[1 + i][:, :])
                last.then_inc(s1["sb"], 1)
                act.wait_ge(s1["n2m"], j + 1)
                nc.scalar.activation(s1nr, s1n2, ACT.Sqrt).then_inc(s1["nr"], 1)
                act.wait_ge(s1["o"], j + 1)
                for bb in range(2):
                    last = nc.scalar.activation(s1o[:, bb * 256:bb * 256 + 256], obank[:, 0, bb * 256:bb * 256 + 256],
                                                ACT.Identity, bias=s1bv[:, bb:bb + 1], scale=nrm[:, 0:1])
                last.then_inc(s1["os"], 1)
                act.wait_ge(s1["y"], j + 1)
                nc.scalar.activation(s1y, obank[:, 1, :], ACT.Identity, bias=bout[:, :]).then_inc(s1["ys"], 1)
                for n in (1, 2):
                    ln_sq_act(512, LN_S1 + 3 * j + n)

            def take_xs(t, buf):
                act.wait_ge(z_ready, t + 1)
                wait(act, v_full, 8 * t - 8)
                nc.scalar.copy(buf[0:64, WIN:KW], Z[0:64, t % B, :])
                nc.scalar.copy(buf[64:P, WIN + 1:KW], Z[64:P, t % B, 0:S - 1]).then_inc(xs_ready, 1)

            def take_raw(t, s):
                act.wait_ge(p_full, 8 * t + s + 1)
                wait(act, n2_raw, 8 * t + s - 1)
                nc.scalar.activation(sq[:, s % 2, :], bank[s % 2][:, :], ACT.Square).then_inc(sq_done, 1)
                wait(act, t_full, 8 * t + s - 7)
                nc.scalar.copy(rot[:, s, :], bank[s % 2][:, :]).then_inc(raw_done, 1)

            def take_values(i, w, s):
                act.wait_ge(v_full, 8 * i + w + 1)
                if w % 4 == 0:
                    wait(act, o_full, 4 * i - 2 + w // 2)
                nc.scalar.copy(vp[0:64, w, :, 0:DH], bank[s % 2][0:64, :].rearrange("p (a d) -> p a d", d=DH))
                nc.scalar.copy(vp[64:P, w, :, DH + 1:2 * DH + 1],
                               bank[s % 2][64:P, :].rearrange("p (a d) -> p a d", d=DH)).then_inc(v_done, 1)

            def take_turned(i, c, s):
                r, kind, half = c // 4, (c // 2) % 2, c % 2
                act.wait_ge(t_full, 8 * i + c + 1)
                if c in (0, 2):
                    wait(act, sc_full, 4 * i - 2 + c)
                src = bank[(s + 1) % 2][:, :].rearrange("p (a n) -> p a n", a=4)
                pairs = slice(4 * half, 4 * half + 4)
                if kind == 0:
                    last = nc.scalar.copy(qT[:, pairs, r * P:r * P + P], src)
                else:
                    lo = WIN + r * P
                    nc.scalar.copy(kT[0:64, pairs, 0, lo:lo + P], src[0:64])
                    last = nc.scalar.copy(kT[64:P, pairs, 1, lo:lo + P], src[64:P])
                last.then_inc(t_done, 1)

            def exps(i, k):
                act.wait_ge(sh_done, 4 * i + k + 1)
                wait(act, pt_full, 8 * i + (PT_PROBS[k - 2] + 1 if k >= 2 else PT_PROBS[k + 2] - 7))
                nc.scalar.activation(px[:, k % 2, :], sh[:, k % 2, :], ACT.Exp).then_inc(px_done, 1)

            def take_probs(i, k):
                act.wait_ge(pt_full, 8 * i + PT_PROBS[k] + 1)
                wait(act, o_full, 4 * i + k - 1)
                nc.scalar.copy(pT[:, k % 2, :], bank[4][:, :]).then_inc(pt_done, 1)

            def take_out(i, k):
                r, g = k // 2, k % 2
                act.wait_ge(pt_full, 8 * i + PT_OUT[k] + 1)
                if k == 0:
                    wait(act, po_full, i)
                nc.scalar.copy(aoT[:, 4 * g:4 * g + 4, r * P:r * P + P],
                               bank[4][:, :].rearrange("p (a n) -> p a n", a=4)).then_inc(pt_done, 1)

            def gelu(i, c):
                n = P if c < 2 else FFR
                act.wait_ge(hd_full, 3 * i + c + 1)
                nc.scalar.activation(ge[0:n, c, :], bank[2 + c % 2][0:n, S:2 * S], ACT.Gelu,
                                     bias=b1g[0:n, c, bass.ds(i // B, 1)]).then_inc(ge_done, 1)

            def step(t, odd, p0, p1, p2):
                i, f = t - 1, t - 2
                for s in range(8):
                    if p0:
                        take_raw(t, s)
                    if s == 0 and p1:
                        take_probs(i, 1)
                    if s == 3 and p1:
                        exps(i, 2)
                    if s == 4 and p1:
                        take_probs(i, 3)
                    if s in (4, 5, 6) and p2:
                        gelu(f, s - 4)
                    if s == 7 and p0:
                        exps(t, 0)
                    if s >= 2 and p0:
                        take_turned(t, s - 2, s)
                    if s < 2 and p1:
                        take_turned(i, s + 6, s)
                    if s == 0 and p2:
                        act.wait_ge(z1_done, f + 1)
                        nc.scalar.copy(xf[0:64, :], Z[0:64, f % B, :])
                        nc.scalar.copy(xf[64:P, 1:S], Z[64:P, f % B, 0:S - 1]).then_inc(xf_ready, 1)
                    if s == 3 and p1:
                        take_probs(i, 2)
                        exps(i, 3)
                    if s == 7 and p0:
                        take_probs(t, 0)
                        exps(t, 1)
                    if s >= 2 and p0:
                        take_values(t, s - 2, s)
                    if s < 2 and p1:
                        take_values(i, s + 6, s)
                    if s in (1, 2, 5, 6) and p1:
                        take_out(i, (0, 0, 1, 0, 0, 2, 3)[s])
                    if s == 0 and p2:
                        ln_sq_act(S, LN_S2 + f)
                    if s == 5 and p0:
                        take_xs(t + 1, xs[:, 1 - odd])

            act.wait_ge(cleared, 1)
            act.wait_ge(ld_vec, 16 * 11)
            take_xs(0, xs[:, 0])
            step(0, 0, True, False, False)
            step(1, 1, True, True, False)
            with act.Fori(2, ITEMS - 1, 2) as t:
                step(t, 0, True, True, True)
                step(t + 1, 1, True, True, True)
            step(ITEMS, 0, False, True, True)
            step(ITEMS + 1, 1, False, False, True)

            act.wait_ge(s3["w"], 1)
            with act.Fori(0, B) as b:
                for n in range(2):
                    ln_sq_act(S, 3 * b + (LN_S3 + n))
                act.wait_ge(s3["qkv"], b + 1)
                nc.scalar.copy(vs[:, :, :, 0:HD], bank[2][:, 0:2 * P].rearrange("p (i h d) -> p i h d", i=2, h=H))\
                    .then_inc(s3["v"], 1)
                for m in range(NJ + 1):
                    if m < NJ:
                        r, heads = JOBS[m]
                        w = P * (r + 1)
                        act.wait_ge(s3["mx"], NJ * b + m + 1)
                        if m >= 2:
                            act.wait_ge(s3["ptf"], NJ * b + m - 1)
                        for n in range(len(heads)):
                            last = nc.scalar.activation(px[:, m % 2, n * w:n * w + w], sh[:, m % 2, n * w:n * w + w], ACT.Exp,
                                                        bias=mx[:, m % 2, n:n + 1])
                        last.then_inc(s3["px"], 1)
                    if m >= 1:
                        act.wait_ge(s3["ptf"], NJ * b + m)
                        if m >= 3:
                            act.wait_ge(s3["pv"], NJ * b + m - 2)
                        nc.scalar.copy(pT[:, (m - 1) % 2, :], lnbank[:, :]).then_inc(s3["pts"], 1)
                act.wait_ge(s3["y"], b + 1)
                nc.scalar.copy(s3y, bank[3][:, 0:S]).then_inc(s3["ys"], 1)
                ln_sq_act(S, 3 * b + (LN_S3 + 2))

            act.wait_ge(ld_gate, 64)
            with act.Fori(0, B // 2) as g:
                ln_sq_act(512, g + LN_S4)
                xg = X[:, :, :].rearrange("p (g b) t -> p g (b t)", b=2)[:, g, :]
                nc.scalar.copy(s4x, xg).then_inc(s4["xc"], 1)
                act.wait_ge(s4["xt"], g + 1)
                nc.scalar.copy(s4xt, bank[1][:, :]).then_inc(s4["xts"], 1)
                act.wait_ge(s4["d"], GATE_OPS * g + 3)
                nc.scalar.activation(pe_[:, :, :], lh[:, :, :], ACT.Exp).then_inc(s4["ex"], 1)
                for n in range(4 * NE):
                    act.wait_ge(s4["hf"], 4 * NE * g + n + 1)
                    nc.scalar.activation(h1[:, (n // 4) % 2, n % 4, :], bank[2 + n % 2][:, :], ACT.Relu,
                                         bias=mb1[:, n // 4, n % 4:n % 4 + 1]).then_inc(s4["relu"], 1)
                act.wait_ge(s4["d"], GATE_OPS * g + 16)
                nc.scalar.activation(ysq, yc, ACT.Square).then_inc(s4["ysq"], 1)
                act.wait_ge(s4["d"], GATE_OPS * g + 17)
                nc.scalar.activation(st[:, 3, :], st[:, 2, :], ACT.Sqrt, bias=eps, scale=1.0 / DIM).then_inc(s4["ystd"], 1)

        @block.vector
        def _(dve):
            tt, red = nc.vector.tensor_tensor, nc.vector.tensor_reduce

            def ln_d_dve(src, w, u):
                dve.wait_ge(ln_mean, u + 1)
                tt(lnd[:, 0:w], src, lnbank[:, 0:w], ALU.subtract).then_inc(ln_d, 1)

            def ln_eps_dve(w, u):
                dve.wait_ge(ln_var, u + 1)
                nc.vector.tensor_scalar(lnv[:, 0:w // P], lnbank[:, 0:2 * (w // P)].rearrange("p (i o) -> p i o", o=2)[:, :, 0],
                                        1e-5, None, ALU.add).then_inc(ln_eps, 1)

            def ln_out_dve(dst, w, u):
                dve.wait_ge(ln_wide, u + 1)
                tt(dst, lnd[:, 0:w], lnbank[:, 0:w], ALU.mult).then_inc(ln_done, 1)

            dve.wait_ge(ld_const, 48)
            nc.vector.tensor_copy(ident_bf, ident)
            nc.vector.tensor_copy(maskv, work[:, 2]).then_inc(masks_cast, 1)
            nc.vector.memset(w2[:, 2, :], 0.0)
            nc.vector.memset(hT[:, 2, :], 0.0)
            nc.vector.memset(xs[:, :, :], 0.0)
            nc.vector.memset(xf[:, :], 0.0)
            nc.vector.memset(kT[:, :, :, :], 0.0)
            nc.vector.memset(vp[:, :, :, :], 0.0).then_inc(cleared, 1)
            dve.wait_ge(cleared, 1)
            nc.vector.memset(vp[0:64, :, :, DH:DH + 1], 1.0)
            nc.vector.memset(vp[64:P, :, :, VB - 1:VB], 1.0)

            dve.wait_ge(ld_const, 48)
            dve.wait_ge(ld_s1, 80)
            dve.wait_ge(s3["u"], 1)
            tt(uh[:, :], bank[2][0:H, 0:384], const("neg")[0:H, :], ALU.add).then_inc(s3["ub"], 1)
            for j in range(B // 2):
                xj = X[:, 2 * j:2 * j + 2, :].rearrange("p b t -> p (b t)")
                u = LN_S1 + 3 * j
                ln_d_dve(xj, 512, u)
                ln_eps_dve(512, u)
                ln_out_dve(s1xn, 512, u)
                dve.wait_ge(s1["g"], j + 1)
                tt(s1bd, bank[3][:, :].rearrange("p (c n) -> p c n", c=4), blk.unsqueeze(1).broadcast_to([P, 4, P]), ALU.mult)
                nc.vector.tensor_scalar(s1bv, bank[4][:, 0:4].rearrange("p (b o) -> p b o", o=2)[:, :, 0], nrm[:, 1:2], None,
                                        ALU.mult).then_inc(s1["bd"], 1)
                dve.wait_ge(s1["u"], j + 1)
                tt(s1pr, s1q, obank[:, 0, :], ALU.mult).then_inc(s1["pr"], 1)
                dve.wait_ge(s1["n2"], j + 1)
                nc.vector.tensor_scalar(s1n2, obank[:, 1, :], 1e-24, None, ALU.max).then_inc(s1["n2m"], 1)
                dve.wait_ge(s1["nr"], j + 1)
                nc.vector.reciprocal(s1pr, s1nr).then_inc(s1["rn"], 1)
                dve.wait_ge(s1["rn"], j + 1)
                tt(s1qg, s1q, s1pr, ALU.mult).then_inc(s1["qg"], 1)
                ln_d_dve(s1y, 512, u + 1)
                ln_eps_dve(512, u + 1)
                ln_out_dve(lnt[:, :], 512, u + 1)
                dve.wait_ge(ln_done, u + 2)
                tt(xj, xj, lnt[:, :], ALU.add).then_inc(s1["x1"], 1)
                dve.wait_ge(s1["x1"], j + 1)
                ln_d_dve(xj, 512, u + 2)
                ln_eps_dve(512, u + 2)
                ln_out_dve(Z[:, 2 * j:2 * j + 2, :].rearrange("p b t -> p (b t)"), 512, u + 2)
            dve.wait_ge(ln_done, LN_S2)
            nc.vector.memset(n2[:, :, :], 0.0).then_inc(z_ready, B)

            dve.wait_ge(ld_vec, 16 * 11)
            rotc = const("rot").rearrange("p (k r d) -> p k r d", k=4, r=2)
            for k in range(2):
                scale = scales[:, k, :, :]
                tt(tab[:, :, 2 * k, :, :], rotc[:, 2 * k].unsqueeze(1).broadcast_to([P, DEPTH, 2, DH]),
                   scale.unsqueeze(2).broadcast_to([P, DEPTH, 2, DH]), ALU.mult)
                for lo, other in ((0, DH // 2), (DH // 2, 0)):
                    last = tt(tab[:, :, 2 * k + 1, :, lo:lo + DH // 2],
                              rotc[:, 2 * k + 1, :, lo:lo + DH // 2].unsqueeze(1).broadcast_to([P, DEPTH, 2, DH // 2]),
                              scale[:, :, other:other + DH // 2].unsqueeze(2).broadcast_to([P, DEPTH, 2, DH // 2]), ALU.mult)
            last.then_inc(tab_done, 1)
            dve.wait_ge(tab_done, 1)

            def heads(ap):
                return ap.rearrange("p (h d) -> p h d", d=DH)

            def norms(t, c):
                dve.wait_ge(sq_done, 8 * t + c + 1)
                red(n2[:, c % 2, :], heads(sq[:, c % 2, :]), AX, ALU.add).then_inc(n2_raw, 1)
                dve.wait_ge(n2_raw, 8 * t + c + 1)
                nc.vector.tensor_scalar(n2m[:, c % 2, :], n2[:, c % 2, :], 1e-24, None, ALU.max).then_inc(n2_done, 1)

            def normalise(t, c):
                r, kind = c // 4, (c // 2) % 2
                dve.wait_ge(raw_done, 8 * t + c + 1)
                dve.wait_ge(rn_done, 8 * t + c + 1)
                tt(heads(qn[:, c % 2, :]), heads(rot[:, c, :]), rn[:, c % 2, :].unsqueeze(2).broadcast_to([P, PAIRS, DH]),
                   ALU.mult).then_inc(qn_done, 1)
                dve.wait_ge(qn_done, 8 * t + c + 1)
                cos = tab[:, bass.ds(t // B, 1), 2 * kind, r, :].broadcast_to([P, PAIRS, DH])
                tt(heads(t1[:, c % 2, :]), heads(qn[:, c % 2, :]), cos, ALU.mult).then_inc(t1_done, 1)

            def rotated(t, c):
                dve.wait_ge(t1_done, 8 * t + c + 1)
                dve.wait_ge(t2_done, 8 * t + c + 1)
                tt(rot[:, c, :], t1[:, c % 2, :], t2[:, c % 2, :], ALU.add).then_inc(rot_done, 1)

            def shift_scores(i, k):
                b = SC_BANK[k]
                dve.wait_ge(sc_full, 4 * i + k + 1)
                red(mx[:, k % 2, :], heads(bank[b][:, :]), AX, ALU.max).then_inc(mx_done, 1)
                dve.wait_ge(mx_done, 4 * i + k + 1)
                wait(dve, px_done, 4 * i + k - 1)
                tt(heads(sh[:, k % 2, :]), heads(bank[b][:, :]), mx[:, k % 2, :].unsqueeze(2).broadcast_to([P, PAIRS, DH]),
                   ALU.subtract).then_inc(sh_done, 1)

            def divide_out(i, k):
                b = k % 2
                dve.wait_ge(o_full, 4 * i + k + 1)
                o = obank[:, :, 0:2 * VB].rearrange("p c (h n) -> p c h n", n=DH + 1)
                nc.vector.reciprocal(rd[:, b, :].rearrange("p (c h) -> p c h", c=2), o[:, :, :, DH]).then_inc(rd_done, 1)
                dve.wait_ge(rd_done, 4 * i + k + 1)
                wait(dve, pt_full, 8 * i + (PT_OUT[k - 2] + 1 if k >= 2 else PT_OUT[k + 2] - 7))
                tt(ao[:, b, :].rearrange("p (c h n) -> p c h n", c=2, h=4), o[:, :, :, 0:DH],
                   rd[:, b, :].rearrange("p (c h) -> p c h", c=2).unsqueeze(3).broadcast_to([P, 2, 4, DH]),
                   ALU.mult).then_inc(ao_done, 1)

            def add_attention(i):
                dve.wait_ge(po_full, i + 1)
                z = Z[:, i % B, :]
                tt(z, z, bank[2][:, 0:S], ALU.add).then_inc(z1_done, 1)

            def scale_norm(i):
                l = bass.ds(i // B, 1)
                ln_out_dve(lnt[:, 0:S], S, LN_S2 + i)
                dve.wait_ge(ln_done, i + (LN_S2 + 1))
                nc.vector.tensor_scalar(lnt[:, S:2 * S], lnt[:, 0:S], lng[:, l], lnb[:, l], ALU.mult, ALU.add).then_inc(ffn_in, 1)

            def gate(i, c):
                l = bass.ds(i // B, 1)
                n = P if c < 2 else FFR
                dve.wait_ge(ge_done, 3 * i + c + 1)
                nc.vector.scalar_tensor_tensor(out=hT[0:n, c, :], in0=bank[2 + c % 2][0:n, 0:S], scalar=b1a[0:n, c, l],
                                               in1=ge[0:n, c, :], op0=ALU.add, op1=ALU.mult).then_inc(h_done, 1)

            def add_feed_forward(i):
                dve.wait_ge(ct_full, i + 1)
                z = Z[:, i % B, :]
                nc.vector.scalar_tensor_tensor(out=z, in0=bank[3][:, 0:S], scalar=b2c[:, bass.ds(i // B, 1)], in1=z, op0=ALU.add,
                                               op1=ALU.add).then_inc(z_ready, 1)

            def step(t, odd, p0, p1, p2):
                i, f = t - 1, t - 2
                for s in range(8):
                    if s >= 2 and p0:
                        rotated(t, s - 2)
                    if s < 2 and p1:
                        rotated(i, s + 6)
                    if s >= 1 and p0:
                        normalise(t, s - 1)
                    if s == 0 and p1:
                        normalise(i, 7)
                    if s in (2, 3) and p1:
                        shift_scores(i, s)
                    if s in (4, 5, 6) and p2:
                        gate(f, s - 4)
                    if s in (6, 7) and p0:
                        shift_scores(t, s - 6)
                    if p0:
                        norms(t, s)
                    if s in (0, 1, 4, 5) and p1:
                        divide_out(i, (0, 1, 0, 0, 2, 3)[s])
                    if s == 0 and p2:
                        ln_d_dve(xf[:, :], S, LN_S2 + f)
                    if s == 1 and p2:
                        ln_eps_dve(S, LN_S2 + f)
                    if s == 2 and p2:
                        scale_norm(f)
                    if s == 7 and p2:
                        add_feed_forward(f)
                    if s == 7 and p1:
                        add_attention(i)

            step(0, 0, True, False, False)
            step(1, 1, True, True, False)
            with dve.Fori(2, ITEMS - 1, 2) as t:
                step(t, 0, True, True, True)
                step(t + 1, 1, True, True, True)
            step(ITEMS, 0, False, True, True)
            step(ITEMS + 1, 1, False, False, True)

            dve.wait_ge(rel_in, 16)
            with dve.Fori(0, B) as b:
                x, u = X[:, b, :], 3 * b + LN_S3
                ln_d_dve(Z[:, b, :], S, u)
                ln_eps_dve(S, u)
                ln_out_dve(lnt[:, 0:S], S, u)
                dve.wait_ge(ln_done, u + 1)
                tt(x, x, lnt[:, 0:S], ALU.add).then_inc(x2_ready, 1)
                dve.wait_ge(x2_ready, b + 1)
                ln_d_dve(x, S, u + 1)
                ln_eps_dve(S, u + 1)
                ln_out_dve(s3xn, S, u + 1)
                dve.wait_ge(s3["qkv"], b + 1)
                for n in range(2):
                    tt(s3part[:, n, :], bank[n][:, :], const("rope")[:, 512 * n:512 * n + 512], ALU.mult).then_inc(s3["part"], 1)
                for n, dst in enumerate((s3q, s3k)):
                    dve.wait_ge(s3["part"], 2 * b + n + 1)
                    tt(dst, s3part[:, n, 0:S], s3part[:, n, S:2 * S], ALU.add).then_inc(s3["qk"], 1)
                for m, (r, hs) in enumerate(JOBS):
                    w = P * (r + 1)
                    dve.wait_ge(s3["full"], NJ * b + m + 1)
                    if m >= 2:
                        dve.wait_ge(s3["px"], NJ * b + m - 1)
                    part = sh[:, m % 2, :].rearrange("p (h n) -> p h n", n=w)
                    tt(part, bank[3 + m % 2][:, :].rearrange("p (h n) -> p h n", n=w), bias[:, hs[0]:hs[-1] + 1, S - w:S]
                       if r == 0 else bias[:, hs[0]:hs[-1] + 1, :], ALU.add).then_inc(s3["add"], 1)
                    dve.wait_ge(s3["add"], NJ * b + m + 1)
                    red(mx[:, m % 2, 0:len(hs)], part, AX, ALU.max, negate=True).then_inc(s3["mx"], 1)
                dve.wait_ge(s3["pv"], NJ * b + NJ)
                nc.vector.reciprocal(s3den, obank[:, :, :]).then_inc(s3["den"], 1)
                dve.wait_ge(s3["den"], b + 1)
                for n in range(2):
                    last = tt(aoTf[:, 512 * n:512 * n + 512].rearrange("p (c t) -> p c t", c=4),
                              bank[n][:, :].rearrange("p (c t) -> p c t", c=4)[:, :, ::-1],
                              s3den[:, n, :].rearrange("p (c t) -> p c t", c=4)[:, :, ::-1], ALU.mult)
                last.then_inc(s3["ot"], 1)
                ln_d_dve(s3y, S, u + 2)
                ln_eps_dve(S, u + 2)
                ln_out_dve(lnt[:, 0:S], S, u + 2)
                dve.wait_ge(ln_done, u + 3)
                tt(x, x, lnt[:, 0:S], ALU.add).then_inc(x3_ready, 1)

            dve.wait_ge(ld_gate, 64)
            dve.wait_ge(x3_ready, B)
            with dve.Fori(0, B // 2) as g:
                ln_d_dve(X[:, :, :].rearrange("p (g b) t -> p g (b t)", b=2)[:, g, :], 512, g + LN_S4)
                ln_eps_dve(512, g + LN_S4)
                ln_out_dve(s4xn, 512, g + LN_S4)
                done = [0]

                def link(ins):
                    done[0] += 1
                    ins.then_inc(s4["d"], 1)
                    dve.wait_ge(s4["d"], GATE_OPS * g + done[0])

                def by_expert(ap):
                    return ap.unsqueeze(2).broadcast_to([P, 4, NE])

                dve.wait_ge(s4["gate"], g + 1)
                link(tt(lg[:, :, :], bank[0][:, 0:4 * NE].rearrange("p (i e) -> p i e", i=4),
                        gb[:, :].unsqueeze(1).broadcast_to([P, 4, NE]), ALU.add))
                link(red(g1[:, :], lg[:, :, :], AX, ALU.max))
                link(tt(lh[:, :, :], lg[:, :, :], by_expert(g1[:, :]), ALU.subtract))
                dve.wait_ge(s4["ex"], g + 1)
                link(red(g1[:, :], pe_[:, :, :], AX, ALU.add))
                link(nc.vector.reciprocal(g2[:, :], g1[:, :]))
                link(tt(pr_[:, :, :], pe_[:, :, :], by_expert(g2[:, :]), ALU.mult))
                other = pr_[:, :, :].unsqueeze(2).broadcast_to([P, 4, NE, NE])
                own = pr_[:, :, :].unsqueeze(3).broadcast_to([P, 4, NE, NE])

                def square(ap):
                    return ap.rearrange("p i (e o) -> p i e o", e=NE)

                link(tt(square(cmp1[:, :, :]), other, own, ALU.is_ge))
                link(tt(square(cmp2[:, :, :]), other, own, ALU.is_gt))
                link(tt(cmp3[:, :, :], cmp1[:, :, :], const("lower").unsqueeze(1).broadcast_to([P, 4, NE * NE]), ALU.mult))
                link(tt(cmp4[:, :, :], cmp2[:, :, :], const("upper").unsqueeze(1).broadcast_to([P, 4, NE * NE]), ALU.mult))
                link(tt(cmp1[:, :, :], cmp3[:, :, :], cmp4[:, :, :], ALU.add))
                link(red(rank[:, :, :], square(cmp1[:, :, :]), AX, ALU.add))
                link(nc.vector.tensor_scalar(msk[:, :, :], rank[:, :, :], 1.5, None, ALU.is_lt))

                def tokens(ap):
                    return ap.rearrange("p (i n) -> p i n", i=4)

                for e in range(NE):
                    dve.wait_ge(s4["of"], NE * g + e + 1)
                    ob = (bank[4][:, :], obank[:, 0, :])[e % 2]
                    tt(tokens(ob2[:, e % 2, :]), tokens(ob), mb2[:, e, :].unsqueeze(1).broadcast_to([P, 4, DIM]), ALU.add)\
                        .then_inc(s4["ofr"], 1)
                    dve.wait_ge(s4["ofr"], NE * g + e + 1)
                    if e >= 2:
                        dve.wait_ge(s4["acc"], (NE - 1) * g + max(e - 2, 1))
                    tt(tokens(oms[:, e % 2, :]), tokens(ob2[:, e % 2, :]), msk[:, :, e:e + 1].broadcast_to([P, 4, DIM]), ALU.mult)\
                        .then_inc(s4["om"], 1)
                dve.wait_ge(s4["acc"], (NE - 1) * g + NE - 1)
                link(red(st[:, 0, :], tokens(acc[:, :]), AX, ALU.add))
                link(nc.vector.tensor_scalar(st[:, 1, :], st[:, 0, :], 1.0 / DIM, None, ALU.mult))
                link(tt(tokens(yc), tokens(acc[:, :]), st[:, 1, :].unsqueeze(2).broadcast_to([P, 4, DIM]), ALU.subtract))
                dve.wait_ge(s4["ysq"], g + 1)
                link(red(st[:, 2, :], tokens(ysq), AX, ALU.add))
                dve.wait_ge(s4["ystd"], g + 1)
                link(nc.vector.reciprocal(st[:, 0, :], st[:, 3, :]))
                link(tt(tokens(yn), tokens(yc), st[:, 0, :].unsqueeze(2).broadcast_to([P, 4, DIM]), ALU.mult))
                assert done[0] == GATE_OPS
                dve.wait_ge(s4["xts"], g + 1)
                dve.wait_ge(stored, g * 16 + 16)
                tt(outs, yn, s4xt, ALU.add).then_inc(s4["out"], 1)

        @block.gpsimd
        def _(pool):
            tt = nc.gpsimd.tensor_tensor
            pool.wait_ge(ld_const, 48)

            def inverse_norms(t, c):
                pool.wait_ge(n2_done, 8 * t + c + 1)
                tt(rn[:, c % 2, :], n2m[:, c % 2, :], const("mhalf"), ALU.pow).then_inc(rn_done, 1)

            def sines(t, c):
                r, kind = c // 4, (c // 2) % 2
                pool.wait_ge(qn_done, 8 * t + c + 1)
                tt(touch[:, c:c + 1], const("mhalf")[:, 0:1], const("mhalf")[:, 0:1], ALU.mult)
                swapped = qn[:, c % 2, :].rearrange("p (h o d) -> p h o d", o=2, d=DH // 2)[:, :, ::-1, :]
                sin = tab[:, bass.ds(t // B, 1), 2 * kind + 1, r, :].rearrange("p l (o d) -> p l o d", o=2)\
                    .broadcast_to([P, PAIRS, 2, DH // 2])
                tt(t2[:, c % 2, :].rearrange("p (h o d) -> p h o d", o=2, d=DH // 2), swapped, sin, ALU.mult).then_inc(t2_done, 1)

            def inverse_deviations(w, u):
                pool.wait_ge(ln_eps, u + 1)
                tt(lnr[:, 0:w // P], lnv[:, 0:w // P], const("mhalf")[:, 0:w // P], ALU.pow).then_inc(ln_rstd, 1)

            for u in range(LN_S1, LN_S2):
                inverse_deviations(512, u)

            pool.wait_ge(tab_done, 1)

            def step(t, odd, p0, p1, p2):
                for s in range(8):
                    if s >= 1 and p0:
                        sines(t, s - 1)
                    if s == 0 and p1:
                        sines(t - 1, 7)
                    if p0:
                        inverse_norms(t, s)
                    if s == 1 and p2:
                        inverse_deviations(S, t - 2 + LN_S2)

            step(0, 0, True, False, False)
            step(1, 1, True, True, False)
            with pool.Fori(2, ITEMS - 1, 2) as t:
                step(t, 0, True, True, True)
                step(t + 1, 1, True, True, True)
            step(ITEMS, 0, False, True, True)
            step(ITEMS + 1, 1, False, False, True)

            pool.wait_ge(v_full, 8 * ITEMS)
            nc.gpsimd.memset(wv[:, 0:4 * P], 0.0).then_inc(cleared, 1)
            pool.wait_ge(o_full, 4 * ITEMS)
            nc.gpsimd.memset(qTf[:, 0:2 * H * WIN], 0.0)
            pool.wait_ge(ld_s3, 16 * 7)
            for k in (0, 2):
                src = s3w[:, k * P:k * P + P].rearrange("p (h o d) -> p h o d", o=2, d=HD // 2)
                dst = s3w[:, k * P + P:k * P + 2 * P].rearrange("p (h o d) -> p h o d", o=2, d=HD // 2)
                nc.gpsimd.tensor_scalar(dst[:, :, 0, :], src[:, :, 1, :], -1.0, None, ALU.mult)
                last = nc.gpsimd.tensor_copy(dst[:, :, 1, :], src[:, :, 0, :])
            last.then_inc(s3["w"], 1)
            with pool.Fori(0, B) as b:
                inverse_deviations(S, 3 * b + LN_S3)
                inverse_deviations(S, 3 * b + (LN_S3 + 1))
                pool.wait_ge(s3["qk"], 2 * b + 1)
                for n in range(2):
                    hs = slice(8 * n, 8 * n + 8)
                    for r in range(2):
                        back = s3q.rearrange("p (r t) -> p r t", r=2)[:, r, ::-1]
                        last = tt(qm[:, hs, r * P:r * P + P], back.unsqueeze(1).broadcast_to([P, 8, P]),
                                  const("headm")[:, hs].unsqueeze(2).broadcast_to([P, 8, P]), ALU.mult)
                    last.then_inc(s3["qm"], 1)
                inverse_deviations(S, 3 * b + (LN_S3 + 2))
            with pool.Fori(0, B // 2) as g:
                inverse_deviations(512, g + LN_S4)
                pool.wait_ge(s4["om"], NE * g + 2)
                tt(acc[:, :], oms[:, 0, :], oms[:, 1, :], ALU.add).then_inc(s4["acc"], 1)
                for e in range(2, NE):
                    pool.wait_ge(s4["om"], NE * g + e + 1)
                    pool.wait_ge(s4["acc"], (NE - 1) * g + e - 1)
                    tt(acc[:, :], acc[:, :], oms[:, e % 2, :], ALU.add).then_inc(s4["acc"], 1)


def constants():
    import math

    import numpy as np

    f = np.float32
    c = {}
    c["ident"] = np.eye(P, dtype=f)
    c["onesm"] = np.full((P, P), 1.0 / DIM, f)
    head = np.arange(P) // HD
    c["blk"] = (head[:, None] == head[None, :]).astype(f)
    c["headm"] = (head[:, None] == np.arange(H)[None, :]).astype(f)
    half = np.arange(0, DH, 2, dtype=f)
    inv_freq = (f(1.0) / f(10000.0) ** (half / f(DH))).astype(f)
    t = np.arange(S, dtype=f)
    freqs = t[:, None] * inv_freq[None, :]
    freqs = np.concatenate([freqs, freqs], -1)
    base = (half + f(0.4 * DH)) / f(1.4 * DH)
    power = (t - f(S // 2)) / f(WIN // 2)
    scale = base[None, :] ** power[:, None]
    scale = np.concatenate([scale, scale], -1).astype(f)
    sign = np.where(np.arange(DH) < DH // 2, -1.0, 1.0).astype(f)
    cos, sin = np.cos(freqs), np.sin(freqs)
    inv = f(1.0) / scale
    rot = np.stack([cos * scale * f(8), sin * scale * sign * f(8), cos * inv, sin * inv * sign])
    c["rot"] = rot.reshape(4, 2, P, DH).transpose(2, 0, 1, 3).reshape(P, -1)
    inv_freq = (f(1.0) / f(10000.0) ** (np.arange(0, HD, 2, dtype=f) / f(HD))).astype(f)
    emb = t[:, None] * inv_freq[None, :]
    emb = np.tile(np.concatenate([emb, emb], -1), (1, H)).T
    cos, sin, down = np.cos(emb), np.sin(emb), f(1.0 / math.sqrt(HD))
    c["rope"] = np.concatenate([cos * down, sin * down, cos, sin], 1)
    dist = (S - 1) - np.arange(384)
    rp = np.maximum(dist, 0)
    large = 16 + (np.log(np.maximum(rp, 1).astype(f) / f(16)) / f(math.log(8.0)) * f(16)).astype(np.int32)
    bucket = np.where(rp < 16, rp, np.minimum(large, 31))
    c["onehot"] = np.zeros((P, 384), f)
    c["onehot"][bucket, np.arange(384)] = 1.0
    c["onehot"][:, dist < 0] = 0.0
    c["neg"] = np.tile(np.where(dist < 0, -1e9, 0.0).astype(f), (P, 1))
    e = np.arange(NE)
    c["lower"] = np.tile((e[None, :] < e[:, None]).astype(f).reshape(1, -1), (P, 1))
    c["upper"] = np.tile((e[None, :] > e[:, None]).astype(f).reshape(1, -1), (P, 1))
    c["eps"] = np.full((P, 1), 1e-5, f)
    c["ones"] = np.ones((P, WIN), f)
    c["mhalf"] = np.full((P, PAIRS), -0.5, f)
    packed = np.concatenate([c[n].astype(f) for n, _ in WIDTHS], 1)
    q, key = np.arange(WIN)[:, None], np.arange(2 * WIN)[None, :] - WIN
    hidden = np.where((key > q) | (key < q - WIN), -1e30, 0.0)
    tile = np.tile(hidden, (4, PAIRS))
    first = tile.copy()
    first[0:WIN] = np.tile(np.where(key < 0, -1e30, hidden), (1, PAIRS))
    return packed, np.concatenate([first, tile], 1).astype(f)


_INS = ["L0_attn_x", "L0_attn_w_qkv", "L0_attn_w_out", "L0_attn_b_out", "L0_attn_norm_g", "L0_attn_norm_b",
        "L0_ffn_Wqkv", "L0_ffn_q_scale", "L0_ffn_k_scale", "L0_ffn_Wo", "L0_ffn_ln_g", "L0_ffn_ln_b", "L0_ffn_W1",
        "L0_ffn_b1", "L0_ffn_W2", "L0_ffn_b2", "L1_attn_Wq", "L1_attn_Wk", "L1_attn_Wv", "L1_attn_Wo",
        "L1_attn_rel_emb", "L1_ffn_gate_w", "L1_ffn_gate_b", "L1_ffn_w1", "L1_ffn_b1", "L1_ffn_w2", "L1_ffn_b2"]


def kernel(**inputs):
    import numpy as _np
    import concourse.bacc as _bacc
    from concourse import mybir as _mybir
    from concourse.bass_utils import run_bass_kernel_spmd as _run

    nc = _bacc.Bacc("TRN2", target_bir_lowering=False, num_devices=1)
    arrays, args = {}, {}
    packed, masks = constants()
    for name, arr in [(n, inputs[n]) for n in _INS] + [("consts", packed), ("window_masks", masks)]:
        arr = _np.ascontiguousarray(arr)
        arrays[f"in_{name}"] = arr
        args[name] = nc.dram_tensor(f"in_{name}", arr.shape, _mybir.dt.from_np(arr.dtype), kind="ExternalInput").ap()
    out = nc.dram_tensor("out_0", (B, S, DIM), _mybir.dt.float32, kind="ExternalOutput").ap()
    build(nc, args, out)
    r = _run(nc, [arrays], core_ids=[0])
    return r.results[0]["out_0"]
```

```python
from contextlib import ExitStack

import concourse.bass as bass
from concourse import mybir
from concourse.alu_op_type import AluOpType as ALU

ACT = mybir.ActivationFunctionType
F32 = mybir.dt.float32
BF16 = mybir.dt.bfloat16
AX = mybir.AxisListType.X

P = 128
B, S, DIM, H = 8, 256, 128, 16
TOK = B * S
DEPTH = 6
ITEMS = DEPTH * B
DH = 64
PAIRS = H // 2
WIN = 32
NW = S // WIN
FF = int(DIM * 4 * 2 / 3)
FFR = FF - 2 * P
HD = DIM // H
NE, EF = 8, 512
VB = 2 * (DH + 1)
KW = WIN + S

WIDTHS = [("ident", P), ("onesm", P), ("blk", P), ("headm", H), ("onehot", 384), ("neg", 384), ("ones", WIN),
          ("mhalf", PAIRS), ("rot", 4 * 2 * DH), ("rope", 4 * S), ("lower", NE * NE), ("upper", NE * NE)]
COL = {}
NCONST = 0
for _name, _width in WIDTHS:
    COL[_name] = (NCONST, NCONST + _width)
    NCONST += _width

EARLY = COL["rot"][0]

LN_S1 = 0
LN_S2 = LN_S1 + 3 * (B // 2)
LN_S3 = LN_S2 + ITEMS
LN_S4 = LN_S3 + 3 * B


def unit_a(j):
    return LN_S1 + max(3 * j - 2, 0)


def unit_b(j):
    return LN_S1 + (3 * j + 2 if j < B // 2 - 1 else 3 * j + 1)


JOBS = [job for n in range(0, H, 4)
        for job in ((0, range(n, n + 4)), (1, range(n, n + 2)), (1, range(n + 2, n + 4)))]
NJ = len(JOBS)
SC_BANK = (3, 2, 2, 3)
PT_PROBS = (0, 1, 4, 5)
PT_OUT = (2, 3, 6, 7)
GATE_OPS, TAIL_OPS = 13, 6


def wait(eng, s, value):
    if not isinstance(value, int) or value > 0:
        eng.wait_ge(s, value)


def build(nc, a, out):
    ctx = ExitStack()
    with ctx:
        def sb(name, shape, dt=F32):
            return ctx.enter_context(nc.sbuf_tensor(name, shape, dt))

        def sem(name):
            return ctx.enter_context(nc.semaphore(name))

        bank = [ctx.enter_context(nc.psum_tensor(f"bank{i}", [P, 512], F32)) for i in range(5)]
        obank = ctx.enter_context(nc.psum_tensor("obank", [P, 2, 512], F32))
        lnbank = ctx.enter_context(nc.psum_tensor("lnbank", [P, 512], F32))
        vbank = lnbank

        cst = sb("cst", [P, NCONST])
        cbf = sb("cbf", [P, P + 2 * 512], BF16)

        def const(name):
            return cst[:, COL[name][0]:COL[name][1]]

        ident, onesm, blk = const("ident"), const("onesm"), const("blk")
        ident_bf = cbf[:, 0:P]
        maskv = cbf[:, P:].rearrange("p (r n) -> p r n", r=2)
        X = sb("X", [P, B, S])
        Z = sb("Z", [P, B, S])
        work = sb("work", [P, 4, 2, 512])
        xin = work[:, 0:2].rearrange("p k a (i m) -> p (k a i) m", m=DIM)
        lnd = sb("lnd", [P, 512])
        lnsq = sb("lnsq", [P, 512])
        lnt = sb("lnt", [P, 512])
        lnv = sb("lnv", [P, 4])
        lnr = sb("lnr", [P, 4])

        wqk = sb("wqk", [P, 2 * H * DH])
        wv = sb("wv", [P, H * DH])
        wo = sb("wo", [P, PAIRS, DIM])
        w1 = sb("w1", [P, 2 * FF])
        w2 = sb("w2", [P, 3, DIM])
        lng = sb("lng", [P, DEPTH])
        lnb = sb("lnb", [P, DEPTH])
        b2c = sb("b2c", [P, DEPTH])
        b1a = sb("b1a", [P, 3, DEPTH])
        b1g = sb("b1g", [P, 3, DEPTH])
        scales = sb("scales", [P, 2, DEPTH, DH])
        tab = sb("tab", [P, DEPTH, 4, 2, DH])
        touch = sb("touch", [P, 8])
        xs = sb("xs", [P, 2, KW])
        xf = sb("xf", [P, S])
        sq = work[:, 0]
        n2 = sb("n2", [P, 2, PAIRS])
        n2m = sb("n2m", [P, 2, PAIRS])
        rn = sb("rn", [P, 2, PAIRS])
        qn = work[:, 1]
        t1 = work[:, 2]
        t2 = work[:, 3]
        rot = sb("rot", [P, 8, 512])
        qT = sb("qT", [P, PAIRS, S])
        kT = sb("kT", [P, PAIRS, 2, KW])
        vp = sb("vp", [P, NW, PAIRS, VB])
        mx = sb("mx", [P, 2, PAIRS])
        sh = sb("sh", [P, 2, 512])
        px = sb("px", [P, 2, 512])
        pT = sb("pT", [P, 2, 512])
        rd = sb("rd", [P, 2, PAIRS])
        ao = sb("ao", [P, 2, 512])
        aoT = sb("aoT", [P, PAIRS, S])
        ge = sb("ge", [P, 3, S])
        hT = sb("hT", [P, 3, S])

        vflat = vp[:, :, :, :].rearrange("p w q n -> p (w q n)")
        qTf = qT[:, :, :].rearrange("p a t -> p (a t)")
        aoTf = aoT[:, :, :].rearrange("p a t -> p (a t)")
        kTf = kT[:, :, :, :].rearrange("p a b t -> p (a b t)")
        rotf = rot[:, :, :].rearrange("p c n -> p (c n)")
        w1raw = rotf[:, 0:512].rearrange("p (c m) -> p c m", c=4)
        w1t = rotf[:, 512:1024]
        s1xn, s1q, s1pr, s1n2 = (qTf[:, 512 * i:512 * i + 512] for i in range(4))
        s1nr, s1qg, s1o, s1y = (aoTf[:, 512 * i:512 * i + 512] for i in range(4))
        s1kv = rotf[:, 1024:2048].rearrange("p (i n) -> p i n", i=4)
        s1bd = rotf[:, 2048:2560].rearrange("p (c n) -> p c n", c=4)
        s1bv = rotf[:, 2560:2562]
        nrm = sb("nrm", [P, 2])
        bout = sb("bout", [P, 1])
        bias = kTf[:, 0:H * S].rearrange("p (h t) -> p h t", h=H)
        relv = sb("relv", [WIN, H])
        uh = sb("uh", [H, 384])
        relu_dram = nc.dram_tensor("rel_by_distance", [H, 384], F32)
        s3w = wqk[:, 0:5 * P]
        s3wo = wv[:, 0:4 * P].rearrange("p (g n) -> p g n", g=4)
        s3xn = t1[:, 0, 0:S]
        s3part = qn
        dn, rdn = (sb(n, [P, 2, 4]) for n in ("dn", "rdn"))
        s3q, s3k = t1[:, 1, 0:S], (t1[:, 1, S:2 * S], t1[:, 0, S:2 * S])
        qm = rotf.rearrange("p (h t) -> p h t", h=H)
        vs = qTf[:, 0:4 * H * WIN].rearrange("p (o i h n) -> p o i h n", o=2, i=2, h=H)
        s3ot = aoTf[:, 0:4 * S].rearrange("p (g t) -> p g t", g=4)
        s3y = aoTf[:, 4 * S:5 * S]
        mw1 = vflat[:, 0:NE * EF].rearrange("p (e f) -> p e f", e=NE)
        mw2 = vflat[:, NE * EF:2 * NE * EF].rearrange("p (e c n) -> p e c n", e=NE, c=4)
        gw = sb("gw", [P, NE])
        gb = sb("gb", [P, NE])
        mb1 = sb("mb1", [P, NE, 4])
        mb2 = sb("mb2", [P, NE, DIM])
        s4xn = (t1[:, 0, :], lnt[:, :])
        s4x = ao[:, 0, :]
        s4xt = (t1[:, 1, :], aoTf[:, 0:512])
        h1 = rotf.rearrange("p (s f n) -> p s f n", s=2, f=4)
        lg, lh, pe_, pr_ = (sb(f"gate{i}", [P, 4, NE]) for i in range(4))
        g1 = sb("g1", [P, 4])
        g2 = sb("g2", [P, 4])
        cmp1, cmp2, cmp3 = (ge[:, i, :].rearrange("p (i n) -> p i n", i=4) for i in range(3))
        cmp4 = hT[:, 0, :].rearrange("p (i n) -> p i n", i=4)
        rank = sb("rank", [P, 4, NE])
        msk = sb("msk", [P, 4, NE])
        ob2 = qn
        oms = t2
        acc = ao[:, 1, :]
        st = sb("st", [P, 4, 4])
        rs = sb("rs", [P, 4])
        yc = sh[:, 0, :]
        ysq = sh[:, 1, :]
        yn = px[:, 0, :]
        outs = px[:, 1, :]

        ld_tables = sem("ld_tables")
        ld_const, ld_x, ld_s1, ld_vec = sem("ld_const"), sem("ld_x"), sem("ld_s1"), sem("ld_vec")
        ld_q, ld_k, ld_v = sem("ld_q"), sem("ld_k"), sem("ld_v")
        ld_o, ld_w1, ld_w2 = sem("ld_o"), sem("ld_w1"), sem("ld_w2")
        ld_s3, ld_s4, ld_gate = sem("ld_s3"), sem("ld_s4"), sem("ld_gate")
        rel_in = sem("rel_in")
        stored = sem("stored")
        vp_cleared = sem("vp_cleared")
        cleared, tab_done, masks_cast = sem("cleared"), sem("tab_done"), sem("masks_cast")
        ln_mean, ln_d, ln_sq, ln_var, ln_eps, ln_rstd, ln_wide, ln_done = (
            sem("ln_" + n) for n in ("mean", "d", "sq", "var", "eps", "rstd", "wide", "done"))
        s1 = {n: sem("s1_" + n) for n in ("wt", "wts", "xt", "x", "qkv", "sb", "g", "bd", "u", "pr", "n2",
                                          "n2m", "nr", "rn", "qg", "o", "os", "y", "ys", "x1")}
        z_ready = sem("z_ready")
        xs_ready = sem("xs_ready")
        p_full, v_full, t_full = sem("p_full"), sem("v_full"), sem("t_full")
        raw_done, v_done, t_done = sem("raw_done"), sem("v_done"), sem("t_done")
        sq_done, n2_done, n2_raw, rn_done = sem("sq_done"), sem("n2_done"), sem("n2_raw"), sem("rn_done")
        qn_done, t1_done, t2_done, rot_done = sem("qn_done"), sem("t1_done"), sem("t2_done"), sem("rot_done")
        sc_full, po_full, hd_full, ct_full = sem("sc_full"), sem("po_full"), sem("hd_full"), sem("ct_full")
        mx_done, sh_done, px_done = sem("mx_done"), sem("sh_done"), sem("px_done")
        pt_full, pt_done = sem("pt_full"), sem("pt_done")
        o_full, rd_done, ao_done = sem("o_full"), sem("rd_done"), sem("ao_done")
        z1_done, xf_ready, ffn_in = sem("z1_done"), sem("xf_ready"), sem("ffn_in")
        ge_done, h_done = sem("ge_done"), sem("h_done")
        s3 = {n: sem("s3_" + n) for n in ("w", "proj", "part", "qk", "qm", "v", "full", "add", "mx", "px", "pn", "rdn",
                                          "ptf", "pts", "pv", "ot", "y", "ys", "u", "ub")}
        x2_ready, x3_ready = sem("x2_ready"), sem("x3_ready")
        s4 = {n: sem("s4_" + n) for n in ("gate", "xc", "xt", "xts", "d", "ex", "hf", "relu", "of", "ofr", "om", "acc",
                                          "ysq", "t", "rs", "out")}

        def pv_bank(odd, n):
            return obank[:, n, :] if odd else bank[n][:, :]

        def group(stream, j):
            return stream[:, 2 * j:2 * j + 2, :].rearrange("p b t -> p (b t)")

        block = ctx.enter_context(nc.Block())

        @block.sync
        def _(sp):
            sp.dma_start(cst[:, 0:EARLY], a["consts"][:, 0:EARLY]).then_inc(ld_const, 16)
            sp.dma_start(xin[:, :, :], a["L0_attn_x"].rearrange("b (i p) m -> p (b i) m", p=P)).then_inc(ld_x, 16)
            sp.dma_start(w1raw[:, 0:3, :], a["L0_attn_w_qkv"].rearrange("(c p) m -> p c m", p=P)).then_inc(ld_s1, 16)
            sp.dma_start(w1raw[:, 3, :], a["L0_attn_w_out"]).then_inc(ld_s1, 16)
            sp.dma_start(bout[:, :], a["L0_attn_b_out"].rearrange("(p o) -> p o", o=1)).then_inc(ld_s1, 16)
            for col, name in enumerate(("L0_attn_norm_g", "L0_attn_norm_b")):
                per_head = a[name].rearrange("o h c d -> h (o c d)")
                sp.dma_start(nrm[:, col:col + 1], bass.AP(per_head.tensor, 0, [[1, H], [0, HD], [1, 1]])).then_inc(ld_s1, 16)
            sp.dma_start(relv[:, :], a["L1_attn_rel_emb"]).then_inc(ld_const, 16)
            sp.dma_start(work[:, 2], a["window_masks"].rearrange("p (r n) -> p r n", r=2)).then_inc(ld_tables, 16)
            sp.dma_start(cst[:, EARLY:], a["consts"][:, EARLY:]).then_inc(ld_tables, 16)
            for k, name in enumerate(("L0_ffn_q_scale", "L0_ffn_k_scale")):
                sp.dma_start(scales[:, k, :, :].rearrange("p l d -> p (l d)"),
                             a[name].rearrange("l d -> (l d)").partition_broadcast(P)).then_inc(ld_vec, 16)

            def load_q(l):
                sp.dma_start(wqk[:, 0:H * DH], a["L0_ffn_Wqkv"][l, :, 0:H * DH]).then_inc(ld_q, 16)

            def load_k(l):
                sp.dma_start(wqk[:, H * DH:2 * H * DH], a["L0_ffn_Wqkv"][l, :, H * DH:2 * H * DH]).then_inc(ld_k, 16)

            def load_v(l):
                sp.dma_start(wv[:, :], a["L0_ffn_Wqkv"][l, :, 2 * H * DH:3 * H * DH]).then_inc(ld_v, 16)

            def load_o(l):
                sp.dma_start(wo[:, :, :], a["L0_ffn_Wo"][l].rearrange("(c p) n -> p c n", p=P)).then_inc(ld_o, 16)

            def load_w1(l):
                sp.dma_start(w1[:, :], a["L0_ffn_W1"][l]).then_inc(ld_w1, 16)

            def load_w2(l):
                sp.dma_start(w2[:, 0:2, :], a["L0_ffn_W2"][l, 0:2 * P, :].rearrange("(c p) n -> p c n", p=P)).then_inc(ld_w2, 16)
                sp.dma_start(w2[0:FFR, 2, :], a["L0_ffn_W2"][l, 2 * P:FF, :]).then_inc(ld_w2, 16)

            load_q(0)
            load_k(0)
            load_v(0)
            sp.wait_ge(cleared, 1)
            load_o(0)
            load_w1(0)
            load_w2(0)
            for t, name in ((lng, "L0_ffn_ln_g"), (lnb, "L0_ffn_ln_b"), (b2c, "L0_ffn_b2")):
                sp.dma_start(t[:, :], a[name].rearrange("l p -> p l"), allow_slow_non_contiguous=True).then_inc(ld_vec, 16)
            for half, t in ((0, b1a), (1, b1g)):
                for c in range(3):
                    n = P if c < 2 else FFR
                    lo = half * FF + c * P
                    sp.dma_start(t[0:n, c, :], a["L0_ffn_b1"][:, lo:lo + n].rearrange("l p -> p l"), allow_slow_non_contiguous=True).then_inc(ld_vec, 16)
            sp.wait_ge(s3["ub"], 1)
            sp.dma_start(relu_dram.ap(), uh[:, :]).then_inc(stored, 16)
            sp.wait_ge(stored, 16)
            sp.dma_start(gw[:, :], a["L1_ffn_gate_w"]).then_inc(ld_gate, 16)
            sp.dma_start(gb[:, :], a["L1_ffn_gate_b"].partition_broadcast(P)).then_inc(ld_gate, 16)
            sp.dma_start(mb1[:, :, :], a["L1_ffn_b1"].rearrange("e (c p) -> p e c", p=P), allow_slow_non_contiguous=True).then_inc(ld_gate, 16)
            sp.dma_start(mb2[:, :, :].rearrange("p e n -> p (e n)"),
                         a["L1_ffn_b2"].rearrange("e n -> (e n)").partition_broadcast(P)).then_inc(ld_gate, 16)
            with sp.Fori(1, DEPTH) as l:
                sp.wait_ge(p_full, l * (8 * B) - 2)
                load_q(l)
                sp.wait_ge(p_full, l * (8 * B))
                load_k(l)
                sp.wait_ge(v_full, l * (4 * B))
                load_v(l)
                sp.wait_ge(po_full, l * B)
                load_o(l)
                sp.wait_ge(hd_full, l * (3 * B))
                load_w1(l)
                sp.wait_ge(ct_full, l * B)
                load_w2(l)
            sp.wait_ge(p_full, 8 * ITEMS)
            for k, name in ((0, "L1_attn_Wq"), (2, "L1_attn_Wk"), (4, "L1_attn_Wv")):
                sp.dma_start(s3w[:, k * P:k * P + P], a[name]).then_inc(ld_s3, 16)
            sp.wait_ge(cleared, 2)
            src = a["L1_attn_Wo"].rearrange("(g j d) n -> j d g n", g=4, j=4)
            for j in range(4):
                sp.dma_start(s3wo[WIN * j:WIN * j + HD, :, :], src[j]).then_inc(ld_s3, 16)
            sp.wait_ge(o_full, 4 * ITEMS)
            sp.dma_start(bias, bass.AP(relu_dram.ap().tensor, 0, [[1, P], [384, H], [1, S]])).then_inc(rel_in, 16)
            sp.dma_start(mw1, a["L1_ffn_w1"].rearrange("e m f -> m e f")).then_inc(ld_s4, 16)
            for e in range(NE):
                sp.dma_start(mw2[:, e], a["L1_ffn_w2"][e].rearrange("(c p) n -> p c n", p=P)).then_inc(ld_s4, 16)
            outv = out.rearrange("(g b) (i p) m -> g p (b i) m", b=2, p=P)
            with sp.Fori(0, B // 2) as g:
                sp.wait_ge(s4["out"], g + 1)
                sp.dma_start(outv[g], outs.rearrange("p (i m) -> p i m", i=4)).then_inc(stored, 16)
            sp.wait_ge(stored, 16 + 16 * (B // 2))

        @block.tensor
        def _(pe):
            def ln_mean_pe(src, w, u, b=lnbank):
                wait(pe, ln_done, u)
                nc.tensor.matmul(b[:, 0:w], onesm, src, start=True, stop=True).then_inc(ln_mean, 1)

            def ln_var_pe(w, u, b=lnbank):
                pe.wait_ge(ln_sq, u + 1)
                for i in range(w // P):
                    mm = nc.tensor.matmul(b[:, 2 * i:2 * i + 2], lnsq[:, i * P:i * P + P], onesm[:, 0:2], start=True, stop=True)
                mm.then_inc(ln_var, 1)

            def ln_wide_pe(w, u, b=lnbank):
                pe.wait_ge(ln_rstd, u + 1)
                for i in range(w // P):
                    mm = nc.tensor.matmul(b[:, i * P:i * P + P], lnr[:, i:i + 1].broadcast_to([P, P]), ident,
                                          start=True, stop=True)
                mm.then_inc(ln_wide, 1)

            pe.wait_ge(ld_const, 32)
            pe.wait_ge(ld_s1, 80)
            for c in range(4):
                mm = nc.tensor.transpose(bank[1][:, c * P:c * P + P], w1raw[:, c, :], ident)
            mm.then_inc(s1["wt"], 1)
            nc.tensor.matmul(bank[2][0:H, 0:384], relv[:, :], const("onehot")[0:WIN, :], start=True, stop=True).then_inc(s3["u"], 1)
            pe.wait_ge(ld_x, 16)
            pe.wait_ge(s1["wts"], 1)
            pe.wait_ge(s3["ub"], 1)
            def norm_units(j, slot):
                if 0 < j and slot == 0:
                    pe.wait_ge(s1["ys"], j)
                    ln_mean_pe(s1y, 512, unit_b(j - 1))
                if 0 < j and slot in (1, 4):
                    ln_var_pe(512, unit_b(j - 1) + slot // 4)
                if 0 < j and slot in (2, 5):
                    ln_wide_pe(512, unit_b(j - 1) + slot // 5)
                if 0 < j and slot == 3:
                    pe.wait_ge(s1["x1"], j)
                    ln_mean_pe(group(X, j - 1), 512, unit_b(j - 1) + 1)
                if j + 1 < B // 2:
                    if slot == 6:
                        wait(pe, s1["sb"], j + 1)
                        for i in range(4):
                            mm = nc.tensor.transpose(bank[0][:, i * P:i * P + P], xin[:, 4 * (j + 1) + i, :], ident)
                        mm.then_inc(s1["xt"], 1)
                        pe.wait_ge(s1["x"], j + 2)
                        ln_mean_pe(group(X, j + 1), 512, unit_a(j + 1))
                    if slot == 7:
                        ln_var_pe(512, unit_a(j + 1))
                    if slot == 8:
                        ln_wide_pe(512, unit_a(j + 1))

            def attend1(j, slot):
                if slot == 0:
                    pe.wait_ge(ln_done, unit_a(j) + 1)
                    nc.tensor.matmul(bank[0][:, :], w1t[:, 0:P], s1xn, start=True, stop=True)
                    for i in range(4):
                        mm = nc.tensor.matmul(bank[1 + i // 2][:, (i % 2) * 256:(i % 2) * 256 + 256], s1xn[:, i * P:i * P + P],
                                              w1t[:, P:3 * P], start=True, stop=True)
                    mm.then_inc(s1["qkv"], 1)
                if slot == 1:
                    pe.wait_ge(s1["sb"], j + 1)
                    for bb in range(2):
                        for i in range(2):
                            nc.tensor.matmul(bank[3][:, bb * 256:bb * 256 + 256], s1kv[:, 2 * bb + i, 0:P], s1kv[:, 2 * bb + i, :],
                                             start=(i == 0), stop=(i == 1))
                    for bb in range(2):
                        for i in range(2):
                            mm = nc.tensor.matmul(bank[4][:, 2 * bb:2 * bb + 2], s1kv[:, 2 * bb + i, P:2 * P], const("ones")[:, 0:2],
                                                  start=(i == 0), stop=(i == 1))
                    mm.then_inc(s1["g"], 1)
                if slot == 2:
                    pe.wait_ge(s1["bd"], j + 1)
                    for bb in range(2):
                        mm = nc.tensor.matmul(obank[:, 0, bb * 256:bb * 256 + 256], s1bd[:, 2 * bb, :], s1q[:, bb * 256:bb * 256 + 256],
                                              start=True, stop=True)
                    mm.then_inc(s1["u"], 1)
                if slot == 3:
                    pe.wait_ge(s1["pr"], j + 1)
                    nc.tensor.matmul(obank[:, 1, :], blk, s1pr, start=True, stop=True).then_inc(s1["n2"], 1)
                if slot == 5:
                    pe.wait_ge(s1["qg"], j + 1)
                    for bb in range(2):
                        mm = nc.tensor.matmul(obank[:, 0, bb * 256:bb * 256 + 256], s1bd[:, 2 * bb + 1, :],
                                              s1qg[:, bb * 256:bb * 256 + 256], start=True, stop=True)
                    mm.then_inc(s1["o"], 1)
                if slot == 7:
                    pe.wait_ge(s1["os"], j + 1)
                    nc.tensor.matmul(obank[:, 1, :], w1t[:, 3 * P:4 * P], s1o, start=True, stop=True).then_inc(s1["y"], 1)

            for slot in range(6, 9):
                norm_units(-1, slot)
            for j in range(B // 2 + 1):
                for slot in range(9):
                    if j < B // 2:
                        attend1(j, slot)
                    norm_units(j, slot)

            def projection(t, s, odd):
                r, kind, half = s // 4, (s // 2) % 2, s % 2
                if s == 0:
                    pe.wait_ge(xs_ready, t + 1)
                    pe.wait_ge(ld_q, (t // B) * 16 + 16)
                if s == 2:
                    pe.wait_ge(ld_k, (t // B) * 16 + 16)
                wait(pe, t_done, 8 * t + s - 2)
                if isinstance(t, int) and (t, s) == (0, 2):
                    pe.wait_ge(raw_done, 1)
                lo = kind * H * DH + half * 512
                nc.tensor.matmul(bank[s % 2][:, :], xs[:, odd, WIN + r * P:WIN + r * P + P], wqk[:, lo:lo + 512],
                                 start=True, stop=True).then_inc(p_full, 1)

            def turn(i, c, s, last=False):
                pe.wait_ge(rot_done, 8 * i + c + 1)
                if last:
                    pe.wait_ge(t_done, 8 * i + c - 1)
                else:
                    pe.wait_ge(raw_done, 8 * i + c + 2)
                for q in range(4):
                    mm = nc.tensor.transpose(bank[(s + 1) % 2][:, q * P:q * P + P], rot[:, c, q * P:q * P + P], ident)
                mm.then_inc(t_full, 1)

            def values(i, w, odd):
                if w == 0:
                    pe.wait_ge(ld_v, (i // B) * 16 + 16)
                wait(pe, v_done, 8 * i + 2 * w)
                for o in range(2):
                    mm = nc.tensor.matmul(vbank[64 * o:64 * o + 64, :], xs[:, odd, (2 * w + 1) * WIN:(2 * w + 3) * WIN],
                                          wv[:, :].rearrange("p (a o d) -> p o a d", o=2, d=DH)[:, o],
                                          start=True, stop=True)
                mm.then_inc(v_full, 1)

            def scores(i, k, *free):
                r, g = k // 2, k % 2
                if g == 0:
                    pe.wait_ge(t_done, 8 * i + 4 * r + 4)
                for bank_free, count in free:
                    wait(pe, bank_free, count)
                s = bank[SC_BANK[k]]
                nc.tensor.matmul(s[:, :], ident_bf, maskv[:, r, :], start=True, stop=False, skip_group_check=True)
                for q in range(4):
                    for w in range(4):
                        lo = r * P + w * WIN
                        mm = nc.tensor.matmul(s[WIN * w:WIN * w + WIN, q * P:q * P + P], qT[:, 4 * g + q, lo:lo + WIN],
                                              kT[:, 4 * g + q, :, lo:lo + 2 * WIN], start=False, stop=True,
                                              skip_group_check=True)
                mm.then_inc(sc_full, 1)

            def turn_probs(i, k):
                pe.wait_ge(px_done, 4 * i + k + 1)
                wait(pe, pt_done, 8 * i + PT_PROBS[k])
                for q in range(4):
                    mm = nc.tensor.transpose(bank[4][:, q * P:q * P + P], px[:, k % 2, q * P:q * P + P], ident)
                mm.then_inc(pt_full, 1)

            def weigh(i, k):
                r, g = k // 2, k % 2
                pe.wait_ge(pt_done, 8 * i + PT_PROBS[k] + 1)
                if g == 0:
                    pe.wait_ge(v_done, 8 * i + 4 * r + 4)
                wait(pe, ao_done, 4 * i + k)
                for w in range(4):
                    for q in range(4):
                        mm = nc.tensor.matmul(obank[WIN * w:WIN * w + WIN, q // 2, (q % 2) * VB:(q % 2) * VB + VB],
                                              pT[:, k % 2, q * P + w * WIN:q * P + w * WIN + WIN],
                                              vp[:, 4 * r + w, 4 * g + q, :], start=True, stop=True)
                mm.then_inc(o_full, 1)

            def turn_out(i, k):
                pe.wait_ge(ao_done, 4 * i + k + 1)
                pe.wait_ge(pt_done, 8 * i + PT_OUT[k])
                for q in range(4):
                    mm = nc.tensor.transpose(bank[4][:, q * P:q * P + P], ao[:, k % 2, q * P:q * P + P], ident)
                mm.then_inc(pt_full, 1)

            def project_out(i, part, next_scores):
                if part == 0:
                    pe.wait_ge(pt_done, 8 * i + 8)
                    pe.wait_ge(ld_o, (i // B) * 16 + 16)
                    if next_scores:
                        pe.wait_ge(sh_done, 4 * i + 6)
                for c in range(4 * part, 4 * part + 4):
                    mm = nc.tensor.matmul(bank[2][:, 0:S], wo[:, c, :], aoT[:, c, :], start=(c == 0), stop=(c == PAIRS - 1))
                if part == 1:
                    mm.then_inc(po_full, 1)

            def hidden(i, c, next_scores):
                if c == 0:
                    pe.wait_ge(ffn_in, i + 1)
                    pe.wait_ge(ld_w1, (i // B) * 16 + 16)
                if c == 2:
                    pe.wait_ge(h_done, 3 * i + 1)
                elif next_scores:
                    pe.wait_ge(sh_done, 4 * i + 7 + c)
                elif c == 1:
                    pe.wait_ge(z_ready, B + i)
                n = P if c < 2 else FFR
                for half in range(2):
                    mm = nc.tensor.matmul(bank[2 + c % 2][0:n, half * S:half * S + S], w1[:, half * FF + c * P:half * FF + c * P + n],
                                          lnt[:, S:2 * S], start=True, stop=True)
                mm.then_inc(hd_full, 1)

            def contract(i, next_scores):
                pe.wait_ge(h_done, 3 * i + 3)
                pe.wait_ge(ld_w2, (i // B) * 32 + 32)
                if next_scores:
                    pe.wait_ge(sh_done, 4 * i + 9)
                for c in range(3):
                    mm = nc.tensor.matmul(bank[3][:, 0:S], w2[:, c, :], hT[:, c, :], start=(c == 0), stop=(c == 2))
                mm.then_inc(ct_full, 1)

            def step(t, odd, p0, p1, p2, p3=True):
                i, f = t - 1, t - 2
                for s in range(8):
                    if p0:
                        projection(t, s, odd)
                    if s in (4, 5, 6) and p2:
                        hidden(f, s - 4, p1)
                    if s == 1 and p2:
                        pe.wait_ge(xf_ready, f + 1)
                        pe.wait_ge(z_ready, B + f)
                        ln_mean_pe(xf[:, :], S, LN_S2 + f, bank[3])
                    if s == 0 and p2:
                        project_out(f, 1, p1)
                    if s == 2 and p1:
                        scores(i, 2, (sh_done, 4 * i + 2), (z1_done, i))
                    if s == 6 and p0:
                        scores(t, 0, (sh_done, 4 * t), *([(h_done, 3 * f + 2)] if p2 else []))
                    if s == 7 and p0:
                        scores(t, 1, (sh_done, 4 * t - 1), *([(h_done, 3 * f + 3)] if p2 else []))
                    if s >= 2 and p0:
                        turn(t, s - 2, s)
                    if s < 2 and p1:
                        turn(i, s + 6, s, s == 1 and not p0)
                    if s == 3 and p1:
                        scores(i, 3, (ln_done, LN_S2 + i) if p2 else (sh_done, 4 * i + 1))
                    if s == 5 and p0:
                        values(t, 1, odd)
                    if s in (0, 1, 4, 5) and p1:
                        weigh(i, (0, 1, 0, 0, 2, 3)[s])
                    if s in (0, 3, 4) and p1:
                        turn_probs(i, (1, 0, 0, 2, 3)[s])
                    if s in (1, 2, 5, 6) and p1:
                        turn_out(i, (0, 0, 1, 0, 0, 2, 3)[s])
                    if s == 1 and p2:
                        ln_var_pe(S, LN_S2 + f, bank[3])
                    if s == 7 and p2:
                        contract(f, p0)
                    if s in (3, 7) and p0:
                        values(t, s // 2 - 1, odd)
                    if s == 1 and p1:
                        values(i, 3, 1 - odd)
                    if s == 2 and p2:
                        ln_wide_pe(S, LN_S2 + f, bank[3])
                    if s == 7 and p0:
                        turn_probs(t, 0)
                    if s == 7 and p1:
                        project_out(i, 0, p0)

            pe.wait_ge(masks_cast, 1)
            step(0, 0, True, False, False, False)
            step(1, 1, True, True, False, False)
            step(2, 0, True, True, True, False)
            step(3, 1, True, True, True)
            with pe.Fori(4, ITEMS - 1, 2) as t:
                step(t, 0, True, True, True)
                step(t + 1, 1, True, True, True)
            step(ITEMS, 0, False, True, True)
            step(ITEMS + 1, 1, False, False, True)

            def project3(b, k, u):
                wait(pe, s3["part"], 2 * b + k)
                if k == 0:
                    pe.wait_ge(ln_done, u + 2)
                if k < 2:
                    for n in range(2):
                        mm = nc.tensor.matmul(lnbank[:, n * S:n * S + S], s3w[:, (2 * k + n) * P:(2 * k + n) * P + P], s3xn,
                                              start=True, stop=True)
                else:
                    for n in range(2):
                        mm = nc.tensor.matmul(lnbank[:, n * P:n * P + P], s3xn[:, n * P:n * P + P], s3w[:, 4 * P:5 * P],
                                              start=True, stop=True)
                mm.then_inc(s3["proj"], 1)

            def out3(b):
                pe.wait_ge(s3["ot"], 2 * b + 2)
                for g in range(4):
                    mm = nc.tensor.matmul(lnbank[:, 0:S], s3wo[:, g, :], s3ot[:, g, :], start=(g == 0), stop=(g == 3))
                mm.then_inc(s3["y"], 1)

            def prepare(b, slot, u):
                if slot == 0:
                    pe.wait_ge(z_ready, b + (ITEMS + 1))
                    wait(pe, s3["v"], b)
                    ln_mean_pe(Z[:, b, :], S, u)
                if slot in (1, 4):
                    ln_var_pe(S, u + slot // 4)
                if slot in (2, 5):
                    ln_wide_pe(S, u + slot // 5)
                if slot == 3:
                    pe.wait_ge(x2_ready, b + 1)
                    ln_mean_pe(X[:, b, :], S, u + 1)
                if slot in (6, 7, 8):
                    project3(b, slot - 6, u)

            def finish(b, slot, u, after_v):
                if slot == 9:
                    pe.wait_ge(s3["v"], b + 3 if after_v else B)
                    pe.wait_ge(ln_done, u)
                    out3(b)
                if slot == 10:
                    pe.wait_ge(s3["ys"], b + 1)
                    ln_mean_pe(s3y, S, u)
                if slot == 11:
                    ln_var_pe(S, u)
                if slot == 12:
                    ln_wide_pe(S, u)

            def attend(b, odd, m):
                if m < NJ:
                    r, heads = JOBS[m]
                    w = P * (r + 1)
                    if m == 0:
                        pe.wait_ge(s3["qk"], 2 * b + 2)
                    if m in (0, 6):
                        pe.wait_ge(s3["qm"], 2 * b + 1 + m // 6)
                    wait(pe, s3["add"], NJ * b + m - 1)
                    for n, h in enumerate(heads):
                        mm = nc.tensor.matmul(bank[3 + m % 2][:, n * w:n * w + w], qm[:, h, r * P:r * P + P],
                                              s3k[odd][:, 0:w], start=True, stop=True)
                    mm.then_inc(s3["full"], 1)
                if 2 <= m <= NJ + 1:
                    n = m - 2
                    pe.wait_ge(s3["pn"], NJ * b + n + 1)
                    wait(pe, s3["pts"], NJ * b + n)
                    for q in range(4):
                        mm = nc.tensor.transpose(bank[2][:, q * P:q * P + P], px[:, n % 2, q * P:q * P + P], ident)
                    mm.then_inc(s3["ptf"], 1)
                if m >= 3:
                    n = m - 3
                    r, heads = JOBS[n]
                    pe.wait_ge(s3["pts"], NJ * b + n + 1)
                    if n == 0:
                        pe.wait_ge(s3["v"], b + 1)
                        wait(pe, s3["ot"], 2 * b - 2)
                    for y, h in enumerate(heads):
                        g, row = h // 4, WIN * (h % 4)
                        lo = (g % 2) * S + r * P
                        for kb in range(r + 1):
                            q = y * (r + 1) + kb
                            mm = nc.tensor.matmul(pv_bank(odd, g // 2)[row:row + WIN, lo:lo + P], vs[:, odd, kb, h, :],
                                                  pT[:, n % 2, q * P:q * P + P], start=(kb == 0), stop=(kb == r))
                    mm.then_inc(s3["pv"], 1)

            def step3(b, odd, next_batch, batch_before):
                u = 3 * b + (LN_S3 + 1)
                for m in range(NJ + 3):
                    attend(b, odd, m)
                    if next_batch:
                        prepare(b + 1, m, u if batch_before else LN_S3 + 2)
                    if batch_before:
                        finish(b - 1, m, u + 2 if next_batch else u, next_batch)

            pe.wait_ge(ld_s3, 16 * 7)
            pe.wait_ge(s3["w"], 1)
            for slot in range(9):
                prepare(0, slot, LN_S3)
            step3(0, 0, True, False)
            with pe.Fori(1, B - 2, 2) as b:
                step3(b, 1, True, True)
                step3(b + 1, 0, True, True)
            step3(B - 1, 1, False, True)
            for slot in range(9, 13):
                finish(B - 1, slot, LN_S4 - 1, False)

            pe.wait_ge(ld_gate, 64)
            pe.wait_ge(ld_s4, 16 * (NE + 1))
            pe.wait_ge(x3_ready, B)
            def norm_input(g, slot):
                if g < B // 2:
                    if slot == 1:
                        ln_mean_pe(group(X, g), 512, g + LN_S4)
                    if slot == 2:
                        ln_var_pe(512, g + LN_S4)
                    if slot == 3:
                        ln_wide_pe(512, g + LN_S4)

            def up(g, e, c):
                n = 4 * e + c
                wait(pe, s4["relu"], 4 * NE * g + n - 1)
                nc.tensor.matmul(bank[2 + n % 2][:, :], mw1[:, e, c * P:c * P + P], s4xn[g % 2], start=True,
                                 stop=True).then_inc(s4["hf"], 1)

            def down(g, e):
                pe.wait_ge(s4["relu"], 4 * NE * g + 4 * e + 4)
                wait(pe, s4["ofr"], NE * g + e - 1)
                ob = (bank[4][:, :], obank[:, 0, :])[e % 2]
                for i in range(4):
                    for c in range(4):
                        mm = nc.tensor.matmul(ob[:, i * P:i * P + P], h1[:, e % 2, c, i * P:i * P + P], mw2[:, e, c, :],
                                              start=(c == 0), stop=(c == 3))
                mm.then_inc(s4["of"], 1)

            for slot in range(1, 4):
                norm_input(0, slot)
            for g in range(B // 2):
                pe.wait_ge(ln_done, g + (LN_S4 + 1))
                for i in range(4):
                    mm = nc.tensor.matmul(bank[0][:, NE * i:NE * i + NE], s4xn[g % 2][:, i * P:i * P + P], gw[:, :],
                                          start=True, stop=True)
                mm.then_inc(s4["gate"], 1)
                pe.wait_ge(s4["xc"], g + 1)
                for i in range(4):
                    mm = nc.tensor.transpose(bank[1][:, i * P:i * P + P], s4x[:, i * P:i * P + P], ident)
                mm.then_inc(s4["xt"], 1)
                for e in range(NE + 1):
                    if e < NE:
                        for c in range(4):
                            up(g, e, c)
                    if e >= 1:
                        down(g, e - 1)
                    norm_input(g + 1, e)

        @block.scalar
        def _(act):
            def ln_sq_act(w, u):
                act.wait_ge(ln_d, u + 1)
                nc.scalar.activation(lnsq[:, 0:w], lnd[:, 0:w], ACT.Square).then_inc(ln_sq, 1)

            act.wait_ge(ld_const, 32)
            act.wait_ge(s1["wt"], 1)
            nc.scalar.copy(w1t, bank[1][:, :]).then_inc(s1["wts"], 1)
            act.wait_ge(ld_s1, 80)
            def norm_units(j, slot):
                if 0 < j and slot in (0, 3):
                    ln_sq_act(512, unit_b(j - 1) + slot // 3)
                if j + 1 < B // 2 and slot == 6:
                    act.wait_ge(s1["xt"], j + 2)
                    nc.scalar.copy(group(X, j + 1), bank[0][:, :]).then_inc(s1["x"], 1)
                    ln_sq_act(512, unit_a(j + 1))

            def attend1(j, slot):
                if slot == 0:
                    act.wait_ge(s1["qkv"], j + 1)
                    nc.scalar.copy(s1q, bank[0][:, :])
                    for i in range(2):
                        last = nc.scalar.copy(s1kv[:, 2 * i:2 * i + 2, :].rearrange("p i n -> p (i n)"), bank[1 + i][:, :])
                    last.then_inc(s1["sb"], 1)
                if slot == 4:
                    act.wait_ge(s1["n2m"], j + 1)
                    nc.scalar.activation(s1nr, s1n2, ACT.Sqrt).then_inc(s1["nr"], 1)
                if slot == 5:
                    act.wait_ge(s1["o"], j + 1)
                    for bb in range(2):
                        last = nc.scalar.activation(s1o[:, bb * 256:bb * 256 + 256], obank[:, 0, bb * 256:bb * 256 + 256],
                                                    ACT.Identity, bias=s1bv[:, bb:bb + 1], scale=nrm[:, 0:1])
                    last.then_inc(s1["os"], 1)
                if slot == 8:
                    act.wait_ge(s1["y"], j + 1)
                    nc.scalar.activation(s1y, obank[:, 1, :], ACT.Identity, bias=bout[:, :]).then_inc(s1["ys"], 1)

            for slot in range(6, 9):
                norm_units(-1, slot)
            for j in range(B // 2 + 1):
                for slot in range(9):
                    if j < B // 2:
                        attend1(j, slot)
                    norm_units(j, slot)

            def take_xs(t, buf):
                act.wait_ge(z_ready, t + 1)
                wait(act, v_full, 4 * t - 4)
                nc.scalar.copy(buf[0:64, WIN:KW], Z[0:64, t % B, :])
                nc.scalar.copy(buf[64:P, WIN + 1:KW], Z[64:P, t % B, 0:S - 1]).then_inc(xs_ready, 1)

            def take_raw(t, s):
                act.wait_ge(p_full, 8 * t + s + 1)
                wait(act, n2_raw, 8 * t + s - 1)
                nc.scalar.activation(sq[:, s % 2, :], bank[s % 2][:, :], ACT.Square).then_inc(sq_done, 1)
                wait(act, t_full, 8 * t + s - 7)
                nc.scalar.copy(rot[:, s, :], bank[s % 2][:, :]).then_inc(raw_done, 1)

            def take_values(i, j, odd):
                act.wait_ge(v_full, 4 * i + j + 1)
                if j < 2:
                    wait(act, o_full, 4 * i - 2 + 2 * j)
                src = vbank[64 * odd:64 * odd + 64, :].rearrange("p (a d) -> p a d", d=DH)
                cols = slice(odd * (DH + 1), odd * (DH + 1) + DH)
                lo = 64 * odd
                nc.scalar.copy(vp[lo:lo + 64, 2 * j + 1, :, cols], src)
                last = nc.scalar.copy(vp[lo + 32:lo + 64, 2 * j, :, cols], src[0:32])
                if j < 3:
                    last = nc.scalar.copy(vp[lo:lo + 32, 2 * j + 2, :, cols], src[32:64])
                last.then_inc(v_done, 1)

            def take_turned(i, c, s):
                r, kind, half = c // 4, (c // 2) % 2, c % 2
                act.wait_ge(t_full, 8 * i + c + 1)
                if c in (0, 2):
                    wait(act, sc_full, 4 * i - 2 + c)
                src = bank[(s + 1) % 2][:, :].rearrange("p (a n) -> p a n", a=4)
                pairs = slice(4 * half, 4 * half + 4)
                if kind == 0:
                    last = nc.scalar.copy(qT[:, pairs, r * P:r * P + P], src)
                else:
                    lo = WIN + r * P
                    nc.scalar.copy(kT[0:64, pairs, 0, lo:lo + P], src[0:64])
                    last = nc.scalar.copy(kT[64:P, pairs, 1, lo:lo + P], src[64:P])
                last.then_inc(t_done, 1)

            def exps(i, k):
                act.wait_ge(sh_done, 4 * i + k + 1)
                wait(act, pt_full, 8 * i + (PT_PROBS[k - 2] + 1 if k >= 2 else PT_PROBS[k + 2] - 7))
                nc.scalar.activation(px[:, k % 2, :], sh[:, k % 2, :], ACT.Exp).then_inc(px_done, 1)

            def take_probs(i, k):
                act.wait_ge(pt_full, 8 * i + PT_PROBS[k] + 1)
                wait(act, o_full, 4 * i + k - 1)
                nc.scalar.copy(pT[:, k % 2, :], bank[4][:, :]).then_inc(pt_done, 1)

            def take_out(i, k):
                r, g = k // 2, k % 2
                act.wait_ge(pt_full, 8 * i + PT_OUT[k] + 1)
                if k == 0:
                    wait(act, po_full, i)
                nc.scalar.copy(aoT[:, 4 * g:4 * g + 4, r * P:r * P + P],
                               bank[4][:, :].rearrange("p (a n) -> p a n", a=4)).then_inc(pt_done, 1)

            def gelu(i, c):
                n = P if c < 2 else FFR
                act.wait_ge(hd_full, 3 * i + c + 1)
                nc.scalar.activation(ge[0:n, c, :], bank[2 + c % 2][0:n, S:2 * S], ACT.Gelu,
                                     bias=b1g[0:n, c, bass.ds(i // B, 1)]).then_inc(ge_done, 1)

            def step(t, odd, p0, p1, p2, p3=True):
                i, f = t - 1, t - 2
                for s in range(8):
                    if p0:
                        take_raw(t, s)
                    if s == 3 and p1:
                        exps(i, 2)
                    if s == 7 and p0:
                        exps(t, 0)
                    if s >= 2 and p0:
                        take_turned(t, s - 2, s)
                    if s < 2 and p1:
                        take_turned(i, s + 6, s)
                    if s in (4, 5, 6) and p2:
                        gelu(f, s - 4)
                    if s == 0 and p2:
                        act.wait_ge(z1_done, f + 1)
                        nc.scalar.copy(xf[0:64, :], Z[0:64, f % B, :])
                        nc.scalar.copy(xf[64:P, 1:S], Z[64:P, f % B, 0:S - 1]).then_inc(xf_ready, 1)
                    if s == 1 and p2:
                        ln_sq_act(S, LN_S2 + f)
                    if s in (4, 6) and p0:
                        take_values(t, s // 2 - 2, 1)
                    if s in (0, 2) and p1:
                        take_values(i, s // 2 + 2, 1)
                    if s in (0, 3, 4) and p1:
                        take_probs(i, (1, 0, 0, 2, 3)[s])
                    if s == 7 and p0:
                        take_probs(t, 0)
                    if s in (1, 2, 5, 6) and p1:
                        take_out(i, (0, 0, 1, 0, 0, 2, 3)[s])
                    if s == 3 and p1:
                        exps(i, 3)
                    if s == 7 and p0:
                        exps(t, 1)
                    if s in (3, 5, 7) and p0:
                        take_values(t, s // 2 - 1, 0)
                    if s == 1 and p1:
                        take_values(i, 3, 0)
                    if s == 6 and p0:
                        take_xs(t + 1, xs[:, 1 - odd])

            act.wait_ge(cleared, 1)
            act.wait_ge(ld_vec, 16 * 11)
            take_xs(0, xs[:, 0])
            step(0, 0, True, False, False, False)
            step(1, 1, True, True, False, False)
            step(2, 0, True, True, True, False)
            step(3, 1, True, True, True)
            with act.Fori(4, ITEMS - 1, 2) as t:
                step(t, 0, True, True, True)
                step(t + 1, 1, True, True, True)
            step(ITEMS, 0, False, True, True)
            step(ITEMS + 1, 1, False, False, True)

            def prepare(b, odd, slot, u):
                if slot in (0, 3):
                    ln_sq_act(S, u + slot // 3)
                if slot == 8:
                    act.wait_ge(s3["proj"], 3 * b + 3)
                    wait(act, s3["pv"], NJ * b - NJ)
                    nc.scalar.copy(vs[:, odd, :, :, 0:HD], lnbank[:, 0:2 * P].rearrange("p (i h d) -> p i h d", i=2, h=H))\
                        .then_inc(s3["v"], 1)

            def finish(b, slot, u):
                if slot == 9:
                    act.wait_ge(s3["y"], b + 1)
                    nc.scalar.copy(s3y, lnbank[:, 0:S]).then_inc(s3["ys"], 1)
                if slot == 10:
                    ln_sq_act(S, u)

            def attend(b, m):
                if 2 <= m <= NJ + 1:
                    act.wait_ge(s3["ptf"], NJ * b + m - 1)
                    wait(act, s3["pv"], NJ * b + m - 3)
                    nc.scalar.copy(pT[:, m % 2, :], bank[2][:, :]).then_inc(s3["pts"], 1)
                if m < NJ:
                    r, heads = JOBS[m]
                    w = P * (r + 1)
                    act.wait_ge(s3["mx"], NJ * b + m + 1)
                    wait(act, s3["ptf"], NJ * b + m - 1)
                    for n in range(len(heads)):
                        last = nc.scalar.activation(px[:, m % 2, n * w:n * w + w], sh[:, m % 2, n * w:n * w + w], ACT.Exp,
                                                    bias=mx[:, m % 2, n:n + 1], accum_out=dn[:, m % 2, n:n + 1])
                    last.then_inc(s3["px"], 1)

            def take_out3(b, odd, n):
                act.wait_ge(s3["pv"], NJ * b + 6 * n + 6)
                wait(act, s3["y"], b)
                nc.scalar.copy(aoTf[:, 512 * n:512 * n + 512].rearrange("p (c t) -> p c t", c=4),
                               pv_bank(odd, n).rearrange("p (c t) -> p c t", c=4)[:, :, ::-1]).then_inc(s3["ot"], 1)

            def step3(b, odd, next_batch, batch_before):
                u = 3 * b + (LN_S3 + 1)
                for m in range(NJ + 3):
                    attend(b, m)
                    if next_batch:
                        prepare(b + 1, 1 - odd, m, u if batch_before else LN_S3 + 2)
                    if batch_before:
                        finish(b - 1, m, u + 2 if next_batch else u)
                    if m in (10, 14):
                        take_out3(b, odd, m // 14)

            act.wait_ge(s3["w"], 1)
            for slot in range(9):
                prepare(0, 0, slot, LN_S3)
            step3(0, 0, True, False)
            with act.Fori(1, B - 2, 2) as b:
                step3(b, 1, True, True)
                step3(b + 1, 0, True, True)
            step3(B - 1, 1, False, True)
            for slot in range(9, 13):
                finish(B - 1, slot, LN_S4 - 1)

            act.wait_ge(ld_gate, 64)
            def token_sources(g):
                if g < B // 2:
                    wait(act, s4["xt"], g)
                    nc.scalar.copy(s4x, group(X, g)).then_inc(s4["xc"], 1)

            def squares_out(g):
                act.wait_ge(s4["t"], TAIL_OPS * g + 3)
                nc.scalar.activation(ysq, yc, ACT.Square).then_inc(s4["ysq"], 1)

            act.wait_ge(x3_ready, B)
            ln_sq_act(512, LN_S4)
            token_sources(0)
            for g in range(B // 2):
                if g:
                    squares_out(g - 1)
                act.wait_ge(s4["xt"], g + 1)
                nc.scalar.copy(s4xt[g % 2], bank[1][:, :]).then_inc(s4["xts"], 1)
                act.wait_ge(s4["d"], GATE_OPS * g + 3)
                nc.scalar.activation(pe_[:, :, :], lh[:, :, :], ACT.Exp).then_inc(s4["ex"], 1)
                for n in range(4 * NE):
                    act.wait_ge(s4["hf"], 4 * NE * g + n + 1)
                    nc.scalar.activation(h1[:, (n // 4) % 2, n % 4, :], bank[2 + n % 2][:, :], ACT.Relu,
                                         bias=mb1[:, n // 4, n % 4:n % 4 + 1]).then_inc(s4["relu"], 1)
                    if n == 7 and g + 1 < B // 2:
                        ln_sq_act(512, g + 1 + LN_S4)
                    if n == 11:
                        token_sources(g + 1)
            squares_out(B // 2 - 1)

        @block.vector
        def _(dve):
            tt, red = nc.vector.tensor_tensor, nc.vector.tensor_reduce

            def ln_d_dve(src, w, u, b=lnbank):
                dve.wait_ge(ln_mean, u + 1)
                tt(lnd[:, 0:w], src, b[:, 0:w], ALU.subtract).then_inc(ln_d, 1)

            def ln_eps_dve(w, u, b=lnbank):
                dve.wait_ge(ln_var, u + 1)
                nc.vector.tensor_scalar(lnv[:, 0:w // P], b[:, 0:2 * (w // P)].rearrange("p (i o) -> p i o", o=2)[:, :, 0],
                                        1e-5, None, ALU.add).then_inc(ln_eps, 1)

            def ln_out_dve(dst, w, u, b=lnbank):
                dve.wait_ge(ln_wide, u + 1)
                tt(dst, lnd[:, 0:w], b[:, 0:w], ALU.mult).then_inc(ln_done, 1)

            nc.vector.memset(w2[:, 2, :], 0.0)
            nc.vector.memset(hT[:, 2, :], 0.0)
            nc.vector.memset(xs[:, :, :], 0.0)
            nc.vector.memset(xf[:, :], 0.0)
            nc.vector.memset(kT[:, :, :, :], 0.0).then_inc(cleared, 1)
            dve.wait_ge(ld_const, 32)
            dve.wait_ge(vp_cleared, 1)
            nc.vector.memset(vp[0:64, :, :, DH:DH + 1], 1.0)
            nc.vector.memset(vp[64:P, :, :, VB - 1:VB], 1.0)

            dve.wait_ge(ld_const, 32)
            dve.wait_ge(ld_s1, 80)
            dve.wait_ge(s3["u"], 1)
            tt(uh[:, :], bank[2][0:H, 0:384], const("neg")[0:H, :], ALU.add).then_inc(s3["ub"], 1)
            def norm_units(j, slot):
                if 0 < j:
                    x, u = group(X, j - 1), unit_b(j - 1)
                    if slot == 0:
                        ln_d_dve(s1y, 512, u)
                    if slot in (1, 4):
                        ln_eps_dve(512, u + slot // 4)
                    if slot == 2:
                        ln_out_dve(lnt[:, :], 512, u)
                        dve.wait_ge(ln_done, u + 1)
                        tt(x, x, lnt[:, :], ALU.add).then_inc(s1["x1"], 1)
                    if slot == 3:
                        dve.wait_ge(s1["x1"], j)
                        ln_d_dve(x, 512, u + 1)
                    if slot == 5:
                        ln_out_dve(group(Z, j - 1), 512, u + 1)
                if j + 1 < B // 2:
                    x, u = group(X, j + 1), unit_a(j + 1)
                    if slot == 6:
                        ln_d_dve(x, 512, u)
                    if slot == 7:
                        ln_eps_dve(512, u)
                    if slot == 8:
                        ln_out_dve(s1xn, 512, u)

            def attend1(j, slot):
                if slot == 1:
                    dve.wait_ge(s1["g"], j + 1)
                    tt(s1bd, bank[3][:, :].rearrange("p (c n) -> p c n", c=4), blk.unsqueeze(1).broadcast_to([P, 4, P]), ALU.mult)
                    nc.vector.tensor_scalar(s1bv, bank[4][:, 0:4].rearrange("p (b o) -> p b o", o=2)[:, :, 0], nrm[:, 1:2], None,
                                            ALU.mult).then_inc(s1["bd"], 1)
                if slot == 2:
                    dve.wait_ge(s1["u"], j + 1)
                    tt(s1pr, s1q, obank[:, 0, :], ALU.mult).then_inc(s1["pr"], 1)
                if slot == 3:
                    dve.wait_ge(s1["n2"], j + 1)
                    nc.vector.tensor_scalar(s1n2, obank[:, 1, :], 1e-24, None, ALU.max).then_inc(s1["n2m"], 1)
                if slot == 4:
                    dve.wait_ge(s1["nr"], j + 1)
                    nc.vector.reciprocal(s1pr, s1nr).then_inc(s1["rn"], 1)
                    dve.wait_ge(s1["rn"], j + 1)
                    tt(s1qg, s1q, s1pr, ALU.mult).then_inc(s1["qg"], 1)

            for slot in range(6, 9):
                norm_units(-1, slot)
            for j in range(B // 2 + 1):
                for slot in range(9):
                    if j < B // 2:
                        attend1(j, slot)
                    norm_units(j, slot)
            dve.wait_ge(ln_done, LN_S2)
            nc.vector.memset(n2[:, :, :], 0.0).then_inc(z_ready, B)

            dve.wait_ge(ld_tables, 32)
            nc.vector.tensor_copy(ident_bf, ident)
            nc.vector.tensor_copy(maskv, work[:, 2]).then_inc(masks_cast, 1)
            dve.wait_ge(ld_vec, 16 * 11)
            rotc = const("rot").rearrange("p (k r d) -> p k r d", k=4, r=2)
            for k in range(2):
                scale = scales[:, k, :, :]
                tt(tab[:, :, 2 * k, :, :], rotc[:, 2 * k].unsqueeze(1).broadcast_to([P, DEPTH, 2, DH]),
                   scale.unsqueeze(2).broadcast_to([P, DEPTH, 2, DH]), ALU.mult)
                for lo, other in ((0, DH // 2), (DH // 2, 0)):
                    last = tt(tab[:, :, 2 * k + 1, :, lo:lo + DH // 2],
                              rotc[:, 2 * k + 1, :, lo:lo + DH // 2].unsqueeze(1).broadcast_to([P, DEPTH, 2, DH // 2]),
                              scale[:, :, other:other + DH // 2].unsqueeze(2).broadcast_to([P, DEPTH, 2, DH // 2]), ALU.mult)
            last.then_inc(tab_done, 1)
            dve.wait_ge(tab_done, 1)

            def heads(ap):
                return ap.rearrange("p (h d) -> p h d", d=DH)

            def norms(t, c):
                dve.wait_ge(sq_done, 8 * t + c + 1)
                red(n2[:, c % 2, :], heads(sq[:, c % 2, :]), AX, ALU.add).then_inc(n2_raw, 1)
                dve.wait_ge(n2_raw, 8 * t + c + 1)
                nc.vector.tensor_scalar(n2m[:, c % 2, :], n2[:, c % 2, :], 1e-24, None, ALU.max).then_inc(n2_done, 1)

            def normalise(t, c):
                r, kind = c // 4, (c // 2) % 2
                dve.wait_ge(raw_done, 8 * t + c + 1)
                dve.wait_ge(rn_done, 8 * t + c + 1)
                tt(heads(qn[:, c % 2, :]), heads(rot[:, c, :]), rn[:, c % 2, :].unsqueeze(2).broadcast_to([P, PAIRS, DH]),
                   ALU.mult).then_inc(qn_done, 1)
                dve.wait_ge(qn_done, 8 * t + c + 1)
                cos = tab[:, bass.ds(t // B, 1), 2 * kind, r, :].broadcast_to([P, PAIRS, DH])
                tt(heads(t1[:, c % 2, :]), heads(qn[:, c % 2, :]), cos, ALU.mult).then_inc(t1_done, 1)

            def rotated(t, c):
                dve.wait_ge(t1_done, 8 * t + c + 1)
                dve.wait_ge(t2_done, 8 * t + c + 1)
                tt(rot[:, c, :], t1[:, c % 2, :], t2[:, c % 2, :], ALU.add).then_inc(rot_done, 1)

            def shift_scores(i, k):
                b = SC_BANK[k]
                dve.wait_ge(sc_full, 4 * i + k + 1)
                red(mx[:, k % 2, :], heads(bank[b][:, :]), AX, ALU.max).then_inc(mx_done, 1)
                dve.wait_ge(mx_done, 4 * i + k + 1)
                wait(dve, px_done, 4 * i + k - 1)
                tt(heads(sh[:, k % 2, :]), heads(bank[b][:, :]), mx[:, k % 2, :].unsqueeze(2).broadcast_to([P, PAIRS, DH]),
                   ALU.subtract).then_inc(sh_done, 1)

            def divide_out(i, k):
                b = k % 2
                dve.wait_ge(o_full, 4 * i + k + 1)
                o = obank[:, :, 0:2 * VB].rearrange("p c (h n) -> p c h n", n=DH + 1)
                nc.vector.reciprocal(rd[:, b, :].rearrange("p (c h) -> p c h", c=2), o[:, :, :, DH]).then_inc(rd_done, 1)
                dve.wait_ge(rd_done, 4 * i + k + 1)
                wait(dve, pt_full, 8 * i + (PT_OUT[k - 2] + 1 if k >= 2 else PT_OUT[k + 2] - 7))
                tt(ao[:, b, :].rearrange("p (c h n) -> p c h n", c=2, h=4), o[:, :, :, 0:DH],
                   rd[:, b, :].rearrange("p (c h) -> p c h", c=2).unsqueeze(3).broadcast_to([P, 2, 4, DH]),
                   ALU.mult).then_inc(ao_done, 1)

            def add_attention(i):
                dve.wait_ge(po_full, i + 1)
                z = Z[:, i % B, :]
                tt(z, z, bank[2][:, 0:S], ALU.add).then_inc(z1_done, 1)

            def scale_norm(i):
                l = bass.ds(i // B, 1)
                ln_out_dve(lnt[:, 0:S], S, LN_S2 + i, bank[3])
                dve.wait_ge(ln_done, i + (LN_S2 + 1))
                nc.vector.tensor_scalar(lnt[:, S:2 * S], lnt[:, 0:S], lng[:, l], lnb[:, l], ALU.mult, ALU.add).then_inc(ffn_in, 1)

            def gate(i, c):
                l = bass.ds(i // B, 1)
                n = P if c < 2 else FFR
                dve.wait_ge(ge_done, 3 * i + c + 1)
                nc.vector.scalar_tensor_tensor(out=hT[0:n, c, :], in0=bank[2 + c % 2][0:n, 0:S], scalar=b1a[0:n, c, l],
                                               in1=ge[0:n, c, :], op0=ALU.add, op1=ALU.mult).then_inc(h_done, 1)

            def add_feed_forward(i):
                dve.wait_ge(ct_full, i + 1)
                z = Z[:, i % B, :]
                nc.vector.scalar_tensor_tensor(out=z, in0=bank[3][:, 0:S], scalar=b2c[:, bass.ds(i // B, 1)], in1=z, op0=ALU.add,
                                               op1=ALU.add).then_inc(z_ready, 1)

            def step(t, odd, p0, p1, p2, p3=True):
                i, f = t - 1, t - 2
                for s in range(8):
                    if s in (5, 6, 7) and p2:
                        gate(f, s - 5)
                    if s == 1 and p2:
                        ln_d_dve(xf[:, :], S, LN_S2 + f, bank[3])
                    if s == 2 and p2:
                        ln_eps_dve(S, LN_S2 + f, bank[3])
                    if s >= 1 and p0:
                        normalise(t, s - 1)
                    if s == 0 and p1:
                        normalise(i, 7)
                    if s == 0 and p2:
                        add_attention(f)
                    if p0:
                        norms(t, s)
                    if s in (0, 1, 4, 5) and p1:
                        divide_out(i, (0, 1, 0, 0, 2, 3)[s])
                    if s in (2, 3) and p1:
                        shift_scores(i, s)
                    if s in (6, 7) and p0:
                        shift_scores(t, s - 6)
                    if s == 0 and p3:
                        add_feed_forward(t - 3)
                    if s >= 1 and p0:
                        rotated(t, s - 1)
                    if s == 0 and p1:
                        rotated(i, 7)
                    if s == 2 and p2:
                        scale_norm(f)

            step(0, 0, True, False, False, False)
            step(1, 1, True, True, False, False)
            step(2, 0, True, True, True, False)
            step(3, 1, True, True, True)
            with dve.Fori(4, ITEMS - 1, 2) as t:
                step(t, 0, True, True, True)
                step(t + 1, 1, True, True, True)
            step(ITEMS, 0, False, True, True)
            step(ITEMS + 1, 1, False, False, True)
            step(ITEMS + 2, 0, False, False, False)

            def prepare(b, odd, slot, u):
                x = X[:, b, :]
                if slot == 0:
                    ln_d_dve(Z[:, b, :], S, u)
                if slot in (1, 4):
                    ln_eps_dve(S, u + slot // 4)
                if slot == 2:
                    ln_out_dve(lnt[:, 0:S], S, u)
                    dve.wait_ge(ln_done, u + 1)
                    tt(x, x, lnt[:, 0:S], ALU.add).then_inc(x2_ready, 1)
                if slot == 3:
                    dve.wait_ge(x2_ready, b + 1)
                    ln_d_dve(x, S, u + 1)
                if slot == 5:
                    wait(dve, s3["v"], b)
                    ln_out_dve(s3xn, S, u + 1)
                if slot in (6, 7):
                    n = slot - 6
                    dve.wait_ge(s3["proj"], 3 * b + n + 1)
                    tt(s3part[:, n, :], lnbank[:, :], const("rope")[:, 512 * n:512 * n + 512], ALU.mult).then_inc(s3["part"], 1)
                    dve.wait_ge(s3["part"], 2 * b + n + 1)
                    if n == 0:
                        wait(dve, s3["qm"], 2 * b)
                    tt((s3q, s3k[odd])[n], s3part[:, n, 0:S], s3part[:, n, S:2 * S], ALU.add).then_inc(s3["qk"], 1)

            def finish(b, slot, u):
                x = X[:, b, :]
                if slot == 10:
                    ln_d_dve(s3y, S, u)
                if slot == 11:
                    ln_eps_dve(S, u)
                if slot == 12:
                    ln_out_dve(lnt[:, 0:S], S, u)
                    dve.wait_ge(ln_done, u + 1)
                    tt(x, x, lnt[:, 0:S], ALU.add).then_inc(x3_ready, 1)

            def attend(b, m):
                r, hs = JOBS[m]
                w = P * (r + 1)
                dve.wait_ge(s3["full"], NJ * b + m + 1)
                wait(dve, s3["px"], NJ * b + m - 1)
                part = sh[:, m % 2, :].rearrange("p (h n) -> p h n", n=w)
                tt(part, bank[3 + m % 2][:, :].rearrange("p (h n) -> p h n", n=w), bias[:, hs[0]:hs[-1] + 1, S - w:S]
                   if r == 0 else bias[:, hs[0]:hs[-1] + 1, :], ALU.add).then_inc(s3["add"], 1)
                dve.wait_ge(s3["add"], NJ * b + m + 1)
                red(mx[:, m % 2, 0:len(hs)], part, AX, ALU.max, negate=True).then_inc(s3["mx"], 1)

            def normalise3(b, m):
                r, hs = JOBS[m]
                n = len(hs)
                dve.wait_ge(s3["px"], NJ * b + m + 1)
                nc.vector.reciprocal(rdn[:, m % 2, 0:n], dn[:, m % 2, 0:n]).then_inc(s3["rdn"], 1)
                dve.wait_ge(s3["rdn"], NJ * b + m + 1)
                part = px[:, m % 2, :].rearrange("p (h n) -> p h n", h=n)
                tt(part, part, rdn[:, m % 2, 0:n].unsqueeze(2).broadcast_to([P, n, P * (r + 1)]), ALU.mult).then_inc(s3["pn"], 1)

            def step3(b, odd, next_batch, batch_before):
                u = 3 * b + (LN_S3 + 1)
                for m in range(NJ + 3):
                    if m < NJ:
                        attend(b, m)
                    if 1 <= m <= NJ:
                        normalise3(b, m - 1)
                    if next_batch:
                        prepare(b + 1, 1 - odd, m, u if batch_before else LN_S3 + 2)
                    if batch_before:
                        finish(b - 1, m, u + 2 if next_batch else u)

            dve.wait_ge(rel_in, 16)
            for slot in range(9):
                prepare(0, 0, slot, LN_S3)
            step3(0, 0, True, False)
            with dve.Fori(1, B - 2, 2) as b:
                step3(b, 1, True, True)
                step3(b + 1, 0, True, True)
            step3(B - 1, 1, False, True)
            for slot in range(9, 13):
                finish(B - 1, slot, LN_S4 - 1)

            dve.wait_ge(ld_gate, 64)
            dve.wait_ge(x3_ready, B)
            def norm_input(g, slot):
                if g < B // 2:
                    if slot == 0:
                        ln_d_dve(group(X, g), 512, g + LN_S4)
                    if slot == 1:
                        ln_eps_dve(512, g + LN_S4)
                    if slot == 2:
                        ln_out_dve(s4xn[g % 2], 512, g + LN_S4)

            gates, tails = [0], [0]

            def link(ins):
                gates[0] += 1
                ins.then_inc(s4["d"], 1)
                dve.wait_ge(s4["d"], gates[0])

            def link_tail(ins):
                tails[0] += 1
                ins.then_inc(s4["t"], 1)
                dve.wait_ge(s4["t"], tails[0])

            def by_expert(ap):
                return ap.unsqueeze(2).broadcast_to([P, 4, NE])

            def square(ap):
                return ap.rearrange("p i (e o) -> p i e o", e=NE)

            def tokens(ap):
                return ap.rearrange("p (i n) -> p i n", i=4)

            def by_token(ap):
                return ap.unsqueeze(2).broadcast_to([P, 4, DIM])

            def gate_logits(g):
                dve.wait_ge(s4["gate"], g + 1)
                link(tt(lg[:, :, :], bank[0][:, 0:4 * NE].rearrange("p (i e) -> p i e", i=4),
                        gb[:, :].unsqueeze(1).broadcast_to([P, 4, NE]), ALU.add))
                link(red(g1[:, :], lg[:, :, :], AX, ALU.max))
                link(tt(lh[:, :, :], lg[:, :, :], by_expert(g1[:, :]), ALU.subtract))

            def choose(g):
                dve.wait_ge(s4["ex"], g + 1)
                link(red(g1[:, :], pe_[:, :, :], AX, ALU.add))
                link(nc.vector.reciprocal(g2[:, :], g1[:, :]))
                link(tt(pr_[:, :, :], pe_[:, :, :], by_expert(g2[:, :]), ALU.mult))
                other = pr_[:, :, :].unsqueeze(2).broadcast_to([P, 4, NE, NE])
                own = pr_[:, :, :].unsqueeze(3).broadcast_to([P, 4, NE, NE])
                link(tt(square(cmp1[:, :, :]), other, own, ALU.is_ge))
                link(tt(square(cmp2[:, :, :]), other, own, ALU.is_gt))
                link(tt(cmp3[:, :, :], cmp1[:, :, :], const("lower").unsqueeze(1).broadcast_to([P, 4, NE * NE]), ALU.mult))
                link(tt(cmp4[:, :, :], cmp2[:, :, :], const("upper").unsqueeze(1).broadcast_to([P, 4, NE * NE]), ALU.mult))
                link(tt(cmp1[:, :, :], cmp3[:, :, :], cmp4[:, :, :], ALU.add))
                link(red(rank[:, :, :], square(cmp1[:, :, :]), AX, ALU.add))
                link(nc.vector.tensor_scalar(msk[:, :, :], rank[:, :, :], 1.5, None, ALU.is_lt))

            def centre_out(g):
                dve.wait_ge(s4["acc"], (NE - 1) * g + NE - 1)
                link_tail(red(st[:, 0, :], tokens(acc[:, :]), AX, ALU.add))
                link_tail(nc.vector.tensor_scalar(st[:, 1, :], st[:, 0, :], 1.0 / DIM, None, ALU.mult))
                link_tail(tt(tokens(yc), tokens(acc[:, :]), by_token(st[:, 1, :]), ALU.subtract))

            def variance_out(g):
                dve.wait_ge(s4["ysq"], g + 1)
                link_tail(red(st[:, 2, :], tokens(ysq), AX, ALU.add))
                link_tail(nc.vector.tensor_scalar(st[:, 3, :], st[:, 2, :], 1.0 / DIM, 1e-5, ALU.mult, ALU.add))

            def result(g):
                dve.wait_ge(s4["rs"], g + 1)
                link_tail(tt(tokens(yn), tokens(yc), by_token(rs[:, :]), ALU.mult))
                dve.wait_ge(s4["xts"], g + 1)
                dve.wait_ge(stored, g * 16 + 16)
                tt(outs, yn, s4xt[g % 2], ALU.add).then_inc(s4["out"], 1)

            for slot in range(3):
                norm_input(0, slot)
            for g in range(B // 2):
                if g:
                    centre_out(g - 1)
                gate_logits(g)
                if g:
                    variance_out(g - 1)
                choose(g)
                if g:
                    result(g - 1)
                for e in range(NE):
                    dve.wait_ge(s4["of"], NE * g + e + 1)
                    ob = (bank[4][:, :], obank[:, 0, :])[e % 2]
                    tt(tokens(ob2[:, e % 2, :]), tokens(ob), mb2[:, e, :].unsqueeze(1).broadcast_to([P, 4, DIM]), ALU.add)\
                        .then_inc(s4["ofr"], 1)
                    dve.wait_ge(s4["ofr"], NE * g + e + 1)
                    wait(dve, s4["acc"], (NE - 1) * g + (max(e - 2, 1) if e >= 2 else 0))
                    tt(tokens(oms[:, e % 2, :]), tokens(ob2[:, e % 2, :]), msk[:, :, e:e + 1].broadcast_to([P, 4, DIM]), ALU.mult)\
                        .then_inc(s4["om"], 1)
                    norm_input(g + 1, e)
            centre_out(B // 2 - 1)
            variance_out(B // 2 - 1)
            result(B // 2 - 1)

        @block.gpsimd
        def _(pool):
            tt = nc.gpsimd.tensor_tensor
            nc.gpsimd.memset(vp[:, :, :, :], 0.0).then_inc(vp_cleared, 1)
            pool.wait_ge(ld_const, 32)

            def inverse_norms(t, c):
                pool.wait_ge(n2_done, 8 * t + c + 1)
                tt(rn[:, c % 2, :], n2m[:, c % 2, :], const("mhalf"), ALU.pow).then_inc(rn_done, 1)

            def sines(t, c):
                r, kind = c // 4, (c // 2) % 2
                pool.wait_ge(qn_done, 8 * t + c + 1)
                tt(touch[:, c:c + 1], const("mhalf")[:, 0:1], const("mhalf")[:, 0:1], ALU.mult)
                swapped = qn[:, c % 2, :].rearrange("p (h o d) -> p h o d", o=2, d=DH // 2)[:, :, ::-1, :]
                sin = tab[:, bass.ds(t // B, 1), 2 * kind + 1, r, :].rearrange("p l (o d) -> p l o d", o=2)\
                    .broadcast_to([P, PAIRS, 2, DH // 2])
                tt(t2[:, c % 2, :].rearrange("p (h o d) -> p h o d", o=2, d=DH // 2), swapped, sin, ALU.mult).then_inc(t2_done, 1)

            def inverse_deviations(w, u):
                pool.wait_ge(ln_eps, u + 1)
                tt(lnr[:, 0:w // P], lnv[:, 0:w // P], const("mhalf")[:, 0:w // P], ALU.pow).then_inc(ln_rstd, 1)

            for u in range(LN_S1, LN_S2):
                inverse_deviations(512, u)

            pool.wait_ge(tab_done, 1)

            def step(t, odd, p0, p1, p2, p3=True):
                for s in range(8):
                    if s == 2 and p2:
                        inverse_deviations(S, t - 2 + LN_S2)
                    if s >= 1 and p0:
                        sines(t, s - 1)
                    if s == 0 and p1:
                        sines(t - 1, 7)
                    if p0:
                        inverse_norms(t, s)

            step(0, 0, True, False, False, False)
            step(1, 1, True, True, False, False)
            step(2, 0, True, True, True, False)
            step(3, 1, True, True, True)
            with pool.Fori(4, ITEMS - 1, 2) as t:
                step(t, 0, True, True, True)
                step(t + 1, 1, True, True, True)
            step(ITEMS, 0, False, True, True)
            step(ITEMS + 1, 1, False, False, True)

            pool.wait_ge(v_full, 4 * ITEMS)
            nc.gpsimd.memset(wv[:, 0:4 * P], 0.0).then_inc(cleared, 1)
            pool.wait_ge(o_full, 4 * ITEMS)
            nc.gpsimd.memset(qTf[:, 0:4 * H * WIN], 0.0)
            pool.wait_ge(ld_s3, 16 * 7)
            for k in (0, 2):
                src = s3w[:, k * P:k * P + P].rearrange("p (h o d) -> p h o d", o=2, d=HD // 2)
                dst = s3w[:, k * P + P:k * P + 2 * P].rearrange("p (h o d) -> p h o d", o=2, d=HD // 2)
                nc.gpsimd.tensor_scalar(dst[:, :, 0, :], src[:, :, 1, :], -1.0, None, ALU.mult)
                last = nc.gpsimd.tensor_copy(dst[:, :, 1, :], src[:, :, 0, :])
            last.then_inc(s3["w"], 1)
            def mask_q(b, n):
                hs = slice(8 * n, 8 * n + 8)
                pool.wait_ge(s3["qk"], 2 * b + 1)
                wait(pool, s3["full"], NJ * b - NJ + 6 * n + 6)
                for r in range(2):
                    back = s3q.rearrange("p (r t) -> p r t", r=2)[:, r, ::-1]
                    last = tt(qm[:, hs, r * P:r * P + P], back.unsqueeze(1).broadcast_to([P, 8, P]),
                              const("headm")[:, hs].unsqueeze(2).broadcast_to([P, 8, P]), ALU.mult)
                last.then_inc(s3["qm"], 1)

            def step3(b, next_batch, batch_before):
                u = 3 * b + (LN_S3 + 1)
                if next_batch:
                    for n in range(2):
                        inverse_deviations(S, (u if batch_before else LN_S3 + 2) + n)
                    mask_q(b + 1, 0)
                if batch_before:
                    inverse_deviations(S, u + 2 if next_batch else u)
                if next_batch:
                    mask_q(b + 1, 1)

            for n in range(2):
                inverse_deviations(S, LN_S3 + n)
            for n in range(2):
                mask_q(0, n)
            step3(0, True, False)
            with pool.Fori(1, B - 1) as b:
                step3(b, True, True)
            step3(B - 1, False, True)
            inverse_deviations(S, LN_S4 - 1)

            def root(g):
                pool.wait_ge(s4["t"], TAIL_OPS * g + 5)
                tt(rs[:, :], st[:, 3, :], const("mhalf")[:, 0:4], ALU.pow).then_inc(s4["rs"], 1)

            inverse_deviations(512, LN_S4)
            for g in range(B // 2):
                if g:
                    root(g - 1)
                pool.wait_ge(s4["om"], NE * g + 2)
                tt(acc[:, :], oms[:, 0, :], oms[:, 1, :], ALU.add).then_inc(s4["acc"], 1)
                if g + 1 < B // 2:
                    inverse_deviations(512, g + 1 + LN_S4)
                for e in range(2, NE):
                    pool.wait_ge(s4["om"], NE * g + e + 1)
                    pool.wait_ge(s4["acc"], (NE - 1) * g + e - 1)
                    tt(acc[:, :], acc[:, :], oms[:, e % 2, :], ALU.add).then_inc(s4["acc"], 1)
            root(B // 2 - 1)


def constants():
    import math

    import numpy as np

    f = np.float32
    c = {}
    c["ident"] = np.eye(P, dtype=f)
    c["onesm"] = np.full((P, P), 1.0 / DIM, f)
    head = np.arange(P) // HD
    c["blk"] = (head[:, None] == head[None, :]).astype(f)
    c["headm"] = (head[:, None] == np.arange(H)[None, :]).astype(f)
    half = np.arange(0, DH, 2, dtype=f)
    inv_freq = (f(1.0) / f(10000.0) ** (half / f(DH))).astype(f)
    t = np.arange(S, dtype=f)
    freqs = t[:, None] * inv_freq[None, :]
    freqs = np.concatenate([freqs, freqs], -1)
    base = (half + f(0.4 * DH)) / f(1.4 * DH)
    power = (t - f(S // 2)) / f(WIN // 2)
    scale = base[None, :] ** power[:, None]
    scale = np.concatenate([scale, scale], -1).astype(f)
    sign = np.where(np.arange(DH) < DH // 2, -1.0, 1.0).astype(f)
    cos, sin = np.cos(freqs), np.sin(freqs)
    inv = f(1.0) / scale
    rot = np.stack([cos * scale * f(8), sin * scale * sign * f(8), cos * inv, sin * inv * sign])
    c["rot"] = rot.reshape(4, 2, P, DH).transpose(2, 0, 1, 3).reshape(P, -1)
    inv_freq = (f(1.0) / f(10000.0) ** (np.arange(0, HD, 2, dtype=f) / f(HD))).astype(f)
    emb = t[:, None] * inv_freq[None, :]
    emb = np.tile(np.concatenate([emb, emb], -1), (1, H)).T
    cos, sin, down = np.cos(emb), np.sin(emb), f(1.0 / math.sqrt(HD))
    c["rope"] = np.concatenate([cos * down, sin * down, cos, sin], 1)
    dist = (S - 1) - np.arange(384)
    rp = np.maximum(dist, 0)
    large = 16 + (np.log(np.maximum(rp, 1).astype(f) / f(16)) / f(math.log(8.0)) * f(16)).astype(np.int32)
    bucket = np.where(rp < 16, rp, np.minimum(large, 31))
    c["onehot"] = np.zeros((P, 384), f)
    c["onehot"][bucket, np.arange(384)] = 1.0
    c["onehot"][:, dist < 0] = 0.0
    c["neg"] = np.tile(np.where(dist < 0, -1e9, 0.0).astype(f), (P, 1))
    e = np.arange(NE)
    c["lower"] = np.tile((e[None, :] < e[:, None]).astype(f).reshape(1, -1), (P, 1))
    c["upper"] = np.tile((e[None, :] > e[:, None]).astype(f).reshape(1, -1), (P, 1))
    c["ones"] = np.ones((P, WIN), f)
    c["mhalf"] = np.full((P, PAIRS), -0.5, f)
    packed = np.concatenate([c[n].astype(f) for n, _ in WIDTHS], 1)
    q, key = np.arange(WIN)[:, None], np.arange(2 * WIN)[None, :] - WIN
    hidden = np.where((key > q) | (key < q - WIN), -1e30, 0.0)
    tile = np.tile(hidden, (4, PAIRS))
    first = tile.copy()
    first[0:WIN] = np.tile(np.where(key < 0, -1e30, hidden), (1, PAIRS))
    return packed, np.concatenate([first, tile], 1).astype(f)


_INS = ["L0_attn_x", "L0_attn_w_qkv", "L0_attn_w_out", "L0_attn_b_out", "L0_attn_norm_g", "L0_attn_norm_b",
        "L0_ffn_Wqkv", "L0_ffn_q_scale", "L0_ffn_k_scale", "L0_ffn_Wo", "L0_ffn_ln_g", "L0_ffn_ln_b", "L0_ffn_W1",
        "L0_ffn_b1", "L0_ffn_W2", "L0_ffn_b2", "L1_attn_Wq", "L1_attn_Wk", "L1_attn_Wv", "L1_attn_Wo",
        "L1_attn_rel_emb", "L1_ffn_gate_w", "L1_ffn_gate_b", "L1_ffn_w1", "L1_ffn_b1", "L1_ffn_w2", "L1_ffn_b2"]


def kernel(**inputs):
    import numpy as _np
    import concourse.bacc as _bacc
    from concourse import mybir as _mybir
    from concourse.bass_utils import run_bass_kernel_spmd as _run

    nc = _bacc.Bacc("TRN2", target_bir_lowering=False, num_devices=1)
    arrays, args = {}, {}
    packed, masks = constants()
    for name, arr in [(n, inputs[n]) for n in _INS] + [("consts", packed), ("window_masks", masks)]:
        arr = _np.ascontiguousarray(arr)
        arrays[f"in_{name}"] = arr
        args[name] = nc.dram_tensor(f"in_{name}", arr.shape, _mybir.dt.from_np(arr.dtype), kind="ExternalInput").ap()
    out = nc.dram_tensor("out_0", (B, S, DIM), _mybir.dt.float32, kind="ExternalOutput").ap()
    build(nc, args, out)
    r = _run(nc, [arrays], core_ids=[0])
    return r.results[0]["out_0"]
```
